# Optimizing a Trainium2 kernel written in Bass

```python
import numpy as np
import jax
import jax.numpy as jnp

def _softmax(x, axis=-1):
    return jax.nn.softmax(x, axis=axis)

def _gelu(x):
    return jax.nn.gelu(x, approximate=True)

def _silu(x):
    return jax.nn.silu(x)

def _sigmoid(x):
    return jax.nn.sigmoid(x)

def _layernorm(x, axis=-1, eps=1e-05):
    m = jnp.mean(x, axis=axis, keepdims=True)
    v = jnp.var(x, axis=axis, keepdims=True)
    return (x - m) / jnp.sqrt(v + eps)

def _scatter_add(tgt, idx, src, axis=0):
    return tgt.at[idx].add(src)

def _segment_sum(src, seg, n):
    return jax.ops.segment_sum(src, seg, n)
kernel_name = 'mk_adaln_d2_jaxref_r8_bb0380'

def setup_inputs(seed: int=0):
    np.random.seed(seed)
    _w = jnp.asarray

    def _L0_attn_setup():
        import jax, jax.numpy as jnp
        import numpy as np
        E = 128
        D = 64
        H = E // D
        EPS = 1e-05
        key = jax.random.key(seed)
        ks = jax.random.split(key, 8)
        std = 0.02
        x = jax.random.normal(ks[0], (2, 128, E), jnp.float32)
        Wq = jax.random.normal(ks[1], (E, E), jnp.float32) * std
        Wk = jax.random.normal(ks[2], (E, E), jnp.float32) * std
        Wv = jax.random.normal(ks[3], (E, E), jnp.float32) * std
        Wo = jax.random.normal(ks[4], (E, E), jnp.float32) * std
        delta = jnp.full((E,), float(np.log(0.99 / 0.01)), jnp.float32)
        G1 = jax.random.normal(ks[5], (E, D), jnp.float32) * std
        G2 = jax.random.normal(ks[6], (D, E), jnp.float32) * std
        norm_w = jnp.ones((E,), jnp.float32)
        return {'x': x, 'Wq': Wq, 'Wk': Wk, 'Wv': Wv, 'Wo': Wo, 'delta': delta, 'G1': G1, 'G2': G2, 'norm_w': norm_w}
    _L0_attn_in = _L0_attn_setup()

    def _L0_ffn_setup():
        import jax, jax.numpy as jnp
        import numpy as np
        DIM = 128
        DEPTH = 2
        HEADS = 8
        DIM_HEAD = 64
        WINDOW = 64
        INNER = HEADS * DIM_HEAD
        HID = int(DIM * 4 * 2 / 3)
        B, N = (2, 1024)
        QK_SCALE = 8.0

        def shift_token(t):
            t1, t2 = jnp.split(t, 2, axis=-1)
            t2 = jnp.pad(t2, ((0, 0), (1, 0), (0, 0)))[:, :-1]
            return jnp.concatenate([t1, t2], axis=-1)

        def l2norm(t):
            return t / jnp.clip(jnp.linalg.norm(t, axis=-1, keepdims=True), 1e-12)

        def rotate_half(x):
            x1, x2 = jnp.split(x, 2, axis=-1)
            return jnp.concatenate([-x2, x1], axis=-1)

        def rotary_xpos(q, k):
            n = q.shape[-2]
            half_idx = jnp.arange(0, DIM_HEAD, 2, dtype=jnp.float32)
            inv_freq = 1.0 / 10000.0 ** (half_idx / DIM_HEAD)
            t = jnp.arange(n, dtype=jnp.float32)
            freqs = t[:, None] * inv_freq[None, :]
            freqs = jnp.concatenate([freqs, freqs], axis=-1)
            base = (half_idx + 0.4 * DIM_HEAD) / (1.4 * DIM_HEAD)
            power = (t - n // 2) / float(WINDOW // 2)
            scale = base[None, :] ** power[:, None]
            scale = jnp.concatenate([scale, scale], axis=-1)
            cos, sin = (jnp.cos(freqs), jnp.sin(freqs))
            q = q * cos * scale + rotate_half(q) * sin * scale
            k = k * cos / scale + rotate_half(k) * sin / scale
            return (q, k)

        def local_attention(q, k, v):
            b, h, n, d = q.shape
            w = n // WINDOW
            bq = q.reshape(b, h, w, WINDOW, d) * QK_SCALE
            bk = k.reshape(b, h, w, WINDOW, d)
            bv = v.reshape(b, h, w, WINDOW, d)

            def look_around(t):
                p = jnp.pad(t, ((0, 0), (0, 0), (1, 0), (0, 0), (0, 0)))
                return jnp.concatenate([p[:, :, :w], p[:, :, 1:]], axis=3)
            bk, bv = (look_around(bk), look_around(bv))
            bt = jnp.arange(n).reshape(w, WINDOW)
            btp = jnp.pad(bt, ((1, 0), (0, 0)), constant_values=-1)
            btk = jnp.concatenate([btp[:w], btp[1:]], axis=1)
            sim = jnp.einsum('bhwid,bhwjd->bhwij', bq, bk)
            i = bt[:, :, None]
            j = btk[:, None, :]
            mask = (i < j) | (i > j + WINDOW) | (j == -1)
            sim = jnp.where(mask, -jnp.finfo(sim.dtype).max, sim)
            attn = jax.nn.softmax(sim, axis=-1)
            out = jnp.einsum('bhwij,bhwjd->bhwid', attn, bv)
            return out.reshape(b, h, n, d)

        def _layer(x, wqkv, qs, ksc, wo, lg, lb, w1, b1, w2, b2):
            b, n, _ = x.shape
            h = shift_token(x)
            qkv = h @ wqkv
            q, k, v = jnp.split(qkv, 3, axis=-1)
            to_heads = lambda t: t.reshape(b, n, HEADS, DIM_HEAD).transpose(0, 2, 1, 3)
            q, k, v = (to_heads(q), to_heads(k), to_heads(v))
            q = l2norm(q) * qs
            k = l2norm(k) * ksc
            q, k = rotary_xpos(q, k)
            o = local_attention(q, k, v)
            o = o.transpose(0, 2, 1, 3).reshape(b, n, INNER)
            x = x + o @ wo
            h = shift_token(x)
            mu = h.mean(-1, keepdims=True)
            var = h.var(-1, keepdims=True)
            h = (h - mu) / jnp.sqrt(var + 1e-05) * lg + lb
            h = h @ w1 + b1
            a, g = jnp.split(h, 2, axis=-1)
            h = a * jax.nn.gelu(g, approximate=False)
            x = x + h @ w2 + b2
            return x
        key = jax.random.key(seed)
        ks = jax.random.split(key, 6)
        return {'x': jax.random.normal(ks[0], (B, N, DIM), jnp.float32), 'wqkv': jax.random.normal(ks[1], (DEPTH, DIM, 3 * INNER), jnp.float32) * 0.02, 'q_scale': jnp.ones((DEPTH, DIM_HEAD), jnp.float32), 'k_scale': jnp.ones((DEPTH, DIM_HEAD), jnp.float32), 'wo': jax.random.normal(ks[2], (DEPTH, INNER, DIM), jnp.float32) * 0.02, 'ln_g': jnp.ones((DEPTH, DIM), jnp.float32), 'ln_b': jnp.zeros((DEPTH, DIM), jnp.float32), 'w1': jax.random.normal(ks[3], (DEPTH, DIM, 2 * HID), jnp.float32) * 0.02, 'b1': jnp.zeros((DEPTH, 2 * HID), jnp.float32), 'w2': jax.random.normal(ks[4], (DEPTH, HID, DIM), jnp.float32) * 0.02, 'b2': jnp.zeros((DEPTH, DIM), jnp.float32)}
    _L0_ffn_in = _L0_ffn_setup()
    _L0_c = _w((lambda *s: np.random.randn(*s).astype(np.float32) * 0.05)(2, 128))
    _L0_wmod = _w((lambda *s: np.random.randn(*s).astype(np.float32) * 0.05)(128, 6 * 128) * 128 ** (-0.5))

    def _L1_attn_setup():
        import jax, jax.numpy as jnp
        import numpy as np
        EMBED_DIM = 128
        NUM_HEADS = 16
        HEAD_DIM = EMBED_DIM // NUM_HEADS
        SCALING = HEAD_DIM ** (-0.5)
        key = jax.random.key(seed)
        k1, k2, k3, k4, k5 = jax.random.split(key, 5)
        B, S, E, H = (2, 256, EMBED_DIM, NUM_HEADS)
        x = jax.random.normal(k1, (B, S, E), dtype=jnp.float32)
        W_A = jax.random.normal(k2, (H, E), dtype=jnp.float32) * E ** (-0.5)
        W_V = jax.random.normal(k3, (E, E), dtype=jnp.float32) * E ** (-0.5)
        W_O = jax.random.normal(k4, (E, E), dtype=jnp.float32) * E ** (-0.5)
        b_O = jax.random.normal(k5, (E,), dtype=jnp.float32) * 0.01
        return {'x': x, 'W_A': W_A, 'W_V': W_V, 'W_O': W_O, 'b_O': b_O}
    _L1_attn_in = _L1_attn_setup()

    def _L1_ffn_setup():
        import jax, jax.numpy as jnp
        import numpy as np
        B, S, H, E = (2, 256, 128, 16)
        key = jax.random.key(seed)
        k0, k1, k2, k3 = jax.random.split(key, 4)
        tokens = jax.random.normal(k0, (B, S, H), dtype=jnp.float32)
        gate_w = jax.random.normal(k1, (E, H), dtype=jnp.float32) * H ** (-0.5)
        expert_w = jax.random.normal(k2, (E, H, H), dtype=jnp.float32) * H ** (-0.5)
        expert_b = jax.random.normal(k3, (E, H), dtype=jnp.float32) * 0.01
        return {'tokens': tokens, 'gate_w': gate_w, 'expert_w': expert_w, 'expert_b': expert_b}
    _L1_ffn_in = _L1_ffn_setup()
    _L1_c = _w((lambda *s: np.random.randn(*s).astype(np.float32) * 0.05)(2, 128))
    _L1_wmod = _w((lambda *s: np.random.randn(*s).astype(np.float32) * 0.05)(128, 6 * 128) * 128 ** (-0.5))
    _d = {'L0_attn_x': _L0_attn_in['x'], 'L0_attn_Wq': _L0_attn_in['Wq'], 'L0_attn_Wk': _L0_attn_in['Wk'], 'L0_attn_Wv': _L0_attn_in['Wv'], 'L0_attn_Wo': _L0_attn_in['Wo'], 'L0_attn_delta': _L0_attn_in['delta'], 'L0_attn_G1': _L0_attn_in['G1'], 'L0_attn_G2': _L0_attn_in['G2'], 'L0_attn_norm_w': _L0_attn_in['norm_w'], 'L0_ffn_wqkv': _L0_ffn_in['wqkv'], 'L0_ffn_q_scale': _L0_ffn_in['q_scale'], 'L0_ffn_k_scale': _L0_ffn_in['k_scale'], 'L0_ffn_wo': _L0_ffn_in['wo'], 'L0_ffn_ln_g': _L0_ffn_in['ln_g'], 'L0_ffn_ln_b': _L0_ffn_in['ln_b'], 'L0_ffn_w1': _L0_ffn_in['w1'], 'L0_ffn_b1': _L0_ffn_in['b1'], 'L0_ffn_w2': _L0_ffn_in['w2'], 'L0_ffn_b2': _L0_ffn_in['b2'], 'L0_c': _L0_c, 'L0_wmod': _L0_wmod, 'L1_attn_W_A': _L1_attn_in['W_A'], 'L1_attn_W_V': _L1_attn_in['W_V'], 'L1_attn_W_O': _L1_attn_in['W_O'], 'L1_attn_b_O': _L1_attn_in['b_O'], 'L1_ffn_gate_w': _L1_ffn_in['gate_w'], 'L1_ffn_expert_w': _L1_ffn_in['expert_w'], 'L1_ffn_expert_b': _L1_ffn_in['expert_b'], 'L1_c': _L1_c, 'L1_wmod': _L1_wmod}
    _x0 = _d['L0_attn_x']
    _d['L0_attn_x'] = jax.random.normal(jax.random.fold_in(jax.random.key(seed), 1), (2, 2048, 128), dtype=_x0.dtype)
    del _x0
    return _d

def reference(L0_attn_x, L0_attn_Wq, L0_attn_Wk, L0_attn_Wv, L0_attn_Wo, L0_attn_delta, L0_attn_G1, L0_attn_G2, L0_attn_norm_w, L0_ffn_wqkv, L0_ffn_q_scale, L0_ffn_k_scale, L0_ffn_wo, L0_ffn_ln_g, L0_ffn_ln_b, L0_ffn_w1, L0_ffn_b1, L0_ffn_w2, L0_ffn_b2, L0_c, L0_wmod, L1_attn_W_A, L1_attn_W_V, L1_attn_W_O, L1_attn_b_O, L1_ffn_gate_w, L1_ffn_expert_w, L1_ffn_expert_b, L1_c, L1_wmod):

    def _L0_attn_ref(x, Wq, Wk, Wv, Wo, delta, G1, G2, norm_w):
        import jax, jax.numpy as jnp
        import numpy as np
        E = 128
        D = 64
        H = E // D
        EPS = 1e-05
        B, T, _ = x.shape
        q = jax.nn.silu(x @ Wq)
        v = x @ Wv
        log_f = jax.nn.log_sigmoid(x @ Wk + delta)
        k = -jnp.expm1(log_f)

        def to_tbhd(a):
            return a.reshape(B, T, H, D).transpose(1, 0, 2, 3)
        qh, kh, vh, gh = map(to_tbhd, (q, k, v, log_f))
        S0 = jnp.zeros((B, H, D, D), x.dtype)

        def step(S, inp):
            q_t, k_t, v_t, g_t = inp
            S = S * jnp.exp(g_t)[..., None] + k_t[..., None] * v_t[..., None, :]
            o_t = jnp.einsum('bhk,bhkv->bhv', q_t, S)
            return (S, o_t)
        _, o = jax.lax.scan(step, S0, (qh, kh, vh, gh))
        o = o.transpose(1, 0, 2, 3).reshape(B, T, E)
        gate = x @ G1 @ G2
        o = o * jax.nn.sigmoid(gate)
        og = o.reshape(B, T, H, D)
        og = og * jax.lax.rsqrt(jnp.mean(og * og, axis=-1, keepdims=True) + EPS)
        o = og.reshape(B, T, E) * norm_w
        return o @ Wo

    def _L0_ffn_ref(x, wqkv, q_scale, k_scale, wo, ln_g, ln_b, w1, b1, w2, b2):
        import jax, jax.numpy as jnp
        import numpy as np
        DIM = 128
        DEPTH = 2
        HEADS = 8
        DIM_HEAD = 64
        WINDOW = 64
        INNER = HEADS * DIM_HEAD
        HID = int(DIM * 4 * 2 / 3)
        B, N = (2, 1024)
        QK_SCALE = 8.0

        def shift_token(t):
            t1, t2 = jnp.split(t, 2, axis=-1)
            t2 = jnp.pad(t2, ((0, 0), (1, 0), (0, 0)))[:, :-1]
            return jnp.concatenate([t1, t2], axis=-1)

        def l2norm(t):
            return t / jnp.clip(jnp.linalg.norm(t, axis=-1, keepdims=True), 1e-12)

        def rotate_half(x):
            x1, x2 = jnp.split(x, 2, axis=-1)
            return jnp.concatenate([-x2, x1], axis=-1)

        def rotary_xpos(q, k):
            n = q.shape[-2]
            half_idx = jnp.arange(0, DIM_HEAD, 2, dtype=jnp.float32)
            inv_freq = 1.0 / 10000.0 ** (half_idx / DIM_HEAD)
            t = jnp.arange(n, dtype=jnp.float32)
            freqs = t[:, None] * inv_freq[None, :]
            freqs = jnp.concatenate([freqs, freqs], axis=-1)
            base = (half_idx + 0.4 * DIM_HEAD) / (1.4 * DIM_HEAD)
            power = (t - n // 2) / float(WINDOW // 2)
            scale = base[None, :] ** power[:, None]
            scale = jnp.concatenate([scale, scale], axis=-1)
            cos, sin = (jnp.cos(freqs), jnp.sin(freqs))
            q = q * cos * scale + rotate_half(q) * sin * scale
            k = k * cos / scale + rotate_half(k) * sin / scale
            return (q, k)

        def local_attention(q, k, v):
            b, h, n, d = q.shape
            w = n // WINDOW
            bq = q.reshape(b, h, w, WINDOW, d) * QK_SCALE
            bk = k.reshape(b, h, w, WINDOW, d)
            bv = v.reshape(b, h, w, WINDOW, d)

            def look_around(t):
                p = jnp.pad(t, ((0, 0), (0, 0), (1, 0), (0, 0), (0, 0)))
                return jnp.concatenate([p[:, :, :w], p[:, :, 1:]], axis=3)
            bk, bv = (look_around(bk), look_around(bv))
            bt = jnp.arange(n).reshape(w, WINDOW)
            btp = jnp.pad(bt, ((1, 0), (0, 0)), constant_values=-1)
            btk = jnp.concatenate([btp[:w], btp[1:]], axis=1)
            sim = jnp.einsum('bhwid,bhwjd->bhwij', bq, bk)
            i = bt[:, :, None]
            j = btk[:, None, :]
            mask = (i < j) | (i > j + WINDOW) | (j == -1)
            sim = jnp.where(mask, -jnp.finfo(sim.dtype).max, sim)
            attn = jax.nn.softmax(sim, axis=-1)
            out = jnp.einsum('bhwij,bhwjd->bhwid', attn, bv)
            return out.reshape(b, h, n, d)

        def _layer(x, wqkv, qs, ksc, wo, lg, lb, w1, b1, w2, b2):
            b, n, _ = x.shape
            h = shift_token(x)
            qkv = h @ wqkv
            q, k, v = jnp.split(qkv, 3, axis=-1)
            to_heads = lambda t: t.reshape(b, n, HEADS, DIM_HEAD).transpose(0, 2, 1, 3)
            q, k, v = (to_heads(q), to_heads(k), to_heads(v))
            q = l2norm(q) * qs
            k = l2norm(k) * ksc
            q, k = rotary_xpos(q, k)
            o = local_attention(q, k, v)
            o = o.transpose(0, 2, 1, 3).reshape(b, n, INNER)
            x = x + o @ wo
            h = shift_token(x)
            mu = h.mean(-1, keepdims=True)
            var = h.var(-1, keepdims=True)
            h = (h - mu) / jnp.sqrt(var + 1e-05) * lg + lb
            h = h @ w1 + b1
            a, g = jnp.split(h, 2, axis=-1)
            h = a * jax.nn.gelu(g, approximate=False)
            x = x + h @ w2 + b2
            return x
        for l in range(DEPTH):
            x = _layer(x, wqkv[l], q_scale[l], k_scale[l], wo[l], ln_g[l], ln_b[l], w1[l], b1[l], w2[l], b2[l])
        return x

    def _L1_attn_ref(x, W_A, W_V, W_O, b_O):
        import jax, jax.numpy as jnp
        import numpy as np
        EMBED_DIM = 128
        NUM_HEADS = 16
        HEAD_DIM = EMBED_DIM // NUM_HEADS
        SCALING = HEAD_DIM ** (-0.5)
        B, S, E = x.shape
        H, D = (NUM_HEADS, HEAD_DIM)
        z = jnp.einsum('bse,he->bsh', x, W_A) * SCALING
        z = jax.nn.softmax(z, axis=1)
        zp = jnp.transpose(z, (0, 2, 1))
        i = jnp.arange(S)[:, None]
        j = jnp.arange(S)[None, :]
        idx = (i - j) % S
        tril = (j <= i).astype(x.dtype)
        roll = zp[:, :, idx] * tril
        v = jnp.einsum('bse,fe->bsf', x, W_V).reshape(B, S, H, D)
        out = jnp.einsum('bhij,bjhd->bihd', roll, v).reshape(B, S, E)
        return jnp.einsum('bse,fe->bsf', out, W_O) + b_O

    def _L1_ffn_ref(tokens, gate_w, expert_w, expert_b):
        import jax, jax.numpy as jnp
        import numpy as np
        B, S, H, E = (2, 256, 128, 16)
        b, s, h = tokens.shape
        logits = jnp.einsum('bsh,eh->bse', tokens, gate_w)
        weights = jax.nn.softmax(logits, axis=-1)
        top2_w, top2_idx = jax.lax.top_k(weights, 2)
        flat = tokens.reshape(b * s, h)
        flat_w = top2_w.reshape(b * s, 2)
        flat_idx = top2_idx.reshape(b * s, 2)
        y = jax.nn.relu(jnp.einsum('nh,edh->ned', flat, expert_w) + expert_b[None, :, :])
        sel = jnp.take_along_axis(y, flat_idx[:, :, None], axis=1)
        out = jnp.sum(sel * flat_w[:, :, None], axis=1)
        return out.reshape(b, s, h)
    x = L0_attn_x
    mod = (_silu(L0_c) @ L0_wmod).reshape(L0_c.shape[0], 6, 1, -1)
    sa, ca, ga, sb, cb, gb = (mod[:, 0], mod[:, 1], mod[:, 2], mod[:, 3], mod[:, 4], mod[:, 5])
    ga = (2 * (ga >= 0) - 1) * jnp.maximum(jnp.abs(ga), 0.25)
    gb = (2 * (gb >= 0) - 1) * jnp.maximum(jnp.abs(gb), 0.25)
    h = _layernorm(x, axis=-1) * (1 + ca) + sa
    x = x + ga * _L0_attn_ref(h, L0_attn_Wq, L0_attn_Wk, L0_attn_Wv, L0_attn_Wo, L0_attn_delta, L0_attn_G1, L0_attn_G2, L0_attn_norm_w)
    h = _layernorm(x, axis=-1) * (1 + cb) + sb
    x = x + gb * _L0_ffn_ref(h, L0_ffn_wqkv, L0_ffn_q_scale, L0_ffn_k_scale, L0_ffn_wo, L0_ffn_ln_g, L0_ffn_ln_b, L0_ffn_w1, L0_ffn_b1, L0_ffn_w2, L0_ffn_b2)
    mod = (_silu(L1_c) @ L1_wmod).reshape(L1_c.shape[0], 6, 1, -1)
    sa, ca, ga, sb, cb, gb = (mod[:, 0], mod[:, 1], mod[:, 2], mod[:, 3], mod[:, 4], mod[:, 5])
    ga = (2 * (ga >= 0) - 1) * jnp.maximum(jnp.abs(ga), 0.25)
    gb = (2 * (gb >= 0) - 1) * jnp.maximum(jnp.abs(gb), 0.25)
    h = _layernorm(x, axis=-1) * (1 + ca) + sa
    x = x + ga * _L1_attn_ref(h, L1_attn_W_A, L1_attn_W_V, L1_attn_W_O, L1_attn_b_O)
    h = _layernorm(x, axis=-1) * (1 + cb) + sb
    x = x + gb * _L1_ffn_ref(h, L1_ffn_gate_w, L1_ffn_expert_w, L1_ffn_expert_b)
    return x

_drawn_inputs = setup_inputs


def setup_inputs(seed=0):
    import zlib

    import numpy as np

    out = dict(_drawn_inputs(seed))
    spreads = {'L0_attn_delta': (4.595119953155518, 0.574),
     'L0_attn_norm_w': (1.0, 0.6),
     'L0_ffn_q_scale': (1.0, 0.6),
     'L0_ffn_k_scale': (1.0, 0.6),
     'L0_ffn_ln_g': (1.0, 0.6),
     'L0_ffn_ln_b': (0.0, 0.8),
     'L0_ffn_b1': (0.0, 0.8),
     'L0_ffn_b2': (0.0, 0.718)}
    factors = {'L0_attn_G1': 8.0,
     'L0_attn_G2': 8.0,
     'L0_ffn_wqkv': 7.85,
     'L0_ffn_wo': 7.774,
     'L0_ffn_w1': 8.0,
     'L0_ffn_w2': 8.0,
     'L1_attn_W_A': 8.0,
     'L1_attn_W_V': 7.135,
     'L1_attn_W_O': 7.103,
     'L1_attn_b_O': 200.0,
     'L1_ffn_expert_b': 200.0,
     'L1_ffn_gate_w': 8.0,
     'L1_ffn_expert_w': 8.0}
    for name, (base, spread) in spreads.items():
        noise = np.random.default_rng([zlib.crc32(name.encode()), seed]).standard_normal(out[name].shape)
        drawn = base * np.exp(spread * noise) if base else spread * noise
        out[name] = jnp.asarray(drawn.astype(out[name].dtype))
    for name, factor in factors.items():
        out[name] = (out[name] * factor).astype(out[name].dtype)
    return out
```

```python
from contextlib import ExitStack

import concourse.bass as bass
import numpy as np
from concourse import mybir

F32 = mybir.dt.float32
BF16 = mybir.dt.bfloat16
U32 = mybir.dt.uint32
ALU = mybir.AluOpType
ACT = mybir.ActivationFunctionType
AX_X = mybir.AxisListType.X

P = 128
B, T, E = 2, 2048, 128
NT = T // P
TILES = B * NT
BANK = 512
LN_EPS = 1e-5
RING = 4
PRIMED = 6

GH, GD = 2, 64
HALVES = (4, 8, 16, 32, 64)
NLEV = len(HALVES)
MAX_EXP = float(np.exp(20.0))
MAX_SIG = 1e18

DEPTH, WH, WD, WIN = 2, 8, 64, 64
INNER = WH * WD
QK_SCALE = 8.0
NEG = -1e30
HID = int(E * 4 * 2 / 3)
HCH = [(0, 128), (128, 128), (256, HID - 256)]

CH, CD = 16, 8
NE = 16


class Steps:

    def __init__(self, sem, *names):
        self.sem, self.names, self.n = sem, names, 0
        self.base = 0

    def __call__(self, name):
        assert self.names[self.n % len(self.names)] == name, (self.names, self.n, name)
        self.n += 1
        return self.sem

    def at(self, name, i):
        if isinstance(i, int):
            i = min(i, TILES - 1)
        return (i + self.base + PRIMED) * len(self.names) + self.names.index(name) + 1


def prime(eng, steps):
    for s in steps:
        eng.sem_inc(s.sem, PRIMED * len(s.names))


def pipeline(eng, stages, n=TILES):
    lag = max(k for _, k in stages)
    start = -(-lag // RING) * RING
    for s in range(start):
        for f, k in stages:
            if 0 <= s - k:
                f(s - k, (s - k) % RING)
    with eng.Fori(0, (n - start) // RING) as j:
        for u in range(RING):
            for f, k in stages:
                f(j * RING + (start + u - k), (start + u - k) % RING)
    for s in range(n, n + lag):
        for f, k in stages:
            if s - k < n:
                f(s - k, (s - k) % RING)


def rows_bc(ap, n):
    return ap.unsqueeze(1).broadcast_to([ap.shape[0], n, ap.shape[1]])


def cols_bc(ap, w):
    return ap.unsqueeze(2).broadcast_to([ap.shape[0], ap.shape[1], w])


def row_tiles(ap):
    return ap.rearrange("b (n p) e -> p (b n) e", p=P)


class Core:

    def __init__(self, nc, ctx, inp):
        self.nc, self.ctx, self.inp = nc, ctx, inp
        self.psum = ctx.enter_context(nc.psum_tensor("psum", [P, 8, BANK], F32))
        self.bank = [self.psum[:, k, :] for k in range(8)]
        sb = self.sb(ctx)
        self.x = sb("x_rows", [P, TILES, E])
        self.ident = sb("ident", [P, P])
        self.mod = sb("mod", [P, 2, B, 6, E])
        self.mean = sb("mean", [P, TILES])
        self.rstd = sb("rstd", [P, TILES])
        self.minus_half = sb("minus_half", [P, TILES])

    def sb(self, ctx):
        return lambda name, shape, dt=F32: ctx.enter_context(self.nc.sbuf_tensor(name, shape, dt))

    def steps(self, ctx, name, *names):
        return Steps(ctx.enter_context(self.nc.semaphore(name)), *names)

    def sem(self, ctx, name):
        return ctx.enter_context(self.nc.semaphore(name))


SA, CA, GA, SB, CB, GB = range(6)


def setup(c):
    nc, inp = c.nc, c.inp
    with ExitStack() as ctx:
        sb = c.sb(ctx)
        cT = sb("cT", [P, 4])
        wmod = sb("wmod", [P, 2, 6 * E])
        ex = sb("ex", [P, 4])
        sig = sb("sig", [P, 4])
        silu = sb("silu", [P, 4])
        lhs = sb("silu_bc", [P, 4, P])
        sign = sb("sign", [P, 2, B, 2, E])
        loaded = c.sem(ctx, "setup_loaded")
        act_done = c.sem(ctx, "setup_act")
        vec = c.sem(ctx, "setup_vec")
        pe_done = c.sem(ctx, "setup_pe")
        LOADS = 5
        with nc.Block() as block:

            @block.sync
            def _(sp):
                for k, name in enumerate(("L0_c", "L1_c")):
                    sp.dma_start(cT[:, 2 * k:2 * k + 2], inp[name].rearrange("b e -> e b")).then_inc(loaded, 16)
                for k, name in enumerate(("L0_wmod", "L1_wmod")):
                    sp.dma_start(wmod[:, k, :], inp[name]).then_inc(loaded, 16)
                sp.dma_start(c.ident[:, :], inp["ident"]).then_inc(loaded, 16)
                sp.dma_start(c.x[:, :, :], row_tiles(inp["L0_attn_x"])).then_inc(loaded, 16)
                sp.wait_ge(loaded, 16 * (LOADS + 1))

            @block.scalar
            def _(act):
                act.wait_ge(loaded, 16 * (LOADS + 1))
                nc.scalar.activation(ex[:, :], cT[:, :], ACT.Exp, scale=-1.0).then_inc(act_done, 1)

            @block.vector
            def _(dve):
                nc.vector.memset(c.minus_half[:, :], -0.5).then_inc(vec, 1)
                dve.wait_ge(act_done, 1)
                nc.vector.tensor_scalar(ex[:, :], ex[:, :], 1.0, None, ALU.add).then_inc(vec, 1)
                dve.wait_ge(vec, 2)
                nc.vector.reciprocal(sig[:, :], ex[:, :]).then_inc(vec, 1)
                dve.wait_ge(vec, 3)
                nc.vector.tensor_tensor(silu[:, :], cT[:, :], sig[:, :], ALU.mult).then_inc(vec, 1)
                dve.wait_ge(vec, 4)
                nc.vector.tensor_copy(lhs[:, :, :], cols_bc(silu[:, :], P)).then_inc(vec, 1)
                flat = c.mod[:, :, :, :, :].rearrange("p k b m e -> p (k b) (m e)")
                for r in range(4):
                    dve.wait_ge(pe_done, r + 1)
                    for h, (lo, hi) in enumerate(((0, 512), (512, 768))):
                        nc.vector.tensor_copy(flat[:, r, lo:hi], c.bank[2 * r + h][:, 0:hi - lo]).then_inc(vec, 1)
                dve.wait_ge(vec, 13)
                m = c.mod[:, :, :, :, :].rearrange("p k b (s m) e -> p (k b) s m e", s=2)
                for r in range(4):
                    nc.vector.tensor_scalar(m[:, r, :, 1, :], m[:, r, :, 1, :], 1.0, None, ALU.add).then_inc(vec, 1)
                    sg = sign[:, r // 2, r % 2, :, :]
                    nc.vector.tensor_scalar(sg, m[:, r, :, 2, :], 0.0, 2.0, ALU.is_ge, ALU.mult).then_inc(vec, 1)
                    mag = m[:, r, :, 2, :]
                    dve.wait_ge(vec, 13 + 5 * r + 2)
                    nc.vector.scalar_tensor_tensor(out=mag, in0=mag, scalar=-1.0, in1=mag, op0=ALU.mult,
                                                   op1=ALU.max).then_inc(vec, 1)
                    dve.wait_ge(vec, 13 + 5 * r + 3)
                    nc.vector.tensor_scalar(mag, mag, 0.25, None, ALU.max).then_inc(vec, 1)
                    dve.wait_ge(vec, 13 + 5 * r + 4)
                    nc.vector.scalar_tensor_tensor(out=m[:, r, :, 2, :], in0=sg, scalar=-1.0,
                                                   in1=m[:, r, :, 2, :], op0=ALU.add,
                                                   op1=ALU.mult).then_inc(vec, 1)
                dve.wait_ge(vec, 33)

            @block.tensor
            def _(pe):
                pe.wait_ge(vec, 5)
                for r in range(4):
                    nc.tensor.matmul(c.bank[2 * r][:, :], lhs[:, r, :], wmod[:, r // 2, 0:512], start=True, stop=True)
                    nc.tensor.matmul(c.bank[2 * r + 1][:, 0:256], lhs[:, r, :], wmod[:, r // 2, 512:768],
                                     start=True, stop=True).then_inc(pe_done, 1)


def row_statistics(c, tag):
    nc = c.nc
    with ExitStack() as ctx:
        sb = c.sb(ctx)
        st = sb(f"{tag}_st", [P, TILES, 6])
        tmp = sb(f"{tag}_tmp", [P, 3, TILES])
        vec = c.sem(ctx, f"{tag}_vec")
        pool = c.sem(ctx, f"{tag}_pool")
        with nc.Block() as block:

            @block.vector
            def _(dve):
                with dve.Fori(0, TILES) as i:
                    nc.vector.bn_stats(st[:, i, :], c.x[:, i, :]).then_inc(vec, 1)
                n = TILES
                me, ve, mo, vo = (st[:, :, k] for k in (1, 2, 4, 5))
                s, d, v = (tmp[:, k, :] for k in range(3))
                dve.wait_ge(vec, n)
                nc.vector.tensor_tensor(s, me, mo, ALU.add).then_inc(vec, 1)
                nc.vector.tensor_tensor(d, me, mo, ALU.subtract).then_inc(vec, 1)
                nc.vector.tensor_tensor(v, ve, vo, ALU.add).then_inc(vec, 1)
                dve.wait_ge(vec, n + 3)
                nc.vector.tensor_scalar(c.mean[:, :], s, 0.5, None, ALU.mult).then_inc(vec, 1)
                nc.vector.tensor_tensor(d, d, d, ALU.mult).then_inc(vec, 1)
                dve.wait_ge(vec, n + 5)
                nc.vector.scalar_tensor_tensor(out=v, in0=d, scalar=E / 4.0, in1=v, op0=ALU.mult,
                                               op1=ALU.add).then_inc(vec, 1)
                dve.wait_ge(vec, n + 6)
                nc.vector.tensor_scalar(v, v, 1.0 / E, LN_EPS, ALU.mult, ALU.add).then_inc(vec, 1)

            @block.gpsimd
            def _(gp):
                gp.wait_ge(vec, TILES + 7)
                nc.gpsimd.tensor_tensor(c.rstd[:, :], tmp[:, 2, :], c.minus_half[:, :], ALU.pow).then_inc(pool, 1)
                gp.wait_ge(pool, 1)


def modulate(c, dve, st, rows, i, block, shift, scale):
    nc, b = c.nc, i // NT
    nc.vector.tensor_scalar(rows, c.x[:, i, :], c.mean[:, bass.ds(i, 1)], c.rstd[:, bass.ds(i, 1)],
                            ALU.subtract, ALU.mult).then_inc(st("norm"), 1)
    dve.wait_ge(st.sem, st.at("norm", i))
    nc.vector.tensor_tensor(rows, rows, c.mod[:, block, b, scale, :], ALU.mult).then_inc(st("scaled"), 1)
    dve.wait_ge(st.sem, st.at("scaled", i))
    nc.vector.tensor_tensor(rows, rows, c.mod[:, block, b, shift, :], ALU.add).then_inc(st("shifted"), 1)


def linear_attention(c):
    nc, inp, bk = c.nc, c.inp, c.bank
    proj, small, tr, out = bk[0], bk[1], bk[6], bk[7]
    level = [c.psum[:, 2:4, P * k:P * k + P] for k in range(4)] + [c.psum[:, 4:6, 0:P]]
    level_step = ("l0123",) * 4 + ("l4",)
    with ExitStack() as ctx:
        sb = c.sb(ctx)
        wk, wq, wv, wo = (sb(f"la_{n}", [P, E]) for n in ("wk", "wq", "wv", "wo"))
        g1 = sb("la_g1", [P, GD])
        g2 = sb("la_g2", [GD, E])
        wog = sb("la_wog", [P, B, E])
        delta = sb("la_delta", [P, 2])
        norm_w = sb("la_norm_w", [P, 1])
        masks = sb("la_masks", [P, NLEV, P], U32)
        ones = sb("la_ones", [P, P])
        reset = sb("la_reset", [P, TILES])
        state = sb("la_state", [P, P])
        ring = lambda name, *shape: sb("la_" + name, [P, RING, *shape])
        rows, hT, v, g1T, y = (ring(n, P) for n in ("rows", "hT", "v", "g1T", "y"))
        ex = ring("ex", 2, P)
        ln = ring("ln", 2, P)
        sg = ring("sg", 2, P)
        kq = ring("kq", 2, P)
        cum = ring("cum", P)
        last = ring("last", 1)
        dist = ring("dist", NLEV, P)
        dec = ring("dec", NLEV + 1, P)
        qe, ke = ring("qe", NLEV, P), ring("ke", NLEV, P)
        dstart, dend = ring("dstart", P), ring("dend", P)
        qs, kend, kendT = ring("qs", P), ring("kend", P), ring("kendT", P)
        attn = ring("attn", GH, P)
        eg, lg, sgate = ring("eg", E), ring("lg", E), ring("sgate", E)
        og, osq, oT = ring("og", E), ring("osq", E), ring("oT", E)
        ms, rr = ring("ms", GH), ring("rr", GH)

        loaded, pre = c.sem(ctx, "la_loaded"), c.sem(ctx, "la_pre")
        st = lambda name, *names: c.steps(ctx, "la_" + name, *names)
        v_norm = st("v_norm", "norm", "scaled", "shifted")
        p_h, a_h = st("p_h", "hT"), st("a_h", "hT")
        p_proj = st("p_proj", "z", "y", "v", "g1")
        a_proj = st("a_proj", "exz", "exy", "y", "v", "g1")
        v_clip = st("v_clip", "exz", "exy")
        a_sig = st("a_sig", "ln", "sg")
        v_kq = st("v_kq", "cum", "last", "k", "q")
        g_dist = st("g_dist", *[f"d{k}" for k in range(NLEV)])
        v_abs = st("v_abs", "abs")
        a_dec = st("a_dec", "start", "end", "base", "inv", "levels")
        v_qk = st("v_qk", "qe", "ke")
        g_qk = st("g_qk", "qs", "kend")
        p_att = st("p_att", "l0123", "l4", "kendT", "gate")
        v_att = st("v_att", *[f"m{k}" for k in range(NLEV)], "clip")
        a_kend = st("a_kend", "kendT", "eg")
        a_gate = st("a_gate", "ln", "sg")
        p_out = st("p_out", "o", "state")
        v_state = st("v_state", "s0", "s1", "og")
        a_sq = st("a_sq", "sq")
        v_ms = st("v_ms", "sum", "eps")
        g_rr = st("g_rr", "pow")
        v_on = st("v_on", "on")
        p_oT, a_oT = st("p_oT", "oT"), st("a_oT", "oT")
        p_wo, v_x = st("p_wo", "wo"), st("v_x", "x")
        every = [v_norm, p_h, a_h, p_proj, a_proj, v_clip, a_sig, v_kq, g_dist, v_abs, a_dec, v_qk, g_qk, p_att,
                 v_att, a_kend, a_gate, p_out, v_state, a_sq, v_ms, g_rr, v_on, p_oT, a_oT, p_wo, v_x]
        LOADS = 10

        with nc.Block() as block:

            @block.sync
            def _(sp):
                for t, name in ((wk, "L0_attn_Wk"), (wq, "L0_attn_Wq"), (wv, "L0_attn_Wv"), (g1, "L0_attn_G1"),
                                (g2, "L0_attn_G2"), (wo, "L0_attn_Wo"), (masks, "level_masks")):
                    sp.dma_start(t[...], inp[name]).then_inc(loaded, 16)
                sp.dma_start(delta[:, 1:2], inp["L0_attn_delta"].unsqueeze(1)).then_inc(loaded, 16)
                sp.dma_start(norm_w[:, :], inp["L0_attn_norm_w"].unsqueeze(1)).then_inc(loaded, 16)
                sp.dma_start(reset[:, :], inp["batch_reset"]).then_inc(loaded, 16)

            @block.gpsimd
            def _(gp):
                prime(gp, every)
                nc.gpsimd.memset(attn[...], 0.0)
                nc.gpsimd.memset(ones[:, :], 1.0)
                nc.gpsimd.memset(state[:, :], 0.0)

            @block.vector
            def _(dve):
                dve.wait_ge(loaded, 16 * LOADS)
                nc.vector.tensor_scalar(delta[:, 0:1], delta[:, 1:2], -1.0, None, ALU.mult).then_inc(pre, 1)
                nc.vector.tensor_scalar(wo[:, :], wo[:, :], norm_w[:, 0:1], None, ALU.mult).then_inc(pre, 1)
                dve.wait_ge(pre, 2)
                nc.vector.tensor_tensor(wog[:, :, :], rows_bc(wo[:, :], B), c.mod[:, 0, :, GA, :],
                                        ALU.mult).then_inc(pre, 1)
                dve.wait_ge(pre, 3)

        with nc.Block() as block:

            @block.vector
            def _(dve):

                def norm(i, u):
                    modulate(c, dve, v_norm, rows[:, u, :], i, 0, SA, CA)

                def clip(i, u):
                    dve.wait_ge(a_proj.sem, a_proj.at("exz", i))
                    nc.vector.tensor_scalar_min(ex[:, u, 0, :], ex[:, u, 0, :], MAX_EXP).then_inc(v_clip("exz"), 1)
                    dve.wait_ge(a_proj.sem, a_proj.at("exy", i))
                    nc.vector.tensor_scalar_min(ex[:, u, 1, :], ex[:, u, 1, :], MAX_SIG).then_inc(v_clip("exy"), 1)

                def keys(i, u):
                    dve.wait_ge(a_sig.sem, a_sig.at("ln", i))
                    nc.vector.tensor_tensor_scan(cum[:, u, :], ones[:, :], ln[:, u, 0, :], 0.0, ALU.mult, ALU.add)\
                      .then_inc(v_kq("cum"), 1)
                    dve.wait_ge(v_kq.sem, v_kq.at("cum", i))
                    nc.vector.tensor_scalar(last[:, u, :], cum[:, u, P - 1:P], -1.0, None, ALU.mult)\
                      .then_inc(v_kq("last"), 1)
                    dve.wait_ge(a_sig.sem, a_sig.at("sg", i))
                    nc.vector.tensor_tensor(kq[:, u, 0, :], ex[:, u, 0, :], sg[:, u, 0, :], ALU.mult)\
                      .then_inc(v_kq("k"), 1)
                    nc.vector.tensor_tensor(kq[:, u, 1, :], y[:, u, :], sg[:, u, 1, :], ALU.mult)\
                      .then_inc(v_kq("q"), 1)

                def absolute(i, u):
                    dve.wait_ge(g_dist.sem, g_dist.at(f"d{NLEV - 1}", i))
                    d = dist[:, u, 1:, :]
                    nc.vector.scalar_tensor_tensor(out=d, in0=d, scalar=-1.0, in1=d, op0=ALU.mult, op1=ALU.min)\
                      .then_inc(v_abs("abs"), 1)

                def scaled(i, u):
                    dve.wait_ge(a_dec.sem, a_dec.at("levels", i))
                    nc.vector.tensor_tensor(qe[:, u, :, :], dec[:, u, 0:NLEV, :], rows_bc(kq[:, u, 1, :], NLEV),
                                            ALU.mult).then_inc(v_qk("qe"), 1)
                    nc.vector.tensor_tensor(ke[:, u, :, :], dec[:, u, 1:NLEV + 1, :],
                                            rows_bc(kq[:, u, 0, :], NLEV), ALU.mult).then_inc(v_qk("ke"), 1)

                def levels(i, u):
                    for k in range(NLEV):
                        dve.wait_ge(p_att.sem, p_att.at(level_step[k], i))
                        if k:
                            dve.wait_ge(v_att.sem, v_att.at(f"m{k - 1}", i))
                        dve.nop(nofuse=True)
                        nc.vector.copy_predicated(attn[:, u, :, :], rows_bc(masks[:, k, :], GH), level[k])\
                          .then_inc(v_att(f"m{k}"), 1)
                    dve.wait_ge(a_kend.sem, a_kend.at("eg", i))
                    nc.vector.tensor_scalar_min(eg[:, u, :], eg[:, u, :], MAX_SIG).then_inc(v_att("clip"), 1)

                def update(i, u):
                    dve.wait_ge(p_out.sem, p_out.at("state", i))
                    for h in range(GH):
                        s = slice(GD * h, GD * h + GD)
                        nc.vector.scalar_tensor_tensor(
                            out=state[s, s], in0=state[s, s], scalar=dstart[s, u, P - 1:P],
                            in1=out[s, E + GD * h:E + GD * h + GD], op0=ALU.mult, op1=ALU.add)\
                          .then_inc(v_state(f"s{h}"), 1)
                    dve.wait_ge(a_gate.sem, a_gate.at("sg", i))
                    nc.vector.tensor_tensor(og[:, u, :], out[:, 0:E], sgate[:, u, :], ALU.mult)\
                      .then_inc(v_state("og"), 1)

                def mean_square(i, u):
                    dve.wait_ge(a_sq.sem, a_sq.at("sq", i))
                    nc.vector.tensor_reduce(ms[:, u, :], osq[:, u, :].rearrange("p (h d) -> p h d", h=GH), AX_X,
                                            ALU.add).then_inc(v_ms("sum"), 1)
                    dve.wait_ge(v_ms.sem, v_ms.at("sum", i))
                    nc.vector.tensor_scalar(ms[:, u, :], ms[:, u, :], 1.0 / GD, 1e-5, ALU.mult, ALU.add)\
                      .then_inc(v_ms("eps"), 1)

                def normed(i, u):
                    dve.wait_ge(g_rr.sem, g_rr.at("pow", i))
                    o3 = og[:, u, :].rearrange("p (h d) -> p h d", h=GH)
                    nc.vector.tensor_tensor(o3, o3, cols_bc(rr[:, u, :], GD), ALU.mult).then_inc(v_on("on"), 1)

                def residual(i, u):
                    dve.wait_ge(p_wo.sem, p_wo.at("wo", i))
                    nc.vector.tensor_tensor(c.x[:, i, :], c.x[:, i, :], small[:, 0:P], ALU.add)\
                      .then_inc(v_x("x"), 1)

                pipeline(dve, [(keys, 2), (update, 4), (normed, 5), (absolute, 2), (levels, 3), (clip, 1),
                               (scaled, 2), (mean_square, 4), (norm, 0), (residual, 5)])

            @block.gpsimd
            def _(gp):

                def distances(i, u):
                    gp.wait_ge(v_kq.sem, v_kq.at("cum", i))
                    for k, h in enumerate(HALVES):
                        blocks = cum[:, u, :].rearrange("p (n w) -> p n w", w=2 * h)
                        nc.gpsimd.tensor_tensor(dist[:, u, k, :].rearrange("p (n w) -> p n w", w=2 * h), blocks,
                                                blocks[:, :, h - 1:h].broadcast_to([P, P // (2 * h), 2 * h]),
                                                ALU.subtract).then_inc(g_dist(f"d{k}"), 1)

                def ends(i, u):
                    gp.wait_ge(v_kq.sem, v_kq.at("q", i))
                    gp.wait_ge(a_dec.sem, a_dec.at("end", i))
                    nc.gpsimd.tensor_tensor(qs[:, u, :], kq[:, u, 1, :], dstart[:, u, :], ALU.mult)\
                      .then_inc(g_qk("qs"), 1)
                    nc.gpsimd.tensor_tensor(kend[:, u, :], kq[:, u, 0, :], dend[:, u, :], ALU.mult)\
                      .then_inc(g_qk("kend"), 1)

                def inverse_rms(i, u):
                    gp.wait_ge(v_ms.sem, v_ms.at("eps", i))
                    nc.gpsimd.tensor_tensor(rr[:, u, :], ms[:, u, :], c.minus_half[:, 0:GH], ALU.pow)\
                      .then_inc(g_rr("pow"), 1)

                pipeline(gp, [(distances, 2), (ends, 2), (inverse_rms, 4)])

            @block.scalar
            def _(act):

                def kend_rows(i, u):
                    act.wait_ge(p_att.sem, p_att.at("gate", i))
                    nc.scalar.activation(kendT[:, u, :], tr[:, 0:P], ACT.Copy).then_inc(a_kend("kendT"), 1)
                    nc.scalar.activation(eg[:, u, :], tr[:, 2 * P:3 * P], ACT.Exp, scale=-1.0)\
                      .then_inc(a_kend("eg"), 1)

                def square(i, u):
                    act.wait_ge(v_state.sem, v_state.at("og", i))
                    nc.scalar.activation(osq[:, u, :], og[:, u, :], ACT.Square).then_inc(a_sq("sq"), 1)

                def o_columns(i, u):
                    act.wait_ge(p_oT.sem, p_oT.at("oT", i))
                    nc.scalar.activation(oT[:, u, :], tr[:, P:2 * P], ACT.Copy).then_inc(a_oT("oT"), 1)

                def decays(i, u):
                    act.wait_ge(v_kq.sem, v_kq.at("last", i))
                    nc.scalar.activation(dstart[:, u, :], cum[:, u, :], ACT.Exp, scale=-1.0,
                                         bias=reset[:, bass.ds(i, 1)]).then_inc(a_dec("start"), 1)
                    nc.scalar.activation(dend[:, u, :], cum[:, u, :], ACT.Exp, bias=last[:, u, :])\
                      .then_inc(a_dec("end"), 1)
                    act.wait_ge(g_dist.sem, g_dist.at("d0", i))
                    nc.scalar.activation(dec[:, u, 0, :], dist[:, u, 0, :], ACT.Exp, scale=-1.0)\
                      .then_inc(a_dec("base"), 1)
                    nc.scalar.activation(dec[:, u, NLEV, :], dist[:, u, 0, :], ACT.Exp).then_inc(a_dec("inv"), 1)
                    act.wait_ge(v_abs.sem, v_abs.at("abs", i))
                    nc.scalar.activation(dec[:, u, 1:NLEV, :], dist[:, u, 1:NLEV, :], ACT.Exp)\
                      .then_inc(a_dec("levels"), 1)

                def projections(i, u):
                    act.wait_ge(p_proj.sem, p_proj.at("g1", i))
                    nc.scalar.activation(ex[:, u, 0, :], proj[:, 0:P], ACT.Exp, bias=delta[:, 0:1], scale=-1.0)\
                      .then_inc(a_proj("exz"), 1)
                    nc.scalar.activation(ex[:, u, 1, :], proj[:, P:2 * P], ACT.Exp, scale=-1.0)\
                      .then_inc(a_proj("exy"), 1)
                    nc.scalar.activation(y[:, u, :], proj[:, P:2 * P], ACT.Copy).then_inc(a_proj("y"), 1)
                    nc.scalar.activation(v[:, u, :], proj[:, 2 * P:3 * P], ACT.Copy).then_inc(a_proj("v"), 1)
                    nc.scalar.activation(g1T[0:GD, u, :], proj[0:GD, 3 * P:4 * P], ACT.Copy)\
                      .then_inc(a_proj("g1"), 1)

                def sigmoids(i, u):
                    act.wait_ge(v_clip.sem, v_clip.at("exy", i))
                    nc.scalar.activation(ln[:, u, :, :], ex[:, u, :, :], ACT.Ln, bias=1.0).then_inc(a_sig("ln"), 1)
                    act.wait_ge(a_sig.sem, a_sig.at("ln", i))
                    nc.scalar.activation(sg[:, u, :, :], ln[:, u, :, :], ACT.Exp, scale=-1.0).then_inc(a_sig("sg"), 1)

                def gate(i, u):
                    act.wait_ge(v_att.sem, v_att.at("clip", i))
                    nc.scalar.activation(lg[:, u, :], eg[:, u, :], ACT.Ln, bias=1.0).then_inc(a_gate("ln"), 1)
                    act.wait_ge(a_gate.sem, a_gate.at("ln", i))
                    nc.scalar.activation(sgate[:, u, :], lg[:, u, :], ACT.Exp, scale=-1.0).then_inc(a_gate("sg"), 1)

                def h_columns(i, u):
                    act.wait_ge(p_h.sem, p_h.at("hT", i))
                    nc.scalar.activation(hT[:, u, :], small[:, 0:P], ACT.Copy).then_inc(a_h("hT"), 1)

                nc.scalar.preload_act_table_set("natural_log_exp_and_others")
                pipeline(act, [(kend_rows, 3), (square, 4), (o_columns, 5), (decays, 2), (projections, 1),
                               (gate, 3), (sigmoids, 1), (h_columns, 0)])

            @block.tensor
            def _(pe):

                def output(i, u):
                    pe.wait_ge(v_state.sem, v_state.at("og", i - 1))
                    pe.wait_ge(g_qk.sem, g_qk.at("qs", i))
                    nc.tensor.matmul(out[:, 0:E], qs[:, u, :], state[:, :], start=True, stop=True)
                    pe.wait_ge(v_att.sem, v_att.at(f"m{NLEV - 1}", i))
                    for h in range(GH):
                        m = nc.tensor.matmul(out[:, GD * h:GD * h + GD], attn[:, u, h, :],
                                             v[:, u, GD * h:GD * h + GD], start=False, stop=True,
                                             skip_group_check=True)
                    m.then_inc(p_out("o"), 1)
                    pe.wait_ge(a_kend.sem, a_kend.at("kendT", i))
                    nc.tensor.matmul(out[:, E:2 * E], kendT[:, u, :], v[:, u, :], start=True, stop=True)\
                      .then_inc(p_out("state"), 1)

                def scores(i, u):
                    pe.wait_ge(v_qk.sem, v_qk.at("ke", i))
                    for k in range(NLEV):
                        pe.wait_ge(v_att.sem, v_att.at("m3" if k < 4 else "m4", i - 1))
                        for h in range(GH):
                            s = slice(GD * h, GD * h + GD)
                            lv = (k + NLEV - 1) % NLEV
                            m = nc.tensor.matmul(level[k][:, h, :], ke[s, u, lv, :], qe[s, u, k, :],
                                                 start=True, stop=True)
                        if k >= 3:
                            m.then_inc(p_att(level_step[k]), 1)
                    pe.wait_ge(g_qk.sem, g_qk.at("kend", i))
                    pe.wait_ge(a_oT.sem, a_oT.at("oT", i - 3))
                    nc.tensor.transpose(tr[:, 0:P], kend[:, u, :], c.ident[:, :]).then_inc(p_att("kendT"), 1)
                    nc.tensor.matmul(tr[:, 2 * P:3 * P], g1T[0:GD, u, :], g2[:, :], start=True, stop=True)\
                      .then_inc(p_att("gate"), 1)

                def o_turn(i, u):
                    pe.wait_ge(a_kend.sem, a_kend.at("eg", i + 2))
                    pe.wait_ge(v_on.sem, v_on.at("on", i))
                    nc.tensor.transpose(tr[:, P:2 * P], og[:, u, :], c.ident[:, :]).then_inc(p_oT("oT"), 1)

                def project(i, u):
                    pe.wait_ge(a_h.sem, a_h.at("hT", i))
                    pe.wait_ge(a_proj.sem, a_proj.at("g1", i - 1))
                    nc.tensor.matmul(proj[:, 0:P], wk[:, :], hT[:, u, :], start=True, stop=True)\
                      .then_inc(p_proj("z"), 1)
                    nc.tensor.matmul(proj[:, P:2 * P], wq[:, :], hT[:, u, :], start=True, stop=True)\
                      .then_inc(p_proj("y"), 1)
                    nc.tensor.matmul(proj[:, 2 * P:3 * P], hT[:, u, :], wv[:, :], start=True, stop=True)\
                      .then_inc(p_proj("v"), 1)
                    nc.tensor.matmul(proj[0:GD, 3 * P:4 * P], g1[:, :], hT[:, u, :], start=True, stop=True)\
                      .then_inc(p_proj("g1"), 1)

                def o_project(i, u):
                    pe.wait_ge(a_oT.sem, a_oT.at("oT", i))
                    pe.wait_ge(a_h.sem, a_h.at("hT", i + 4))
                    nc.tensor.matmul(small[:, 0:P], oT[:, u, :], wog[:, i // NT, :], start=True, stop=True)\
                      .then_inc(p_wo("wo"), 1)

                def h_turn(i, u):
                    pe.wait_ge(v_norm.sem, v_norm.at("shifted", i))
                    pe.wait_ge(v_x.sem, v_x.at("x", i - 5))
                    pe.wait_ge(a_h.sem, a_h.at("hT", i - 1))
                    nc.tensor.transpose(small[:, 0:P], rows[:, u, :], c.ident[:, :]).then_inc(p_h("hT"), 1)

                pipeline(pe, [(output, 4), (scores, 3), (o_turn, 5), (project, 1), (o_project, 5), (h_turn, 0)])


def start_layers(c, y):
    nc = c.nc
    with ExitStack() as ctx:
        v_norm = c.steps(ctx, "sl_norm", "norm", "scaled", "shifted")
        with nc.Block() as block:

            @block.gpsimd
            def _(gp):
                prime(gp, [v_norm])

            @block.vector
            def _(dve):
                dve.wait_ge(v_norm.sem, PRIMED * 3)
                with dve.Fori(0, TILES) as i:
                    modulate(c, dve, v_norm, y[:, i, :], i, 0, SB, CB)


def end_layers(c, y):
    nc = c.nc
    with ExitStack() as ctx:
        done = c.sem(ctx, "el_done")
        with nc.Block() as block:

            @block.vector
            def _(dve):
                for b in range(B):
                    t = slice(b * NT, b * NT + NT)
                    nc.vector.tensor_tensor(y[:, t, :], y[:, t, :], rows_bc(c.mod[:, 0, b, GB, :], NT), ALU.mult)\
                      .then_inc(done, 1)
                    dve.wait_ge(done, 2 * b + 1)
                    nc.vector.tensor_tensor(c.x[:, t, :], c.x[:, t, :], y[:, t, :], ALU.add).then_inc(done, 1)


def windowed_attention(c, y, ctx):
    nc, inp, bk = c.nc, c.inp, c.bank
    sb = c.sb(ctx)
    wqkv = sb("wa_wqkv", [P, 3 * INNER])
    wo = sb("wa_wo", [P, INNER // P, E])
    tabs = sb("wa_tabs", [P, 4, NT, WD])
    scales = sb("wa_scales", [P, 4, WD])
    bias32 = sb("wa_bias32", [P, 2, P])
    bias = sb("wa_bias", [P, 2, P], BF16)
    identb = sb("wa_identb", [P, P], BF16)
    keep = sb("wa_keep", [P, TILES + 1])
    ring = lambda name, *shape: sb("wa_" + name, [P, RING, *shape])
    rows, hT = ring("rows", E), ring("hT", P + 1)
    ks = ring("v", INNER)
    vm = ring("vm", INNER)
    pair = lambda name, *shape: sb("wa_" + name, [P, 2, *shape])
    sq = pair("sq", 2, INNER)
    ss, rn, rq = ring("ss", 2 * WH), ring("rn", 2 * WH), ring("rq", WH)
    qr, kr = ring("qr", INNER), ring("kr", INNER)
    tmp = pair("tmp", 2, INNER)
    qT, kT = pair("qT", WH // 2, P), pair("kT", WH // 2, P)
    kbT = pair("kbT", WH // 2, WIN)
    mx, nb, rs, rrs = (ring(n, WH) for n in ("mx", "nb", "rs", "rrs"))
    pr = pair("p", WH, P)
    pT = pair("pT", 2, WH // 2, P)
    ob, oT = pair("o", INNER), pair("oT", INNER // P, P)

    loaded, pre = c.sem(ctx, "wa_loaded"), c.sem(ctx, "wa_pre")
    st = lambda name, *names: c.steps(ctx, "wa_" + name, *names)
    g_stage = st("g_stage", "rows")
    p_h, a_h = st("p_h", "hT"), st("a_h", "lo", "hi", "carry")
    p_qkv = st("p_qkv", "q", "k", "v")
    a_sq = st("a_sq", "q", "k", "v")
    v_rot = st("v_rot", "q1", "q2", "q3", "k1", "k2", "k3")
    v_ss = st("v_ss", "sum", "clip")
    g_rot = st("g_rot", "q", "pow", "k", "vlo", "vhi")
    v_scale = st("v_scale", "rq", "k")
    p_turn = st("p_turn", "qT", "kT")
    a_turn = st("a_turn", "qT", "kT", "kbT")
    p_sim = st("p_sim", "s")
    v_max = st("v_max", "m0", "m1", "nb")
    a_exp = st("a_exp", *[f"e{h}" for h in range(WH)])
    p_pT, a_pT = st("p_pT", "even", "odd"), st("a_pT", "even", "odd")
    p_pv = st("p_pv", "o")
    v_o = st("v_o", "rrs", "o")
    p_oT, a_oT = st("p_oT", "oT"), st("a_oT", "oT")
    p_wo, v_y = st("p_wo", "wo"), st("v_y", "y")
    every = [g_stage, p_h, a_h, p_qkv, a_sq, v_rot, v_ss, g_rot, v_scale, p_turn, a_turn, p_sim, v_max, a_exp,
             p_pT, a_pT, p_pv, v_o, p_oT, a_oT, p_wo, v_y]

    def prepare():
        with nc.Block() as block:

            @block.gpsimd
            def _(gp):
                prime(gp, every)
                nc.gpsimd.memset(kbT[...], 0.0)
                nc.gpsimd.memset(vm[...], 0.0)
                nc.gpsimd.memset(hT[...], 0.0)

            @block.sync
            def _(sp):
                for t, name in ((bias32, "window_bias"), (keep, "batch_keep")):
                    sp.dma_start(t[...], inp[name]).then_inc(loaded, 16)

            @block.vector
            def _(dve):
                nc.vector.tensor_copy(identb[:, :], c.ident[:, :]).then_inc(pre, 1)
                dve.wait_ge(loaded, 32)
                nc.vector.tensor_copy(bias[...], bias32[...]).then_inc(pre, 1)
                dve.wait_ge(pre, 2)

    def load_layer(l):
        n = 10
        with nc.Block() as block:

            @block.sync
            def _(sp):
                li = bass.ds(l, 1)
                sp.dma_start(tabs[...], inp["rotations"]).then_inc(loaded, 16)
                for k, name in enumerate(("L0_ffn_q_scale", "L0_ffn_k_scale")):
                    row = inp[name][li, :]
                    h = WD // 2
                    for dst, lo in ((scales[:, 2 * k, :], 0), (scales[:, 2 * k + 1, 0:h], h),
                                    (scales[:, 2 * k + 1, h:WD], 0)):
                        w = dst.shape[1]
                        sp.dma_start(dst, row[:, lo:lo + w].broadcast_to([P, w])).then_inc(loaded, 16)
                sp.dma_start(wqkv[:, :], inp["L0_ffn_wqkv"][li, :, :].rearrange("a e n -> (a e) n"))\
                  .then_inc(loaded, 16)
                sp.dma_start(wo[...], inp["L0_ffn_wo"][li, :, :].rearrange("a (c p) e -> p (a c) e", p=P))\
                  .then_inc(loaded, 16)

            @block.vector
            def _(dve):
                dve.wait_ge(loaded, l * (16 * 9) + 16 * 11)
                for k in range(4):
                    nc.vector.tensor_tensor(tabs[:, k, :, :], tabs[:, k, :, :], rows_bc(scales[:, k, :], NT),
                                            ALU.mult).then_inc(pre, 1)
                dve.wait_ge(pre, 4 * l + 6)
                dve.nop(nofuse=True)

    def run(l):
        for s in every:
            s.base = l * TILES
        q_bank, k_bank, v_bank, hw_bank, turn_bank, even, odd, o_bank = bk
        heads = lambda ap: ap.rearrange("p (h d) -> p h d", d=WD)
        with nc.Block() as block:

            @block.gpsimd
            def _(gp):

                def stage(i, u):
                    gp.wait_ge(g_rot.sem, g_rot.at("vhi", i - 2))
                    gp.nop(nofuse=True)
                    nc.gpsimd.tensor_copy(rows[:, u, :], y[:, i, :]).then_inc(g_stage("rows"), 1)

                def rotate(i, u):
                    gp.wait_ge(g_rot.sem, g_rot.at("vhi", i - 1))
                    gp.wait_ge(v_rot.sem, v_rot.at("q3", i))
                    nc.gpsimd.tensor_tensor(qr[:, u, :], qr[:, u, :], tmp[:, u % 2, 0, :], ALU.add)\
                      .then_inc(g_rot("q"), 1)
                    gp.wait_ge(v_ss.sem, v_ss.at("clip", i))
                    nc.gpsimd.tensor_tensor(rn[:, u, :], ss[:, u, :], c.minus_half[:, 0:2 * WH], ALU.pow)\
                      .then_inc(g_rot("pow"), 1)
                    gp.wait_ge(v_rot.sem, v_rot.at("k3", i))
                    nc.gpsimd.tensor_tensor(kr[:, u, :], kr[:, u, :], tmp[:, u % 2, 1, :], ALU.add)\
                      .then_inc(g_rot("k"), 1)
                    gp.wait_ge(a_sq.sem, a_sq.at("v", i))
                    gp.wait_ge(g_rot.sem, g_rot.at("k", i))
                    gp.nop(nofuse=True)
                    nc.gpsimd.tensor_copy(vm[0:WIN, u, :], ks[0:WIN, u, :]).then_inc(g_rot("vlo"), 1)
                    gp.wait_ge(g_rot.sem, g_rot.at("vlo", i))
                    gp.nop(nofuse=True)
                    nc.gpsimd.tensor_copy(vm[WIN:P, (u + 1) % RING, :], ks[WIN:P, u, :]).then_inc(g_rot("vhi"), 1)

                pipeline(gp, [(stage, 0), (rotate, 1)])

            @block.vector
            def _(dve):

                def rotate(i, u):
                    for k, (name, bank, dst) in enumerate((("q", q_bank, qr), ("k", k_bank, kr))):
                        src, out, cross = heads(bank), heads(dst[:, u, :]), heads(tmp[:, u % 2, k, :])
                        cos, sin = tabs[:, 2 * k, i % NT, :], tabs[:, 2 * k + 1, i % NT, :]
                        h = WD // 2
                        dve.wait_ge(a_sq.sem, a_sq.at(name, i))
                        nc.vector.tensor_tensor(out, src, rows_bc(cos, WH), ALU.mult).then_inc(v_rot(name + "1"), 1)
                        nc.vector.tensor_tensor(cross[:, :, 0:h], src[:, :, h:WD], rows_bc(sin[:, 0:h], WH),
                                                ALU.mult).then_inc(v_rot(name + "2"), 1)
                        nc.vector.tensor_tensor(cross[:, :, h:WD], src[:, :, 0:h], rows_bc(sin[:, h:WD], WH),
                                                ALU.mult).then_inc(v_rot(name + "3"), 1)

                def norms(i, u):
                    nc.vector.tensor_reduce(ss[:, u, :], sq[:, u % 2, :, :].rearrange("p a (h d) -> p (a h) d", d=WD),
                                            AX_X, ALU.add).then_inc(v_ss("sum"), 1)
                    dve.wait_ge(v_ss.sem, v_ss.at("sum", i))
                    nc.vector.tensor_scalar_max(ss[:, u, :], ss[:, u, :], 1e-24).then_inc(v_ss("clip"), 1)

                def scale(i, u):
                    dve.wait_ge(g_rot.sem, g_rot.at("pow", i))
                    nc.vector.tensor_scalar(rq[:, u, :], rn[:, u, 0:WH], QK_SCALE, None, ALU.mult)\
                      .then_inc(v_scale("rq"), 1)
                    dve.wait_ge(g_rot.sem, g_rot.at("k", i))
                    kh = heads(kr[:, u, :])
                    nc.vector.tensor_tensor(kh, kh, cols_bc(rn[:, u, WH:2 * WH], WD), ALU.mult)\
                      .then_inc(v_scale("k"), 1)

                def row_max(i, u):
                    dve.wait_ge(p_sim.sem, p_sim.at("s", i))
                    m = mx[:, u, :].rearrange("p (h r) -> p r h", r=2)
                    for r, bank in enumerate((even, odd)):
                        nc.vector.tensor_reduce(m[:, r, :], bank.rearrange("p (h k) -> p h k", k=P), AX_X, ALU.max)\
                          .then_inc(v_max(f"m{r}"), 1)
                    dve.wait_ge(v_max.sem, v_max.at("m1", i))
                    nc.vector.scalar_tensor_tensor(out=nb[:, u, :], in0=mx[:, u, :], scalar=-1.0, in1=rq[:, u, :],
                                                   op0=ALU.mult, op1=ALU.mult).then_inc(v_max("nb"), 1)

                def output(i, u):
                    dve.wait_ge(a_exp.sem, a_exp.at(f"e{WH - 1}", i))
                    nc.vector.reciprocal(rrs[:, u, :], rs[:, u, :]).then_inc(v_o("rrs"), 1)
                    dve.wait_ge(v_o.sem, v_o.at("rrs", i))
                    dve.wait_ge(p_pv.sem, p_pv.at("o", i))
                    nc.vector.tensor_tensor(heads(ob[:, u % 2, :]), heads(o_bank), cols_bc(rrs[:, u, :], WD), ALU.mult)\
                      .then_inc(v_o("o"), 1)

                def residual(i, u):
                    dve.wait_ge(p_wo.sem, p_wo.at("wo", i))
                    nc.vector.tensor_tensor(y[:, i, :], y[:, i, :], hw_bank[:, 0:E], ALU.add).then_inc(v_y("y"), 1)

                pipeline(dve, [(rotate, 1), (residual, 4), (norms, 1), (output, 3), (scale, 1), (row_max, 2)])

            @block.scalar
            def _(act):

                def o_columns(i, u):
                    act.wait_ge(p_oT.sem, p_oT.at("oT", i))
                    nc.scalar.activation(oT[:, u % 2, :, :].rearrange("p c t -> p (c t)"), turn_bank, ACT.Copy)\
                      .then_inc(a_oT("oT"), 1)

                def squares(i, u):
                    for k, (name, bank) in enumerate((("q", q_bank), ("k", k_bank))):
                        act.wait_ge(p_qkv.sem, p_qkv.at(name, i))
                        nc.scalar.activation(sq[:, u % 2, k, :], bank, ACT.Square).then_inc(a_sq(name), 1)
                    act.wait_ge(p_qkv.sem, p_qkv.at("v", i))
                    nc.scalar.activation(ks[:, u, :], v_bank, ACT.Copy).then_inc(a_sq("v"), 1)

                def turned(name, dst):
                    def f(i, u):
                        act.wait_ge(p_turn.sem, p_turn.at(name, i))
                        nc.scalar.activation(dst[:, u % 2, :, :].rearrange("p c t -> p (c t)"), turn_bank, ACT.Copy)\
                          .then_inc(a_turn(name), 1)
                        if name == "kT":
                            last = turn_bank.rearrange("p (c t) -> p c t", t=P)[:, :, WIN:P]
                            nc.scalar.activation(kbT[:, (u + 1) % 2, :, :], last, ACT.Copy,
                                                 scale=keep[:, bass.ds(i + 1, 1)]).then_inc(a_turn("kbT"), 1)
                    return f

                def p_columns(i, u):
                    for r, (name, bank) in enumerate((("even", even), ("odd", odd))):
                        act.wait_ge(p_pT.sem, p_pT.at(name, i))
                        nc.scalar.activation(pT[:, u % 2, r, :, :].rearrange("p c t -> p (c t)"), bank, ACT.Copy)\
                          .then_inc(a_pT(name), 1)

                def h_columns(i, u):
                    h = E // 2
                    act.wait_ge(p_h.sem, p_h.at("hT", i))
                    nc.scalar.activation(hT[0:h, u, 0:P], hw_bank[0:h, 0:P], ACT.Copy).then_inc(a_h("lo"), 1)
                    nc.scalar.activation(hT[h:P, u, 1:P + 1], hw_bank[h:P, 0:P], ACT.Copy).then_inc(a_h("hi"), 1)
                    act.wait_ge(a_h.sem, a_h.at("hi", i - 1))
                    nc.scalar.activation(hT[h:P, u, 0:1], hT[h:P, (u - 1) % RING, P:P + 1], ACT.Copy,
                                         scale=keep[h:P, bass.ds(i, 1)]).then_inc(a_h("carry"), 1)

                def exps(i, u):
                    act.wait_ge(v_max.sem, v_max.at("nb", i))
                    for h in range(WH):
                        bank = (even, odd)[h % 2]
                        nc.scalar.activation(pr[:, u % 2, h, :], bank[:, P * (h // 2):P * (h // 2) + P], ACT.Exp,
                                             bias=nb[:, u, h:h + 1], scale=rq[:, u, h:h + 1],
                                             accum_out=rs[:, u, h:h + 1]).then_inc(a_exp(f"e{h}"), 1)

                nc.scalar.preload_act_table_set("natural_log_exp_and_others")
                pipeline(act, [(o_columns, 4), (squares, 1), (turned("qT", qT), 2), (p_columns, 3),
                               (turned("kT", kT), 2), (h_columns, 0), (exps, 2)])

            @block.tensor
            def _(pe):

                def turn_o(i, u):
                    pe.wait_ge(v_o.sem, v_o.at("o", i))
                    pe.wait_ge(a_turn.sem, a_turn.at("kbT", i + 1))
                    for k in range(INNER // P):
                        m = nc.tensor.transpose(turn_bank[:, P * k:P * k + P], ob[:, u % 2, P * k:P * k + P],
                                                c.ident[:, :])
                    m.then_inc(p_oT("oT"), 1)

                def qkv(i, u):
                    pe.wait_ge(a_h.sem, a_h.at("carry", i))
                    for k, (name, bank) in enumerate((("q", q_bank), ("k", k_bank), ("v", v_bank))):
                        if name == "v":
                            pe.wait_ge(a_sq.sem, a_sq.at("v", i - 1))
                        else:
                            pe.wait_ge(v_rot.sem, v_rot.at(name + "3", i - 1))
                        nc.tensor.matmul(bank, hT[:, u, 0:P], wqkv[:, INNER * k:INNER * k + INNER], start=True,
                                         stop=True).then_inc(p_qkv(name), 1)

                def project(i, u):
                    pe.wait_ge(a_oT.sem, a_oT.at("oT", i))
                    pe.wait_ge(a_h.sem, a_h.at("carry", i + 3))
                    n = INNER // P
                    for k in range(n):
                        m = nc.tensor.matmul(hw_bank[:, 0:E], oT[:, u % 2, k, :], wo[:, k, :], start=k == 0,
                                             stop=k == n - 1)
                    m.then_inc(p_wo("wo"), 1)

                def turn_q(i, u):
                    pe.wait_ge(g_rot.sem, g_rot.at("q", i))
                    pe.wait_ge(a_oT.sem, a_oT.at("oT", i - 2))
                    for k in range(WH // 2):
                        m = nc.tensor.transpose(turn_bank[:, P * k:P * k + P], qr[:, u, P * k:P * k + P],
                                                c.ident[:, :])
                    m.then_inc(p_turn("qT"), 1)

                def turn_p(i, u):
                    pe.wait_ge(a_exp.sem, a_exp.at(f"e{WH - 1}", i))
                    for r, (name, bank) in enumerate((("even", even), ("odd", odd))):
                        for k in range(WH // 2):
                            m = nc.tensor.transpose(bank[:, P * k:P * k + P], pr[:, u % 2, 2 * k + r, :],
                                                    c.ident[:, :])
                        m.then_inc(p_pT(name), 1)

                def turn_k(i, u):
                    pe.wait_ge(v_scale.sem, v_scale.at("k", i))
                    pe.wait_ge(a_turn.sem, a_turn.at("qT", i))
                    for k in range(WH // 2):
                        m = nc.tensor.transpose(turn_bank[:, P * k:P * k + P], kr[:, u, P * k:P * k + P],
                                                c.ident[:, :])
                    m.then_inc(p_turn("kT"), 1)

                def values(i, u):
                    pe.wait_ge(a_pT.sem, a_pT.at("odd", i))
                    pe.wait_ge(v_o.sem, v_o.at("o", i - 1))
                    pe.wait_ge(g_rot.sem, g_rot.at("vlo", i))
                    for h in range(WH):
                        p, d = pT[:, u % 2, h % 2, h // 2, :], slice(WD * h, WD * h + WD)
                        nc.tensor.matmul(o_bank[0:WIN, d], p[:, 0:WIN], vm[:, u, d], start=True, stop=True)
                        m = nc.tensor.matmul(o_bank[WIN:P, d], p[:, WIN:P], ks[:, u, d], start=True, stop=True)
                    m.then_inc(p_pv("o"), 1)

                def turn_h(i, u):
                    pe.wait_ge(g_stage.sem, g_stage.at("rows", i))
                    pe.wait_ge(v_y.sem, v_y.at("y", i - 4))
                    pe.wait_ge(a_h.sem, a_h.at("carry", i - 1))
                    nc.tensor.transpose(hw_bank[:, 0:P], rows[:, u, :], c.ident[:, :]).then_inc(p_h("hT"), 1)

                def scores(i, u):
                    pe.wait_ge(a_turn.sem, a_turn.at("kT", i))
                    pe.wait_ge(a_pT.sem, a_pT.at("odd", i - 1))
                    lo, hi = slice(0, WIN), slice(WIN, P)
                    n = WH // 2
                    for bank in (even, odd):
                        nc.tensor.matmul(bank.rearrange("p (h k) -> p h k", k=P), identb[:, :],
                                         rows_bc(bias[:, (i % NT + NT - 1) // NT, :], n), start=True, stop=False, skip_group_check=True)
                    for h in range(WH):
                        bank = (even, odd)[h % 2].rearrange("p (h k) -> p h k", k=P)[:, h // 2, :]
                        s = slice(WD * (h % 2), WD * (h % 2) + WD)
                        q, k, kb = qT[s, u % 2, h // 2, :], kT[s, u % 2, h // 2, :], kbT[s, u % 2, h // 2, :]
                        last = h >= WH - 2
                        for dst, a, b in ((bank[:, lo], q, k[:, lo]), (bank[hi, hi], q[:, hi], k[:, hi]),
                                          (bank[lo, hi], q[:, lo], kb)):
                            m = nc.tensor.matmul(dst, a, b, start=False, stop=last, skip_group_check=True)
                    m.then_inc(p_sim("s"), 1)

                pipeline(pe, [(turn_o, 4), (qkv, 1), (project, 4), (turn_q, 2), (turn_p, 3), (turn_k, 2),
                              (values, 3), (turn_h, 0), (scores, 2)])

    return prepare, load_layer, run


def gated_mlp(c, y, ctx):
    nc, inp, bk = c.nc, c.inp, c.bank
    sb = c.sb(ctx)
    w1 = sb("ml_w1", [P, 2 * HID])
    w2 = sb("ml_w2", [P, len(HCH), E])
    b1 = sb("ml_b1", [P, 2, len(HCH)])
    lng = sb("ml_ln", [P, 2])
    keep = sb("ml_keep", [P, TILES + 1])
    ring = lambda name, *shape: sb("ml_" + name, [P, RING, *shape])
    rows, hT, hn, hnT = ring("rows", E), ring("hT", P + 1), ring("hn", E), ring("hnT", P)
    st6, mv, rstd = ring("st6", 6), ring("mv", 2), ring("rstd", 1)
    gl, mT = ring("gelu", len(HCH), P), ring("mT", len(HCH), P)
    loaded = c.sem(ctx, "ml_loaded")
    st = lambda name, *names: c.steps(ctx, "ml_" + name, *names)
    g_stage = st("g_stage", "rows")
    p_h, a_h = st("p_h", "hT"), st("a_h", "lo", "hi", "carry")
    p_back = st("p_back", "h")
    v_ln = st("v_ln", "stats", "aggr", "eps")
    g_ln = st("g_ln", "pow")
    v_hn = st("v_hn", "hn")
    p_hn, a_hn = st("p_hn", "hnT"), st("a_hn", "hnT")
    p_up = st("p_up", "g", "a")
    a_gelu = st("a_gelu", "g0", "g1", "g2")
    v_mul = st("v_mul", "m0", "m1", "m2")
    p_down, v_y = st("p_down", "y"), st("v_y", "y")
    every = [g_stage, p_h, a_h, p_back, v_ln, g_ln, v_hn, p_hn, a_hn, p_up, a_gelu, v_mul, p_down, v_y]
    LAST, WL = len(HCH) - 1, HCH[-1][1]

    def prepare():
        with nc.Block() as block:

            @block.gpsimd
            def _(gp):
                prime(gp, every)
                nc.gpsimd.memset(hT[...], 0.0)
                nc.gpsimd.memset(mT[...], 1.0)

            @block.sync
            def _(sp):
                sp.dma_start(keep[...], inp["batch_keep"]).then_inc(loaded, 16)
                sp.wait_ge(loaded, 16)

    def load_layer(l):
        with nc.Block() as block:

            @block.sync
            def _(sp):
                li = bass.ds(l, 1)
                sp.dma_start(w1[:, :], inp["L0_ffn_w1"][li, :, :].rearrange("a e n -> (a e) n")).then_inc(loaded, 16)
                w2d = inp["L0_ffn_w2"][li, :, :].rearrange("a n e -> (a n) e")
                b1d = inp["L0_ffn_b1"][li, :].rearrange("a n -> n a")
                for k, (lo, w) in enumerate(HCH):
                    sp.dma_start(w2[0:w, k, :], w2d[lo:lo + w, :]).then_inc(loaded, 16)
                    for g in range(2):
                        sp.dma_start(b1[0:w, g, k:k + 1], b1d[g * HID + lo:g * HID + lo + w, :]).then_inc(loaded, 16)
                sp.dma_start(w2[WL:WL + 1, LAST, :], inp["L0_ffn_b2"][li, :]).then_inc(loaded, 16)
                sp.dma_start(lng[:, 0:1], inp["L0_ffn_ln_g"][li, :].rearrange("a n -> n a")).then_inc(loaded, 16)
                sp.dma_start(lng[:, 1:2], inp["L0_ffn_ln_b"][li, :].rearrange("a n -> n a")).then_inc(loaded, 16)
                sp.wait_ge(loaded, l * (16 * 13) + 16 * 14)
                sp.nop(nofuse=True)

    def run(l):
        for s in every:
            s.base = l * TILES
        h_bank, back_bank, hn_bank, g_bank, a_bank, y_bank = bk[0:6]
        with nc.Block() as block:

            @block.gpsimd
            def _(gp):

                def stage(i, u):
                    gp.nop(nofuse=True)
                    nc.gpsimd.tensor_copy(rows[:, u, :], y[:, i, :]).then_inc(g_stage("rows"), 1)

                def inverse_std(i, u):
                    gp.wait_ge(v_ln.sem, v_ln.at("eps", i))
                    nc.gpsimd.tensor_tensor(rstd[:, u, :], mv[:, u, 1:2], c.minus_half[:, 0:1], ALU.pow)\
                      .then_inc(g_ln("pow"), 1)

                pipeline(gp, [(stage, 0), (inverse_std, 1)])

            @block.vector
            def _(dve):

                def statistics(i, u):
                    dve.wait_ge(p_back.sem, p_back.at("h", i))
                    nc.vector.bn_stats(st6[:, u, :], back_bank[:, 0:E]).then_inc(v_ln("stats"), 1)
                    dve.wait_ge(v_ln.sem, v_ln.at("stats", i))
                    dve.nop(nofuse=True)
                    nc.vector.bn_aggr(mv[:, u, :], st6[:, u, :]).then_inc(v_ln("aggr"), 1)
                    dve.wait_ge(v_ln.sem, v_ln.at("aggr", i))
                    nc.vector.tensor_scalar(mv[:, u, 1:2], mv[:, u, 1:2], LN_EPS, None, ALU.add)\
                      .then_inc(v_ln("eps"), 1)

                def normalize(i, u):
                    dve.wait_ge(g_ln.sem, g_ln.at("pow", i))
                    nc.vector.tensor_scalar(hn[:, u, :], back_bank[:, 0:E], mv[:, u, 0:1], rstd[:, u, :],
                                            ALU.subtract, ALU.mult).then_inc(v_hn("hn"), 1)

                def multiply(i, u):
                    dve.wait_ge(p_up.sem, p_up.at("a", i))
                    for k, (_, w) in enumerate(HCH):
                        dve.wait_ge(a_gelu.sem, a_gelu.at(f"g{k}", i))
                        nc.vector.scalar_tensor_tensor(out=mT[0:w, u, k, :], in0=a_bank[0:w, P * k:P * k + P],
                                                       scalar=b1[0:w, 0, k:k + 1], in1=gl[0:w, u, k, :],
                                                       op0=ALU.add, op1=ALU.mult).then_inc(v_mul(f"m{k}"), 1)

                def residual(i, u):
                    dve.wait_ge(p_down.sem, p_down.at("y", i))
                    nc.vector.tensor_tensor(y[:, i, :], y[:, i, :], y_bank[:, 0:E], ALU.add).then_inc(v_y("y"), 1)

                pipeline(dve, [(statistics, 1), (residual, 3), (multiply, 2), (normalize, 1)])

            @block.scalar
            def _(act):

                def h_columns(i, u):
                    h = E // 2
                    act.wait_ge(p_h.sem, p_h.at("hT", i))
                    nc.scalar.activation(hT[0:h, u, 0:P], h_bank[0:h, 0:P], ACT.Copy).then_inc(a_h("lo"), 1)
                    nc.scalar.activation(hT[h:P, u, 1:P + 1], h_bank[h:P, 0:P], ACT.Copy).then_inc(a_h("hi"), 1)
                    act.wait_ge(a_h.sem, a_h.at("hi", i - 1))
                    nc.scalar.activation(hT[h:P, u, 0:1], hT[h:P, (u - 1) % RING, P:P + 1], ACT.Copy,
                                         scale=keep[h:P, bass.ds(i, 1)]).then_inc(a_h("carry"), 1)

                def hn_columns(i, u):
                    act.wait_ge(p_hn.sem, p_hn.at("hnT", i))
                    nc.scalar.activation(hnT[:, u, :], hn_bank[:, 0:P], ACT.Identity, scale=lng[:, 0:1],
                                         bias=lng[:, 1:2]).then_inc(a_hn("hnT"), 1)

                def gelu(i, u):
                    act.wait_ge(p_up.sem, p_up.at("g", i))
                    for k, (_, w) in enumerate(HCH):
                        nc.scalar.activation(gl[0:w, u, k, :], g_bank[0:w, P * k:P * k + P], ACT.Gelu,
                                             bias=b1[0:w, 1, k:k + 1]).then_inc(a_gelu(f"g{k}"), 1)

                nc.scalar.preload_act_table_set("gelu_and_others")
                pipeline(act, [(hn_columns, 2), (h_columns, 0), (gelu, 2)])

            @block.tensor
            def _(pe):

                def turn_hn(i, u):
                    pe.wait_ge(v_hn.sem, v_hn.at("hn", i))
                    pe.wait_ge(a_hn.sem, a_hn.at("hnT", i - 1))
                    nc.tensor.transpose(hn_bank[:, 0:P], hn[:, u, :], c.ident[:, :]).then_inc(p_hn("hnT"), 1)

                def down(i, u):
                    pe.wait_ge(v_mul.sem, v_mul.at("m2", i))
                    pe.wait_ge(v_y.sem, v_y.at("y", i - 1))
                    for k, (_, w) in enumerate(HCH):
                        w += k == LAST
                        m = nc.tensor.matmul(y_bank[:, 0:E], mT[0:w, u, k, :], w2[0:w, k, :], start=k == 0,
                                             stop=k == LAST)
                    m.then_inc(p_down("y"), 1)

                def turn_back(i, u):
                    pe.wait_ge(a_h.sem, a_h.at("carry", i))
                    pe.wait_ge(v_hn.sem, v_hn.at("hn", i - 1))
                    nc.tensor.transpose(back_bank[:, 0:P], hT[:, u, 0:P], c.ident[:, :]).then_inc(p_back("h"), 1)

                def turn_h(i, u):
                    pe.wait_ge(g_stage.sem, g_stage.at("rows", i))
                    pe.wait_ge(a_h.sem, a_h.at("carry", i - 1))
                    nc.tensor.transpose(h_bank[:, 0:P], rows[:, u, :], c.ident[:, :]).then_inc(p_h("hT"), 1)

                def up(i, u):
                    pe.wait_ge(a_hn.sem, a_hn.at("hnT", i))
                    for name, bank, off in (("g", g_bank, HID), ("a", a_bank, 0)):
                        if name == "g":
                            pe.wait_ge(a_gelu.sem, a_gelu.at("g2", i - 1))
                        else:
                            pe.wait_ge(v_mul.sem, v_mul.at("m2", i - 1))
                        for k, (lo, w) in enumerate(HCH):
                            m = nc.tensor.matmul(bank[0:w, P * k:P * k + P], w1[:, off + lo:off + lo + w],
                                                 hnT[:, u, :], start=True, stop=True)
                        m.then_inc(p_up(name), 1)

                pipeline(pe, [(turn_hn, 2), (turn_back, 1), (down, 3), (turn_h, 0), (up, 2)])

    return prepare, load_layer, run


def causal_convolution(c):
    nc, inp, bk = c.nc, c.inp, c.bank
    PAIRS = B * CH
    with ExitStack() as ctx:
        sb = c.sb(ctx)
        w_in = sb("cv_w_in", [P, 3, E])
        waT, wvT, woT = sb("cv_waT", [P, CH]), sb("cv_wvT", [P, E]), sb("cv_woT", [P, E])
        wog, bog = sb("cv_wog", [P, B, E]), sb("cv_bog", [P, B, E])
        bo = sb("cv_bo", [P, E])
        flip = sb("cv_flip", [P, P])
        zs = sb("cv_z", [CH, B, T])
        zeros = sb("cv_zeros", [PAIRS, P])
        zmax, zneg, zsum, zrec = (sb(f"cv_{n}", [CH, B]) for n in ("zmax", "zneg", "zsum", "zrec"))
        vall, oall = sb("cv_v", [P, TILES, E]), sb("cv_o", [P, TILES, E])
        ring = lambda name, *shape: sb("cv_" + name, [P, RING, *shape])
        rows, hT, orow, oT = (ring(n, w) for n, w in (("rows", P), ("hT", 2 * P), ("orow", P), ("oT", P)))
        toep = ring("toep", T)
        zpad = nc.dram_tensor("cv_zpad", (PAIRS, P + T), F32).ap()

        loaded, turned, evac = c.sem(ctx, "cv_loaded"), c.sem(ctx, "cv_turned"), c.sem(ctx, "cv_evac")
        pre, vec, spread = c.sem(ctx, "cv_pre"), c.sem(ctx, "cv_vec"), c.sem(ctx, "cv_spread")
        expo = c.sem(ctx, "cv_exp")
        st = lambda name, *names: c.steps(ctx, "cv_" + name, *names)
        v_norm = st("v_norm", "norm", "scaled", "shifted")
        p_h, a_h = st("p_h", "hT"), st("a_h", "hT")
        p_zv, a_zv = st("p_zv", "z", "v"), st("a_zv", "z", "v")
        p_conv, v_conv = st("p_conv", "o"), st("v_conv", "o")
        g_o, p_oT, a_oT, p_wo = st("g_o", "rows"), st("p_oT", "oT"), st("a_oT", "oT"), st("p_wo", "wo")
        v_x = st("v_x", "bias", "x")
        toep_in = [c.sem(ctx, f"cv_toep_in{u}") for u in range(RING)]

        with nc.Block() as block:

            @block.sync
            def _(sp):
                sp.dma_start(w_in[:, 0, :], inp["L1_attn_W_V"]).then_inc(loaded, 16)
                sp.dma_start(w_in[:, 1, :], inp["L1_attn_W_O"]).then_inc(loaded, 16)
                sp.dma_start(w_in[0:CH, 2, :], inp["L1_attn_W_A"]).then_inc(loaded, 16)
                sp.dma_start(bo[:, :], inp["L1_attn_b_O"].unsqueeze(0).broadcast_to([P, E])).then_inc(loaded, 16)
                sp.dma_start(flip[:, :], inp["flip"]).then_inc(loaded, 16)

            @block.gpsimd
            def _(gp):
                prime(gp, [v_norm, p_h, a_h, p_zv, a_zv, p_conv, v_conv, g_o, p_oT, a_oT, p_wo, v_x])
                nc.gpsimd.memset(zeros[:, :], 0.0)

            @block.tensor
            def _(pe):
                pe.wait_ge(loaded, 80)
                nc.tensor.transpose(bk[0][:, 0:P], w_in[:, 0, :], c.ident[:, :])
                nc.tensor.transpose(bk[0][:, P:2 * P], w_in[:, 1, :], c.ident[:, :])
                nc.tensor.transpose(bk[0][:, 2 * P:2 * P + CH], w_in[0:CH, 2, :], c.ident[0:CH, 0:CH])\
                  .then_inc(turned, 1)

            @block.vector
            def _(dve):
                dve.wait_ge(turned, 1)
                nc.vector.tensor_copy(wvT[:, :], bk[0][:, 0:P]).then_inc(pre, 1)
                nc.vector.tensor_copy(woT[:, :], bk[0][:, P:2 * P]).then_inc(pre, 1)
                nc.vector.tensor_copy(waT[:, :], bk[0][:, 2 * P:2 * P + CH]).then_inc(pre, 1)
                dve.wait_ge(pre, 2)
                nc.vector.tensor_tensor(wog[...], rows_bc(woT[:, :], B), c.mod[:, 1, :, GA, :], ALU.mult)\
                  .then_inc(pre, 1)
                nc.vector.tensor_tensor(bog[...], rows_bc(bo[:, :], B), c.mod[:, 1, :, GA, :], ALU.mult)\
                  .then_inc(pre, 1)

        with nc.Block() as block:

            @block.vector
            def _(dve):

                def norm(i, u):
                    dve.wait_ge(p_h.sem, p_h.at("hT", i - RING))
                    modulate(c, dve, v_norm, rows[:, u, :], i, 1, SA, CA)

                pipeline(dve, [(norm, 0)])

            @block.tensor
            def _(pe):

                def turn_h(i, u):
                    pe.wait_ge(v_norm.sem, v_norm.at("shifted", i))
                    pe.wait_ge(a_h.sem, a_h.at("hT", i - 1))
                    nc.tensor.transpose(bk[0][:, 0:P], rows[:, u, :], c.ident[:, :])
                    nc.tensor.matmul(bk[0][:, P:2 * P], rows[:, u, :], flip[:, :], start=True, stop=True)\
                      .then_inc(p_h("hT"), 1)

                def project(i, u):
                    pe.wait_ge(a_h.sem, a_h.at("hT", i))
                    pe.wait_ge(a_zv.sem, a_zv.at("v", i - 1))
                    nc.tensor.matmul(bk[1][0:CH, 0:P], waT[:, :], hT[:, u, 0:P], start=True, stop=True)\
                      .then_inc(p_zv("z"), 1)
                    nc.tensor.matmul(bk[1][:, P:2 * P], hT[:, u, P:2 * P], wvT[:, :], start=True, stop=True)\
                      .then_inc(p_zv("v"), 1)

                pipeline(pe, [(turn_h, 0), (project, 1)])

            @block.scalar
            def _(act):

                def h_columns(i, u):
                    act.wait_ge(p_h.sem, p_h.at("hT", i))
                    nc.scalar.activation(hT[:, u, :], bk[0][:, 0:2 * P], ACT.Copy).then_inc(a_h("hT"), 1)

                def outputs(i, u):
                    act.wait_ge(p_zv.sem, p_zv.at("v", i))
                    zflat = zs[:, :, :].rearrange("h b t -> h (b t)")
                    nc.scalar.activation(zflat[:, bass.ds(i * P, P)], bk[1][0:CH, 0:P], ACT.Copy,
                                         scale=float(CD ** -0.5)).then_inc(a_zv("z"), 1)
                    nc.scalar.activation(vall[:, i, :], bk[1][:, P:2 * P], ACT.Copy).then_inc(a_zv("v"), 1)

                pipeline(act, [(outputs, 1), (h_columns, 0)])

        with nc.Block() as block:

            @block.vector
            def _(dve):
                nc.vector.tensor_reduce(zmax[:, :], zs[...], AX_X, ALU.max).then_inc(vec, 1)
                dve.wait_ge(vec, 1)
                nc.vector.tensor_scalar(zneg[:, :], zmax[:, :], -1.0, None, ALU.mult).then_inc(vec, 1)
                dve.wait_ge(expo, B)
                nc.vector.reciprocal(zrec[:, :], zsum[:, :]).then_inc(vec, 1)
                dve.wait_ge(vec, 3)
                for b in range(B):
                    nc.vector.tensor_scalar(zs[:, b, :], zs[:, b, :], zrec[:, b:b + 1], None, ALU.mult)\
                      .then_inc(vec, 1)

            @block.scalar
            def _(act):
                act.wait_ge(vec, 2)
                for b in range(B):
                    nc.scalar.activation(zs[:, b, :], zs[:, b, :], ACT.Exp, bias=zneg[:, b:b + 1],
                                         accum_out=zsum[:, b:b + 1]).then_inc(expo, 1)

            @block.sync
            def _(sp):
                sp.dma_start(zpad[:, 0:P], zeros[:, :]).then_inc(spread, 16)
                for b in range(B):
                    sp.wait_ge(vec, 4 + b)
                    sp.dma_start(zpad[b * CH:b * CH + CH, P:P + T], zs[:, b, :]).then_inc(spread, 16)
                sp.wait_ge(spread, 16 * (B + 1))

        with nc.Block() as block:

            @block.sync
            def _(sp):

                def fetch(s, u):
                    sp.wait_ge(p_conv.sem, p_conv.at("o", s - RING))
                    row = bass.AP(tensor=zpad.tensor, offset=s * (P + T) + 1, ap=[[1, P], [1, T]])
                    sp.dma_start(toep[:, u, :], row).then_inc(toep_in[u], 16)

                pipeline(sp, [(fetch, 0)], n=PAIRS)
                sp.nop(nofuse=True)

            @block.tensor
            def _(pe):

                def convolve(s, u):
                    pe.wait_ge(toep_in[u], (s // RING) * 16 + 16)
                    pe.wait_ge(v_conv.sem, v_conv.at("o", s - 2))
                    b, h = s // CH, s % CH
                    for m in range(NT):
                        v = vall[:, bass.ds(b * NT, NT - m), bass.ds(h * CD, CD)]
                        mm = nc.tensor.matmul(bk[u % 2][:, CD * m:P].rearrange("p (n d) -> p n d", d=CD),
                                              toep[:, u, P * m:P * m + P], v, start=m == 0, stop=True,
                                              skip_group_check=True)
                    mm.then_inc(p_conv("o"), 1)

                pipeline(pe, [(convolve, 0)], n=PAIRS)

            @block.vector
            def _(dve):

                def keep(s, u):
                    dve.wait_ge(p_conv.sem, p_conv.at("o", s))
                    b, h = s // CH, s % CH
                    nc.vector.tensor_copy(oall[:, bass.ds(b * NT, NT), bass.ds(h * CD, CD)],
                                          bk[u % 2][:, 0:P].rearrange("p (n d) -> p n d", d=CD))\
                      .then_inc(v_conv("o"), 1)

                pipeline(dve, [(keep, 0)], n=PAIRS)

        with nc.Block() as block:

            @block.gpsimd
            def _(gp):

                def stage(i, u):
                    gp.wait_ge(p_oT.sem, p_oT.at("oT", i - RING))
                    gp.nop(nofuse=True)
                    nc.gpsimd.tensor_copy(orow[:, u, :], oall[:, i, :]).then_inc(g_o("rows"), 1)

                pipeline(gp, [(stage, 0)])

            @block.tensor
            def _(pe):

                def turn_o(i, u):
                    pe.wait_ge(g_o.sem, g_o.at("rows", i))
                    pe.wait_ge(a_oT.sem, a_oT.at("oT", i - 1))
                    nc.tensor.transpose(bk[0][:, 0:P], orow[:, u, :], c.ident[:, :]).then_inc(p_oT("oT"), 1)

                def project(i, u):
                    pe.wait_ge(a_oT.sem, a_oT.at("oT", i))
                    pe.wait_ge(v_x.sem, v_x.at("x", i - 1))
                    nc.tensor.matmul(bk[1][:, 0:P], oT[:, u, :], wog[:, i // NT, :], start=True, stop=True)\
                      .then_inc(p_wo("wo"), 1)

                pipeline(pe, [(turn_o, 0), (project, 1)])

            @block.scalar
            def _(act):

                def o_columns(i, u):
                    act.wait_ge(p_oT.sem, p_oT.at("oT", i))
                    nc.scalar.activation(oT[:, u, :], bk[0][:, 0:P], ACT.Copy).then_inc(a_oT("oT"), 1)

                pipeline(act, [(o_columns, 0)])

            @block.vector
            def _(dve):

                def residual(i, u):
                    x = c.x[:, i, :]
                    nc.vector.tensor_tensor(x, x, bog[:, i // NT, :], ALU.add).then_inc(v_x("bias"), 1)
                    dve.wait_ge(v_x.sem, v_x.at("bias", i))
                    dve.wait_ge(p_wo.sem, p_wo.at("wo", i))
                    nc.vector.tensor_tensor(x, x, bk[1][:, 0:P], ALU.add).then_inc(v_x("x"), 1)

                pipeline(dve, [(residual, 1)])


def experts(c, out_ap):
    nc, inp, bk = c.nc, c.inp, c.bank
    with ExitStack() as ctx:
        sb = c.sb(ctx)
        w_in = sb("ex_w_in", [P, NE, E])
        wT = sb("ex_wT", [P, NE * E])
        gate_in, gateT = sb("ex_gate_in", [NE, E]), sb("ex_gateT", [P, NE])
        b_in, b_rest = sb("ex_b_in", [NE, E]), sb("ex_b_rest", [NE, 2, E])
        b_parts = sb("ex_b_parts", [NE, 3, E], BF16)
        b_rows = sb("ex_b_rows", [3, NE, E], BF16)
        ones = sb("ex_ones", [3, P], BF16)
        iota = sb("ex_iota", [P, NE])
        ring = lambda name, *shape: sb("ex_" + name, [P, RING, *shape])
        rows, hT, total = ring("rows", P), ring("hT", P), ring("total", P)
        zmax, zneg, zsum, zrec = (ring(n, 1) for n in ("zmax", "zneg", "zsum", "zrec"))
        prob, top, topf, sel, w = ring("prob", NE), ring("top", 8), ring("topf", 8), ring("sel", NE), ring("w", NE)
        topi = ctx.enter_context(nc.sbuf_tensor("ex_topi", [P, RING, 8], U32))
        yw = sb("ex_yw", [P, 2, NE, E])

        loaded, turned, pre = c.sem(ctx, "ex_loaded"), c.sem(ctx, "ex_turned"), c.sem(ctx, "ex_pre")
        copied, moved, stored = c.sem(ctx, "ex_copied"), c.sem(ctx, "ex_moved"), c.sem(ctx, "ex_stored")
        st = lambda name, *names: c.steps(ctx, "ex_" + name, *names)
        v_norm = st("v_norm", "norm", "scaled", "shifted")
        p_h, a_h = st("p_h", "hT"), st("a_h", "hT")
        p_gate = st("p_gate", "logits")
        v_max, a_exp = st("v_max", "max", "neg"), st("a_exp", "exp")
        v_top = st("v_top", "rec", "prob", "top", "idx", "float", "first", "both", "w")
        p_up = st("p_up", "01", "23")
        v_relu, a_relu = st("v_relu", "y0", "y1"), st("a_relu", *[f"e{e}" for e in range(NE // 2, NE)])
        v_out = st("v_out", "sum", "gated", "x")
        every = [v_norm, p_h, a_h, p_gate, v_max, a_exp, v_top, p_up, v_relu, a_relu, v_out]

        with nc.Block() as block:

            @block.sync
            def _(sp):
                sp.dma_start(w_in[...], inp["L1_ffn_expert_w"].rearrange("e d h -> d e h")).then_inc(loaded, 16)
                sp.dma_start(gate_in[...], inp["L1_ffn_gate_w"]).then_inc(loaded, 16)
                sp.dma_start(b_in[...], inp["L1_ffn_expert_b"]).then_inc(loaded, 16)
                sp.dma_start(iota[...], inp["expert_numbers"]).then_inc(loaded, 16)
                sp.wait_ge(pre, 5)
                for k in range(3):
                    sp.dma_start(b_rows[k:k + 1, :, :], b_parts[:, k, :]).then_inc(moved, 16)
                sp.wait_ge(moved, 48)

            @block.gpsimd
            def _(gp):
                prime(gp, every)
                nc.gpsimd.memset(ones[...], 1.0)

            @block.vector
            def _(dve):
                dve.wait_ge(loaded, 64)
                src = b_in[...]
                for k in range(3):
                    nc.vector.tensor_copy(b_parts[:, k, :], src).then_inc(pre, 1)
                    if k < 2:
                        dve.wait_ge(pre, 2 * k + 1)
                        nc.vector.tensor_tensor(b_rest[:, k, :], src, b_parts[:, k, :], ALU.subtract)\
                          .then_inc(pre, 1)
                        src = b_rest[:, k, :]
                        dve.wait_ge(pre, 2 * k + 2)

            @block.tensor
            def _(pe):
                pe.wait_ge(loaded, 64)
                for e in range(NE):
                    m = nc.tensor.transpose(bk[e // 4][:, P * (e % 4):P * (e % 4) + P], w_in[:, e, :], c.ident[:, :])
                    if e % 4 == 3:
                        m.then_inc(turned, 1)
                nc.tensor.transpose(bk[4][:, 0:NE], gate_in[...], c.ident[0:NE, 0:NE]).then_inc(turned, 1)

            @block.scalar
            def _(act):
                for k in range(NE // 4):
                    act.wait_ge(turned, k + 1)
                    nc.scalar.activation(wT[:, BANK * k:BANK * k + BANK], bk[k], ACT.Copy).then_inc(copied, 1)
                act.wait_ge(turned, NE // 4 + 1)
                nc.scalar.activation(gateT[...], bk[4][:, 0:NE], ACT.Copy).then_inc(copied, 1)

        h_bank, gate_bank = bk[6], bk[7]
        with nc.Block() as block:

            @block.vector
            def _(dve):

                def norm(i, u):
                    dve.wait_ge(p_h.sem, p_h.at("hT", i - RING))
                    modulate(c, dve, v_norm, rows[:, u, :], i, 1, SB, CB)

                def gate_max(i, u):
                    dve.wait_ge(p_gate.sem, p_gate.at("logits", i))
                    nc.vector.tensor_reduce(zmax[:, u, :], gate_bank[:, 0:NE], AX_X, ALU.max)\
                      .then_inc(v_max("max"), 1)
                    dve.wait_ge(v_max.sem, v_max.at("max", i))
                    nc.vector.tensor_scalar(zneg[:, u, :], zmax[:, u, :], -1.0, None, ALU.mult)\
                      .then_inc(v_max("neg"), 1)

                def choose(i, u):
                    def after(name):
                        dve.wait_ge(v_top.sem, v_top.at(name, i))
                    dve.wait_ge(a_exp.sem, a_exp.at("exp", i))
                    nc.vector.reciprocal(zrec[:, u, :], zsum[:, u, :]).then_inc(v_top("rec"), 1)
                    after("rec")
                    nc.vector.tensor_scalar(prob[:, u, :], prob[:, u, :], zrec[:, u, :], None, ALU.mult)\
                      .then_inc(v_top("prob"), 1)
                    after("prob")
                    dve.nop(nofuse=True)
                    nc.vector.max(top[:, u, :], prob[:, u, :]).then_inc(v_top("top"), 1)
                    after("top")
                    dve.nop(nofuse=True)
                    nc.vector.max_index(topi[:, u, :], top[:, u, :], prob[:, u, :]).then_inc(v_top("idx"), 1)
                    after("idx")
                    nc.vector.tensor_copy(topf[:, u, :], topi[:, u, :]).then_inc(v_top("float"), 1)
                    after("float")
                    nc.vector.tensor_scalar(sel[:, u, :], iota[:, :], topf[:, u, 0:1], None, ALU.is_equal)\
                      .then_inc(v_top("first"), 1)
                    after("first")
                    nc.vector.scalar_tensor_tensor(out=sel[:, u, :], in0=iota[:, :], scalar=topf[:, u, 1:2],
                                                   in1=sel[:, u, :], op0=ALU.is_equal, op1=ALU.add)\
                      .then_inc(v_top("both"), 1)
                    after("both")
                    nc.vector.tensor_tensor(w[:, u, :], prob[:, u, :], sel[:, u, :], ALU.mult)\
                      .then_inc(v_top("w"), 1)

                def relu(i, u):
                    dve.wait_ge(p_up.sem, p_up.at("01", i))
                    dve.wait_ge(v_top.sem, v_top.at("w", i))
                    for k in range(2):
                        nc.vector.scalar_tensor_tensor(
                            out=yw[:, u % 2, 4 * k:4 * k + 4, :], in0=bk[k].rearrange("p (e f) -> p e f", f=E),
                            scalar=0.0, in1=cols_bc(w[:, u, 4 * k:4 * k + 4], E), op0=ALU.max, op1=ALU.mult)\
                          .then_inc(v_relu(f"y{k}"), 1)

                def residual(i, u):
                    dve.wait_ge(a_relu.sem, a_relu.at(f"e{NE - 1}", i))
                    dve.wait_ge(v_relu.sem, v_relu.at("y1", i))
                    nc.vector.tensor_reduce(total[:, u, :], yw[:, u % 2, :, :].rearrange("p e f -> p f e"), AX_X,
                                            ALU.add).then_inc(v_out("sum"), 1)
                    dve.wait_ge(v_out.sem, v_out.at("sum", i))
                    nc.vector.tensor_tensor(total[:, u, :], total[:, u, :], c.mod[:, 1, i // NT, GB, :], ALU.mult)\
                      .then_inc(v_out("gated"), 1)
                    dve.wait_ge(v_out.sem, v_out.at("gated", i))
                    nc.vector.tensor_tensor(c.x[:, i, :], c.x[:, i, :], total[:, u, :], ALU.add)\
                      .then_inc(v_out("x"), 1)

                pipeline(dve, [(norm, 0), (gate_max, 1), (relu, 2), (choose, 1), (residual, 3)])

            @block.tensor
            def _(pe):

                def turn_h(i, u):
                    pe.wait_ge(v_norm.sem, v_norm.at("shifted", i))
                    pe.wait_ge(a_h.sem, a_h.at("hT", i - 1))
                    nc.tensor.transpose(h_bank[:, 0:P], rows[:, u, :], c.ident[:, :]).then_inc(p_h("hT"), 1)

                def gate(i, u):
                    pe.wait_ge(a_h.sem, a_h.at("hT", i))
                    pe.wait_ge(a_exp.sem, a_exp.at("exp", i - 1))
                    nc.tensor.matmul(gate_bank[:, 0:NE], hT[:, u, :], gateT[:, :], start=True, stop=True)\
                      .then_inc(p_gate("logits"), 1)

                def up(i, u):
                    for half in range(2):
                        if half:
                            pe.wait_ge(a_relu.sem, a_relu.at(f"e{NE - 1}", i - 1))
                        else:
                            pe.wait_ge(v_relu.sem, v_relu.at("y1", i - 1))
                        for k in range(2 * half, 2 * half + 2):
                            brow = b_rows[:, 4 * k:4 * k + 4, :].rearrange("p e f -> p (e f)")
                            nc.tensor.matmul(bk[k], ones[:, :], brow, start=True, stop=False)
                            m = nc.tensor.matmul(bk[k], hT[:, u, :], wT[:, BANK * k:BANK * k + BANK], start=False,
                                                 stop=True)
                        m.then_inc(p_up(("01", "23")[half]), 1)

                pipeline(pe, [(turn_h, 0), (gate, 1), (up, 2)])

            @block.scalar
            def _(act):

                def h_columns(i, u):
                    act.wait_ge(p_h.sem, p_h.at("hT", i))
                    nc.scalar.activation(hT[:, u, :], h_bank[:, 0:P], ACT.Copy).then_inc(a_h("hT"), 1)

                def gate_exp(i, u):
                    act.wait_ge(v_max.sem, v_max.at("neg", i))
                    nc.scalar.activation(prob[:, u, :], gate_bank[:, 0:NE], ACT.Exp, bias=zneg[:, u, :],
                                         accum_out=zsum[:, u, :]).then_inc(a_exp("exp"), 1)

                def relu(i, u):
                    act.wait_ge(p_up.sem, p_up.at("23", i))
                    act.wait_ge(v_top.sem, v_top.at("w", i))
                    act.wait_ge(v_out.sem, v_out.at("sum", i - 2))
                    for e in range(NE // 2, NE):
                        nc.scalar.activation(yw[:, u % 2, e, :], bk[e // 4][:, P * (e % 4):P * (e % 4) + P], ACT.Relu,
                                             scale=w[:, u, e:e + 1]).then_inc(a_relu(f"e{e}"), 1)

                nc.scalar.preload_act_table_set("natural_log_exp_and_others")
                pipeline(act, [(h_columns, 0), (gate_exp, 1), (relu, 2)])

            @block.sync
            def _(sp):

                def write(i, u):
                    sp.wait_ge(v_out.sem, v_out.at("x", i))
                    sp.dma_start(row_tiles(out_ap)[:, i, :], c.x[:, i, :]).then_inc(stored, 16)

                with sp.Fori(0, TILES) as i:
                    write(i, 0)
                sp.wait_ge(stored, 16 * TILES)
                sp.nop(nofuse=True)


def adaln_program(nc, inp, out):
    with ExitStack() as ctx:
        ctx.enter_context(nc.allow_non_contiguous_dma(reason="weight vectors as columns"))
        c = Core(nc, ctx, inp)
        setup(c)
        row_statistics(c, "st0")
        linear_attention(c)
        row_statistics(c, "st1")
        with ExitStack() as scope:
            y = c.sb(scope)("y_rows", [P, TILES, E])
            start_layers(c, y)
            attn_prepare, attn_load, attn_run = windowed_attention(c, y, scope)
            mlp_prepare, mlp_load, mlp_run = gated_mlp(c, y, scope)
            attn_prepare()
            mlp_prepare()
            with nc.Fori(0, DEPTH) as l:
                attn_load(l)
                attn_run(l)
                mlp_load(l)
                mlp_run(l)
            end_layers(c, y)
        row_statistics(c, "st2")
        causal_convolution(c)
        row_statistics(c, "st3")
        experts(c, out)


def shape_constants():
    s, t = np.arange(P)[:, None], np.arange(P)[None, :]
    masks = np.zeros((P, NLEV, P), np.uint32)
    masks[:, 0] = (s // (2 * HALVES[0]) == t // (2 * HALVES[0])) & (s <= t)
    for k in range(1, NLEV):
        h = HALVES[k]
        masks[:, k] = (s // (2 * h) == t // (2 * h)) & (s % (2 * h) < h) & (t % (2 * h) >= h)
    reset = np.zeros((P, TILES), np.float32)
    reset[:, ::NT] = -200.0
    keep = np.ones((P, TILES + 1), np.float32)
    keep[:, ::NT] = 0.0
    q, k = np.arange(WIN)[:, None], np.arange(WIN)[None, :]
    own, before, none = np.where(k <= q, 0.0, NEG), np.where(k >= q, 0.0, NEG), np.full((WIN, WIN), NEG)
    tile = np.block([[own, before], [before, own]])
    first = np.block([[own, none], [before, own]])
    bias = np.stack([first, tile], 1).astype(np.float32)
    f32 = np.float32
    half = np.arange(0, WD, 2, dtype=f32)
    t = np.arange(T, dtype=f32)
    freq = t[:, None] * (f32(1) / np.power(f32(10000), half / f32(WD)))[None, :]
    base = ((half + f32(0.4 * WD)) / f32(1.4 * WD)).astype(np.float64)
    scale = base[None, :] ** ((t - T // 2) / f32(WIN // 2))[:, None].astype(np.float64)
    cos, sin = np.cos(freq.astype(np.float64)), np.sin(freq.astype(np.float64))
    tabs = [np.concatenate(p, 1) for p in ((cos * scale, cos * scale), (-sin * scale, sin * scale),
                                           (cos / scale, cos / scale), (-sin / scale, sin / scale))]
    rot = np.stack(tabs).astype(f32).reshape(4, NT, P, WD).transpose(2, 0, 1, 3)
    eye = np.eye(P, dtype=f32)
    return {"ident": eye, "level_masks": masks, "batch_reset": reset,
            "batch_keep": keep, "window_bias": bias, "rotations": rot, "flip": np.ascontiguousarray(eye[::-1]),
            "expert_numbers": np.tile(np.arange(NE, dtype=f32), (P, 1))}


_INS = ["L0_attn_x", "L0_attn_Wq", "L0_attn_Wk", "L0_attn_Wv", "L0_attn_Wo", "L0_attn_delta", "L0_attn_G1",
        "L0_attn_G2", "L0_attn_norm_w", "L0_ffn_wqkv", "L0_ffn_q_scale", "L0_ffn_k_scale", "L0_ffn_wo",
        "L0_ffn_ln_g", "L0_ffn_ln_b", "L0_ffn_w1", "L0_ffn_b1", "L0_ffn_w2", "L0_ffn_b2", "L0_c", "L0_wmod",
        "L1_attn_W_A", "L1_attn_W_V", "L1_attn_W_O", "L1_attn_b_O", "L1_ffn_gate_w", "L1_ffn_expert_w",
        "L1_ffn_expert_b", "L1_c", "L1_wmod"]


def kernel(**inputs):
    import concourse.bacc as bacc
    from concourse.bass_utils import run_bass_kernel_spmd

    nc = bacc.Bacc("TRN2", target_bir_lowering=False, num_devices=1)
    arrays, aps = {}, {}
    for name, a in [(n, inputs[n]) for n in _INS] + list(shape_constants().items()):
        a = np.ascontiguousarray(a)
        arrays[f"in_{name}_dram"] = a
        aps[name] = nc.dram_tensor(f"in_{name}_dram", a.shape, mybir.dt.from_np(a.dtype), kind="ExternalInput").ap()
    out = nc.dram_tensor("out_0_dram", (B, T, E), F32, kind="ExternalOutput").ap()
    adaln_program(nc, aps, out)
    r = run_bass_kernel_spmd(nc, [arrays], core_ids=[0])
    return r.results[0]["out_0_dram"]
```

```python
from contextlib import ExitStack

import concourse.bass as bass
import numpy as np
from concourse import mybir

F32 = mybir.dt.float32
BF16 = mybir.dt.bfloat16
U32 = mybir.dt.uint32
ALU = mybir.AluOpType
ACT = mybir.ActivationFunctionType
AX_X = mybir.AxisListType.X

P = 128
B, T, E = 2, 2048, 128
NT = T // P
TILES = B * NT
BANK = 512
LN_EPS = 1e-5
RING = 4
PRIMED = 8

GH, GD = 2, 64
HALVES = (4, 8, 16, 32, 64)
NLEV = len(HALVES)
MAX_EXP = float(np.exp(20.0))
MAX_SIG = 1e18

DEPTH, WH, WD, WIN = 2, 8, 64, 64
INNER = WH * WD
QK_SCALE = 8.0
NEG = -1e30
HID = int(E * 4 * 2 / 3)
HCH = [(0, 128), (128, 128), (256, HID - 256)]

CH, CD = 16, 8
NE = 16


class Steps:

    def __init__(self, sem, *names):
        self.sem, self.names, self.n = sem, names, 0
        self.base = 0

    def __call__(self, name):
        assert self.names[self.n % len(self.names)] == name, (self.names, self.n, name)
        self.n += 1
        return self.sem

    def at(self, name, i):
        if isinstance(i, int):
            i = min(i, TILES - 1)
        return (i + self.base + PRIMED) * len(self.names) + self.names.index(name) + 1


def prime(eng, steps):
    for s in steps:
        eng.sem_inc(s.sem, PRIMED * len(s.names))


def pipeline(eng, stages, n=TILES):
    lag = max(k for _, k in stages)
    start = -(-lag // RING) * RING
    for s in range(start):
        for f, k in stages:
            if 0 <= s - k:
                f(s - k, (s - k) % RING)
    with eng.Fori(0, (n - start) // RING) as j:
        for u in range(RING):
            for f, k in stages:
                f(j * RING + (start + u - k), (start + u - k) % RING)
    for s in range(n, n + lag):
        for f, k in stages:
            if s - k < n:
                f(s - k, (s - k) % RING)


def rows_bc(ap, n):
    return ap.unsqueeze(1).broadcast_to([ap.shape[0], n, ap.shape[1]])


def cols_bc(ap, w):
    return ap.unsqueeze(2).broadcast_to([ap.shape[0], ap.shape[1], w])


def row_tiles(ap):
    return ap.rearrange("b (n p) e -> p (b n) e", p=P)


class Core:

    def __init__(self, nc, ctx, inp):
        self.nc, self.ctx, self.inp = nc, ctx, inp
        self.psum = ctx.enter_context(nc.psum_tensor("psum", [P, 8, BANK], F32))
        self.bank = [self.psum[:, k, :] for k in range(8)]
        sb = self.sb(ctx)
        self.x = sb("x_rows", [P, TILES, E])
        self.ident = sb("ident", [P, P])
        self.mod = sb("mod", [P, 2, B, 6, E])
        self.mean = sb("mean", [P, TILES])
        self.rstd = sb("rstd", [P, TILES])
        self.minus_half = sb("minus_half", [P, TILES])

    def sb(self, ctx):
        return lambda name, shape, dt=F32: ctx.enter_context(self.nc.sbuf_tensor(name, shape, dt))

    def steps(self, ctx, name, *names):
        return Steps(ctx.enter_context(self.nc.semaphore(name)), *names)

    def sem(self, ctx, name):
        return ctx.enter_context(self.nc.semaphore(name))


SA, CA, GA, SB, CB, GB = range(6)


def setup(c):
    nc, inp = c.nc, c.inp
    with ExitStack() as ctx:
        sb = c.sb(ctx)
        cT = sb("cT", [P, 4])
        wmod = sb("wmod", [P, 2, 6 * E])
        ex = sb("ex", [P, 4])
        sig = sb("sig", [P, 4])
        silu = sb("silu", [P, 4])
        lhs = sb("silu_bc", [P, 4, P])
        sign = sb("sign", [P, 2, B, 2, E])
        loaded = c.sem(ctx, "setup_loaded")
        act_done = c.sem(ctx, "setup_act")
        vec = c.sem(ctx, "setup_vec")
        pe_done = c.sem(ctx, "setup_pe")
        LOADS = 5
        with nc.Block() as block:

            @block.sync
            def _(sp):
                for k, name in enumerate(("L0_c", "L1_c")):
                    sp.dma_start(cT[:, 2 * k:2 * k + 2], inp[name].rearrange("b e -> e b")).then_inc(loaded, 16)
                for k, name in enumerate(("L0_wmod", "L1_wmod")):
                    sp.dma_start(wmod[:, k, :], inp[name]).then_inc(loaded, 16)
                sp.dma_start(c.ident[:, :], inp["ident"]).then_inc(loaded, 16)
                sp.dma_start(c.x[:, :, :], row_tiles(inp["L0_attn_x"])).then_inc(loaded, 16)
                sp.wait_ge(loaded, 16 * (LOADS + 1))

            @block.scalar
            def _(act):
                act.wait_ge(loaded, 16 * (LOADS + 1))
                nc.scalar.activation(ex[:, :], cT[:, :], ACT.Exp, scale=-1.0).then_inc(act_done, 1)

            @block.vector
            def _(dve):
                nc.vector.memset(c.minus_half[:, :], -0.5).then_inc(vec, 1)
                dve.wait_ge(act_done, 1)
                nc.vector.tensor_scalar(ex[:, :], ex[:, :], 1.0, None, ALU.add).then_inc(vec, 1)
                dve.wait_ge(vec, 2)
                nc.vector.reciprocal(sig[:, :], ex[:, :]).then_inc(vec, 1)
                dve.wait_ge(vec, 3)
                nc.vector.tensor_tensor(silu[:, :], cT[:, :], sig[:, :], ALU.mult).then_inc(vec, 1)
                dve.wait_ge(vec, 4)
                nc.vector.tensor_copy(lhs[:, :, :], cols_bc(silu[:, :], P)).then_inc(vec, 1)
                flat = c.mod[:, :, :, :, :].rearrange("p k b m e -> p (k b) (m e)")
                for r in range(4):
                    dve.wait_ge(pe_done, r + 1)
                    for h, (lo, hi) in enumerate(((0, 512), (512, 768))):
                        nc.vector.tensor_copy(flat[:, r, lo:hi], c.bank[2 * r + h][:, 0:hi - lo]).then_inc(vec, 1)
                dve.wait_ge(vec, 13)
                m = c.mod[:, :, :, :, :].rearrange("p k b (s m) e -> p (k b) s m e", s=2)
                for r in range(4):
                    nc.vector.tensor_scalar(m[:, r, :, 1, :], m[:, r, :, 1, :], 1.0, None, ALU.add).then_inc(vec, 1)
                    sg = sign[:, r // 2, r % 2, :, :]
                    nc.vector.tensor_scalar(sg, m[:, r, :, 2, :], 0.0, 2.0, ALU.is_ge, ALU.mult).then_inc(vec, 1)
                    mag = m[:, r, :, 2, :]
                    dve.wait_ge(vec, 13 + 5 * r + 2)
                    nc.vector.scalar_tensor_tensor(out=mag, in0=mag, scalar=-1.0, in1=mag, op0=ALU.mult,
                                                   op1=ALU.max).then_inc(vec, 1)
                    dve.wait_ge(vec, 13 + 5 * r + 3)
                    nc.vector.tensor_scalar(mag, mag, 0.25, None, ALU.max).then_inc(vec, 1)
                    dve.wait_ge(vec, 13 + 5 * r + 4)
                    nc.vector.scalar_tensor_tensor(out=m[:, r, :, 2, :], in0=sg, scalar=-1.0,
                                                   in1=m[:, r, :, 2, :], op0=ALU.add,
                                                   op1=ALU.mult).then_inc(vec, 1)
                dve.wait_ge(vec, 33)

            @block.tensor
            def _(pe):
                pe.wait_ge(vec, 5)
                for r in range(4):
                    nc.tensor.matmul(c.bank[2 * r][:, :], lhs[:, r, :], wmod[:, r // 2, 0:512], start=True, stop=True)
                    nc.tensor.matmul(c.bank[2 * r + 1][:, 0:256], lhs[:, r, :], wmod[:, r // 2, 512:768],
                                     start=True, stop=True).then_inc(pe_done, 1)


def row_statistics(c, ctx, tag):
    nc, sb = c.nc, c.sb(ctx)
    st = sb(f"{tag}_stats", [P, TILES, 6])
    tmp = sb(f"{tag}_stats_tmp", [P, 3, TILES])
    vec = c.sem(ctx, f"{tag}_stats_vec")
    pool = c.sem(ctx, f"{tag}_stats_pool")
    n, step = TILES, 8

    def on_vector(dve):
        with dve.Fori(0, n // step) as j:
            for u in range(step):
                i = j * step + u
                nc.vector.bn_stats(st[:, i, :], c.x[:, i, :]).then_inc(vec, 1)
        me, ve, mo, vo = (st[:, :, k] for k in (1, 2, 4, 5))
        s, d, v = (tmp[:, k, :] for k in range(3))
        dve.wait_ge(vec, n)
        nc.vector.tensor_tensor(s, me, mo, ALU.add).then_inc(vec, 1)
        nc.vector.tensor_tensor(d, me, mo, ALU.subtract).then_inc(vec, 1)
        nc.vector.tensor_tensor(v, ve, vo, ALU.add).then_inc(vec, 1)
        dve.wait_ge(vec, n + 3)
        nc.vector.tensor_scalar(c.mean[:, :], s, 0.5, None, ALU.mult).then_inc(vec, 1)
        nc.vector.tensor_tensor(d, d, d, ALU.mult).then_inc(vec, 1)
        dve.wait_ge(vec, n + 5)
        nc.vector.scalar_tensor_tensor(out=v, in0=d, scalar=E / 4.0, in1=v, op0=ALU.mult,
                                       op1=ALU.add).then_inc(vec, 1)
        dve.wait_ge(vec, n + 6)
        nc.vector.tensor_scalar(v, v, 1.0 / E, LN_EPS, ALU.mult, ALU.add).then_inc(vec, 1)

    def on_gpsimd(gp):
        gp.wait_ge(vec, n + 7)
        nc.gpsimd.tensor_tensor(c.rstd[:, :], tmp[:, 2, :], c.minus_half[:, :], ALU.pow).then_inc(pool, 1)
        gp.wait_ge(pool, 1)

    return on_vector, on_gpsimd


def normalize(c, st, rows, i):
    c.nc.vector.tensor_scalar(rows, c.x[:, i, :], c.mean[:, bass.ds(i, 1)], c.rstd[:, bass.ds(i, 1)],
                              ALU.subtract, ALU.mult).then_inc(st("norm"), 1)


def modulate(c, eng, st, rows, i, block, shift, scale):
    b = i // NT
    eng.tensor_tensor(rows, rows, c.mod[:, block, b, scale, :], ALU.mult).then_inc(st("scaled"), 1)
    eng.wait_ge(st.sem, st.at("scaled", i))
    eng.tensor_tensor(rows, rows, c.mod[:, block, b, shift, :], ALU.add).then_inc(st("shifted"), 1)


def linear_attention(c):
    nc, inp, bk = c.nc, c.inp, c.bank
    proj, small, tr, out = bk[0], bk[1], bk[6], bk[7]
    level = [c.psum[:, 2:4, P * k:P * k + P] for k in range(4)] + [c.psum[:, 4:6, 0:P]]
    level_step = ("l0123",) * 4 + ("l4",)
    with ExitStack() as ctx:
        sb = c.sb(ctx)
        wk, wq, wv, wo = (sb(f"la_{n}", [P, E]) for n in ("wk", "wq", "wv", "wo"))
        g1 = sb("la_g1", [P, GD])
        g2 = sb("la_g2", [GD, E])
        wog = sb("la_wog", [P, B, E])
        delta = sb("la_delta", [P, 2])
        norm_w = sb("la_norm_w", [P, 1])
        masks = sb("la_masks", [P, NLEV, P], U32)
        ones = sb("la_ones", [P, P])
        reset = sb("la_reset", [P, TILES])
        state = sb("la_state", [P, P])
        ring = lambda name, *shape: sb("la_" + name, [P, RING, *shape])
        rows, hT, v, g1T, y = (ring(n, P) for n in ("rows", "hT", "v", "g1T", "y"))
        ex = ring("ex", 2, P)
        ln = ring("ln", 2, P)
        sg = ring("sg", 2, P)
        kq = ring("kq", 2, P)
        cum = ring("cum", P)
        last = ring("last", 1)
        dist = ring("dist", NLEV, P)
        dec = ring("dec", NLEV + 1, P)
        qe, ke = ring("qe", NLEV, P), ring("ke", NLEV, P)
        dstart, dend = ring("dstart", P), ring("dend", P)
        qs, kend, kendT = ring("qs", P), ring("kend", P), ring("kendT", P)
        attn = ring("attn", GH, P)
        eg, lg, sgate = ring("eg", E), ring("lg", E), ring("sgate", E)
        og, osq, oT = ring("og", E), ring("osq", E), ring("oT", E)
        ms, rr = ring("ms", GH), ring("rr", GH)

        loaded, pre = c.sem(ctx, "la_loaded"), c.sem(ctx, "la_pre")
        st = lambda name, *names: c.steps(ctx, "la_" + name, *names)
        v_norm, g_norm = st("v_norm", "norm"), st("g_norm", "scaled", "shifted")
        p_h, a_h = st("p_h", "hT"), st("a_h", "hT")
        p_proj = st("p_proj", "z", "y", "v", "g1")
        a_proj = st("a_proj", "exz", "exy", "y", "v", "g1")
        v_clip = st("v_clip", "exz", "exy")
        a_sig = st("a_sig", "ln", "sg")
        v_kq = st("v_kq", "cum", "last", "k", "q")
        g_dist = st("g_dist", *[f"d{k}" for k in range(NLEV)])
        v_abs = st("v_abs", "abs")
        a_dec = st("a_dec", "start", "end", "base", "inv", "levels")
        v_qk = st("v_qk", "qe", "ke")
        g_qk = st("g_qk", "qs", "kend")
        p_att = st("p_att", "l0123", "l4", "kendT", "gate")
        v_att = st("v_att", *[f"m{k}" for k in range(NLEV)], "clip")
        a_kend = st("a_kend", "kendT", "eg")
        a_gate = st("a_gate", "ln", "sg")
        p_out = st("p_out", "o", "state")
        v_state = st("v_state", "s0", "s1", "og")
        a_sq = st("a_sq", "sq")
        v_ms = st("v_ms", "sum", "eps")
        g_rr = st("g_rr", "pow")
        v_on = st("v_on", "on")
        p_oT, a_oT = st("p_oT", "oT"), st("a_oT", "oT")
        p_wo, v_x = st("p_wo", "wo"), st("v_x", "x")
        every = [v_norm, g_norm, p_h, a_h, p_proj, a_proj, v_clip, a_sig, v_kq, g_dist, v_abs, a_dec, v_qk, g_qk, p_att,
                 v_att, a_kend, a_gate, p_out, v_state, a_sq, v_ms, g_rr, v_on, p_oT, a_oT, p_wo, v_x]
        LOADS = 10
        statistics, inverse = row_statistics(c, ctx, "la")

        with nc.Block() as block:

            @block.sync
            def _(sp):
                for t, name in ((wk, "L0_attn_Wk"), (wq, "L0_attn_Wq"), (wv, "L0_attn_Wv"), (g1, "L0_attn_G1"),
                                (g2, "L0_attn_G2"), (wo, "L0_attn_Wo"), (masks, "level_masks")):
                    sp.dma_start(t[...], inp[name]).then_inc(loaded, 16)
                sp.dma_start(delta[:, 1:2], inp["L0_attn_delta"].unsqueeze(1)).then_inc(loaded, 16)
                sp.dma_start(norm_w[:, :], inp["L0_attn_norm_w"].unsqueeze(1)).then_inc(loaded, 16)
                sp.dma_start(reset[:, :], inp["batch_reset"]).then_inc(loaded, 16)

            @block.gpsimd
            def _(gp):
                prime(gp, every)
                nc.gpsimd.memset(attn[...], 0.0)
                nc.gpsimd.memset(ones[:, :], 1.0)
                nc.gpsimd.memset(state[:, :], 0.0)
                inverse(gp)

            @block.vector
            def _(dve):
                statistics(dve)
                dve.wait_ge(loaded, 16 * LOADS)
                nc.vector.tensor_scalar(delta[:, 0:1], delta[:, 1:2], -1.0, None, ALU.mult).then_inc(pre, 1)
                nc.vector.tensor_scalar(wo[:, :], wo[:, :], norm_w[:, 0:1], None, ALU.mult).then_inc(pre, 1)
                dve.wait_ge(pre, 2)
                nc.vector.tensor_tensor(wog[:, :, :], rows_bc(wo[:, :], B), c.mod[:, 0, :, GA, :],
                                        ALU.mult).then_inc(pre, 1)
                dve.wait_ge(pre, 3)

        with nc.Block() as block:

            @block.vector
            def _(dve):

                def norm(i, u):
                    dve.wait_ge(p_h.sem, p_h.at("hT", i - RING))
                    normalize(c, v_norm, rows[:, u, :], i)

                def clip(i, u):
                    dve.wait_ge(a_proj.sem, a_proj.at("exz", i))
                    nc.vector.tensor_scalar_min(ex[:, u, 0, :], ex[:, u, 0, :], MAX_EXP).then_inc(v_clip("exz"), 1)
                    dve.wait_ge(a_proj.sem, a_proj.at("exy", i))
                    nc.vector.tensor_scalar_min(ex[:, u, 1, :], ex[:, u, 1, :], MAX_SIG).then_inc(v_clip("exy"), 1)

                def keys(i, u):
                    dve.wait_ge(a_sig.sem, a_sig.at("ln", i))
                    nc.vector.tensor_tensor_scan(cum[:, u, :], ones[:, :], ln[:, u, 0, :], 0.0, ALU.mult, ALU.add)\
                      .then_inc(v_kq("cum"), 1)
                    dve.wait_ge(v_kq.sem, v_kq.at("cum", i))
                    nc.vector.tensor_scalar(last[:, u, :], cum[:, u, P - 1:P], -1.0, None, ALU.mult)\
                      .then_inc(v_kq("last"), 1)
                    dve.wait_ge(a_sig.sem, a_sig.at("sg", i))
                    nc.vector.tensor_tensor(kq[:, u, 0, :], ex[:, u, 0, :], sg[:, u, 0, :], ALU.mult)\
                      .then_inc(v_kq("k"), 1)
                    nc.vector.tensor_tensor(kq[:, u, 1, :], y[:, u, :], sg[:, u, 1, :], ALU.mult)\
                      .then_inc(v_kq("q"), 1)

                def absolute(i, u):
                    dve.wait_ge(g_dist.sem, g_dist.at(f"d{NLEV - 1}", i))
                    d = dist[:, u, 1:, :]
                    nc.vector.scalar_tensor_tensor(out=d, in0=d, scalar=-1.0, in1=d, op0=ALU.mult, op1=ALU.min)\
                      .then_inc(v_abs("abs"), 1)

                def scaled(i, u):
                    dve.wait_ge(a_dec.sem, a_dec.at("levels", i))
                    nc.vector.tensor_tensor(qe[:, u, :, :], dec[:, u, 0:NLEV, :], rows_bc(kq[:, u, 1, :], NLEV),
                                            ALU.mult).then_inc(v_qk("qe"), 1)
                    nc.vector.tensor_tensor(ke[:, u, :, :], dec[:, u, 1:NLEV + 1, :],
                                            rows_bc(kq[:, u, 0, :], NLEV), ALU.mult).then_inc(v_qk("ke"), 1)

                def levels(i, u):
                    for k in range(NLEV):
                        dve.wait_ge(p_att.sem, p_att.at(level_step[k], i))
                        if k:
                            dve.wait_ge(v_att.sem, v_att.at(f"m{k - 1}", i))
                        dve.nop(nofuse=True)
                        nc.vector.copy_predicated(attn[:, u, :, :], rows_bc(masks[:, k, :], GH), level[k])\
                          .then_inc(v_att(f"m{k}"), 1)
                    dve.wait_ge(a_kend.sem, a_kend.at("eg", i))
                    nc.vector.tensor_scalar_min(eg[:, u, :], eg[:, u, :], MAX_SIG).then_inc(v_att("clip"), 1)

                def update(i, u):
                    dve.wait_ge(p_out.sem, p_out.at("state", i))
                    for h in range(GH):
                        s = slice(GD * h, GD * h + GD)
                        nc.vector.scalar_tensor_tensor(
                            out=state[s, s], in0=state[s, s], scalar=dstart[s, u, P - 1:P],
                            in1=out[s, E + GD * h:E + GD * h + GD], op0=ALU.mult, op1=ALU.add)\
                          .then_inc(v_state(f"s{h}"), 1)
                    dve.wait_ge(a_gate.sem, a_gate.at("sg", i))
                    nc.vector.tensor_tensor(og[:, u, :], out[:, 0:E], sgate[:, u, :], ALU.mult)\
                      .then_inc(v_state("og"), 1)

                def mean_square(i, u):
                    dve.wait_ge(a_sq.sem, a_sq.at("sq", i))
                    nc.vector.tensor_reduce(ms[:, u, :], osq[:, u, :].rearrange("p (h d) -> p h d", h=GH), AX_X,
                                            ALU.add).then_inc(v_ms("sum"), 1)
                    dve.wait_ge(v_ms.sem, v_ms.at("sum", i))
                    nc.vector.tensor_scalar(ms[:, u, :], ms[:, u, :], 1.0 / GD, 1e-5, ALU.mult, ALU.add)\
                      .then_inc(v_ms("eps"), 1)

                def normed(i, u):
                    dve.wait_ge(g_rr.sem, g_rr.at("pow", i))
                    o3 = og[:, u, :].rearrange("p (h d) -> p h d", h=GH)
                    nc.vector.tensor_tensor(o3, o3, cols_bc(rr[:, u, :], GD), ALU.mult).then_inc(v_on("on"), 1)

                def residual(i, u):
                    dve.wait_ge(p_wo.sem, p_wo.at("wo", i))
                    nc.vector.tensor_tensor(c.x[:, i, :], c.x[:, i, :], tr[:, 3 * P:4 * P], ALU.add)\
                      .then_inc(v_x("x"), 1)

                pipeline(dve, [(clip, 3), (normed, 7), (absolute, 4), (levels, 6), (keys, 3), (norm, 0),
                               (update, 6), (scaled, 4), (residual, 7), (mean_square, 6)])

            @block.gpsimd
            def _(gp):

                def distances(i, u):
                    gp.wait_ge(v_kq.sem, v_kq.at("cum", i))
                    for k, h in enumerate(HALVES):
                        blocks = cum[:, u, :].rearrange("p (n w) -> p n w", w=2 * h)
                        nc.gpsimd.tensor_tensor(dist[:, u, k, :].rearrange("p (n w) -> p n w", w=2 * h), blocks,
                                                blocks[:, :, h - 1:h].broadcast_to([P, P // (2 * h), 2 * h]),
                                                ALU.subtract).then_inc(g_dist(f"d{k}"), 1)

                def ends(i, u):
                    gp.wait_ge(v_kq.sem, v_kq.at("q", i))
                    gp.wait_ge(a_dec.sem, a_dec.at("end", i))
                    nc.gpsimd.tensor_tensor(qs[:, u, :], kq[:, u, 1, :], dstart[:, u, :], ALU.mult)\
                      .then_inc(g_qk("qs"), 1)
                    nc.gpsimd.tensor_tensor(kend[:, u, :], kq[:, u, 0, :], dend[:, u, :], ALU.mult)\
                      .then_inc(g_qk("kend"), 1)

                def inverse_rms(i, u):
                    gp.wait_ge(v_ms.sem, v_ms.at("eps", i))
                    nc.gpsimd.tensor_tensor(rr[:, u, :], ms[:, u, :], c.minus_half[:, 0:GH], ALU.pow)\
                      .then_inc(g_rr("pow"), 1)

                def shift(i, u):
                    gp.wait_ge(v_norm.sem, v_norm.at("norm", i))
                    modulate(c, nc.gpsimd, g_norm, rows[:, u, :], i, 0, SA, CA)

                pipeline(gp, [(inverse_rms, 7), (ends, 4), (distances, 3), (shift, 0)])

            @block.scalar
            def _(act):

                def kend_rows(i, u):
                    act.wait_ge(p_att.sem, p_att.at("gate", i))
                    nc.scalar.activation(kendT[:, u, :], tr[:, 0:P], ACT.Copy).then_inc(a_kend("kendT"), 1)
                    nc.scalar.activation(eg[:, u, :], tr[:, 2 * P:3 * P], ACT.Exp, scale=-1.0)\
                      .then_inc(a_kend("eg"), 1)

                def square(i, u):
                    act.wait_ge(v_state.sem, v_state.at("og", i))
                    nc.scalar.activation(osq[:, u, :], og[:, u, :], ACT.Square).then_inc(a_sq("sq"), 1)

                def o_columns(i, u):
                    act.wait_ge(p_oT.sem, p_oT.at("oT", i))
                    nc.scalar.activation(oT[:, u, :], tr[:, P:2 * P], ACT.Copy).then_inc(a_oT("oT"), 1)

                def decays(i, u):
                    act.wait_ge(v_kq.sem, v_kq.at("last", i))
                    nc.scalar.activation(dstart[:, u, :], cum[:, u, :], ACT.Exp, scale=-1.0,
                                         bias=reset[:, bass.ds(i, 1)]).then_inc(a_dec("start"), 1)
                    nc.scalar.activation(dend[:, u, :], cum[:, u, :], ACT.Exp, bias=last[:, u, :])\
                      .then_inc(a_dec("end"), 1)
                    act.wait_ge(g_dist.sem, g_dist.at("d0", i))
                    nc.scalar.activation(dec[:, u, 0, :], dist[:, u, 0, :], ACT.Exp, scale=-1.0)\
                      .then_inc(a_dec("base"), 1)
                    nc.scalar.activation(dec[:, u, NLEV, :], dist[:, u, 0, :], ACT.Exp).then_inc(a_dec("inv"), 1)
                    act.wait_ge(v_abs.sem, v_abs.at("abs", i))
                    nc.scalar.activation(dec[:, u, 1:NLEV, :], dist[:, u, 1:NLEV, :], ACT.Exp)\
                      .then_inc(a_dec("levels"), 1)

                def projections(i, u):
                    act.wait_ge(p_proj.sem, p_proj.at("g1", i))
                    act.wait_ge(p_out.sem, p_out.at("state", i - 4))
                    nc.scalar.activation(ex[:, u, 0, :], proj[:, 0:P], ACT.Exp, bias=delta[:, 0:1], scale=-1.0)\
                      .then_inc(a_proj("exz"), 1)
                    nc.scalar.activation(ex[:, u, 1, :], proj[:, P:2 * P], ACT.Exp, scale=-1.0)\
                      .then_inc(a_proj("exy"), 1)
                    nc.scalar.activation(y[:, u, :], proj[:, P:2 * P], ACT.Copy).then_inc(a_proj("y"), 1)
                    nc.scalar.activation(v[:, u, :], proj[:, 2 * P:3 * P], ACT.Copy).then_inc(a_proj("v"), 1)
                    nc.scalar.activation(g1T[0:GD, u, :], proj[0:GD, 3 * P:4 * P], ACT.Copy)\
                      .then_inc(a_proj("g1"), 1)

                def sigmoids(i, u):
                    act.wait_ge(v_clip.sem, v_clip.at("exy", i))
                    nc.scalar.activation(ln[:, u, :, :], ex[:, u, :, :], ACT.Ln, bias=1.0).then_inc(a_sig("ln"), 1)
                    act.wait_ge(a_sig.sem, a_sig.at("ln", i))
                    nc.scalar.activation(sg[:, u, :, :], ln[:, u, :, :], ACT.Exp, scale=-1.0).then_inc(a_sig("sg"), 1)

                def gate(i, u):
                    act.wait_ge(v_att.sem, v_att.at("clip", i))
                    nc.scalar.activation(lg[:, u, :], eg[:, u, :], ACT.Ln, bias=1.0).then_inc(a_gate("ln"), 1)
                    act.wait_ge(a_gate.sem, a_gate.at("ln", i))
                    nc.scalar.activation(sgate[:, u, :], lg[:, u, :], ACT.Exp, scale=-1.0).then_inc(a_gate("sg"), 1)

                def h_columns(i, u):
                    act.wait_ge(p_h.sem, p_h.at("hT", i))
                    nc.scalar.activation(hT[:, u, :], small[:, 0:P], ACT.Copy).then_inc(a_h("hT"), 1)

                nc.scalar.preload_act_table_set("natural_log_exp_and_others")
                pipeline(act, [(sigmoids, 3), (kend_rows, 6), (decays, 4), (gate, 6), (o_columns, 7),
                               (h_columns, 1), (projections, 2), (square, 6)])

            @block.tensor
            def _(pe):

                def output(i, u):
                    pe.wait_ge(v_state.sem, v_state.at("og", i - 1))
                    pe.wait_ge(g_qk.sem, g_qk.at("qs", i))
                    nc.tensor.matmul(out[:, 0:E], qs[:, u, :], state[:, :], start=True, stop=True)
                    pe.wait_ge(v_att.sem, v_att.at(f"m{NLEV - 1}", i))
                    for h in range(GH):
                        m = nc.tensor.matmul(out[:, GD * h:GD * h + GD], attn[:, u, h, :],
                                             v[:, u, GD * h:GD * h + GD], start=False, stop=True,
                                             skip_group_check=True)
                    m.then_inc(p_out("o"), 1)
                    pe.wait_ge(a_kend.sem, a_kend.at("kendT", i))
                    nc.tensor.matmul(out[:, E:2 * E], kendT[:, u, :], v[:, u, :], start=True, stop=True)\
                      .then_inc(p_out("state"), 1)

                def scores(i, u):
                    pe.wait_ge(v_qk.sem, v_qk.at("ke", i))
                    for k in range(NLEV):
                        pe.wait_ge(v_att.sem, v_att.at("m3" if k < 4 else "m4", i - 1))
                        for h in range(GH):
                            s = slice(GD * h, GD * h + GD)
                            lv = (k + NLEV - 1) % NLEV
                            m = nc.tensor.matmul(level[k][:, h, :], ke[s, u, lv, :], qe[s, u, k, :],
                                                 start=True, stop=True)
                        if k >= 3:
                            m.then_inc(p_att(level_step[k]), 1)
                    pe.wait_ge(g_qk.sem, g_qk.at("kend", i))
                    pe.wait_ge(v_x.sem, v_x.at("x", i - 2))
                    pe.wait_ge(a_kend.sem, a_kend.at("eg", i - 1))
                    nc.tensor.transpose(tr[:, 0:P], kend[:, u, :], c.ident[:, :]).then_inc(p_att("kendT"), 1)
                    nc.tensor.matmul(tr[:, 2 * P:3 * P], g1T[0:GD, u, :], g2[:, :], start=True, stop=True)\
                      .then_inc(p_att("gate"), 1)

                def o_turn(i, u):
                    pe.wait_ge(a_kend.sem, a_kend.at("eg", i + 1))
                    pe.wait_ge(v_on.sem, v_on.at("on", i))
                    nc.tensor.transpose(tr[:, P:2 * P], og[:, u, :], c.ident[:, :]).then_inc(p_oT("oT"), 1)

                def project(i, u):
                    pe.wait_ge(a_h.sem, a_h.at("hT", i))
                    pe.wait_ge(a_proj.sem, a_proj.at("g1", i - 1))
                    nc.tensor.matmul(proj[:, 0:P], wk[:, :], hT[:, u, :], start=True, stop=True)\
                      .then_inc(p_proj("z"), 1)
                    nc.tensor.matmul(proj[:, P:2 * P], wq[:, :], hT[:, u, :], start=True, stop=True)\
                      .then_inc(p_proj("y"), 1)
                    nc.tensor.matmul(proj[:, 2 * P:3 * P], hT[:, u, :], wv[:, :], start=True, stop=True)\
                      .then_inc(p_proj("v"), 1)
                    nc.tensor.matmul(proj[0:GD, 3 * P:4 * P], g1[:, :], hT[:, u, :], start=True, stop=True)\
                      .then_inc(p_proj("g1"), 1)

                def o_project(i, u):
                    pe.wait_ge(a_oT.sem, a_oT.at("oT", i))
                    nc.tensor.matmul(tr[:, 3 * P:4 * P], oT[:, u, :], wog[:, i // NT, :], start=True, stop=True)\
                      .then_inc(p_wo("wo"), 1)

                def h_turn(i, u):
                    pe.wait_ge(g_norm.sem, g_norm.at("shifted", i))
                    pe.wait_ge(a_h.sem, a_h.at("hT", i - 1))
                    nc.tensor.transpose(small[:, 0:P], rows[:, u, :], c.ident[:, :]).then_inc(p_h("hT"), 1)

                pipeline(pe, [(project, 2), (o_turn, 7), (h_turn, 1), (output, 6), (o_project, 7), (scores, 5)])


def start_layers(c, y):
    nc = c.nc
    with ExitStack() as ctx:
        normed = c.sem(ctx, "sl_normed")
        statistics, inverse = row_statistics(c, ctx, "sl")
        shifted = [c.sem(ctx, f"sl_shifted{b}") for b in range(B)]

        def modulate_batch(eng, b):
            t = y[:, b * NT:b * NT + NT, :]
            eng.tensor_tensor(t, t, rows_bc(c.mod[:, 0, b, CB, :], NT), ALU.mult).then_inc(shifted[b], 1)
            eng.wait_ge(shifted[b], 1)
            eng.tensor_tensor(t, t, rows_bc(c.mod[:, 0, b, SB, :], NT), ALU.add).then_inc(shifted[b], 1)
            eng.wait_ge(shifted[b], 2)

        with nc.Block() as block:

            @block.vector
            def _(dve):
                statistics(dve)

            @block.gpsimd
            def _(gp):
                inverse(gp)

        with nc.Block() as block:

            @block.vector
            def _(dve):
                for b in (1, 0):
                    with dve.Fori(0, NT // 8) as j:
                        for u in range(8):
                            i = j * 8 + (b * NT + u)
                            nc.vector.tensor_scalar(y[:, i, :], c.x[:, i, :], c.mean[:, bass.ds(i, 1)],
                                                    c.rstd[:, bass.ds(i, 1)], ALU.subtract, ALU.mult)\
                              .then_inc(normed, 1)
                dve.wait_ge(normed, TILES)
                modulate_batch(nc.vector, 0)

            @block.gpsimd
            def _(gp):
                gp.wait_ge(normed, NT)
                modulate_batch(nc.gpsimd, 1)


def end_layers(c, y):
    nc = c.nc
    with ExitStack() as ctx:
        done = c.sem(ctx, "el_done")
        with nc.Block() as block:

            @block.vector
            def _(dve):
                for b in range(B):
                    t = slice(b * NT, b * NT + NT)
                    nc.vector.tensor_tensor(y[:, t, :], y[:, t, :], rows_bc(c.mod[:, 0, b, GB, :], NT), ALU.mult)\
                      .then_inc(done, 1)
                    dve.wait_ge(done, 2 * b + 1)
                    nc.vector.tensor_tensor(c.x[:, t, :], c.x[:, t, :], y[:, t, :], ALU.add).then_inc(done, 1)


def windowed_attention(c, y, ctx):
    nc, inp, bk = c.nc, c.inp, c.bank
    sb = c.sb(ctx)
    wqkv = sb("wa_wqkv", [P, 3 * INNER])
    wo = sb("wa_wo", [P, INNER // P, E])
    tabs = sb("wa_tabs", [P, 4, NT, WD])
    scales = sb("wa_scales", [P, 4, WD])
    bias32 = sb("wa_bias32", [P, 2, P])
    bias = sb("wa_bias", [P, 2, P], BF16)
    identb = sb("wa_identb", [P, P], BF16)
    keep = sb("wa_keep", [P, TILES + 1])
    ring = lambda name, *shape: sb("wa_" + name, [P, RING, *shape])
    rows, hT = ring("rows", E), ring("hT", P + 1)
    ks = ring("v", INNER)
    vm = ring("vm", INNER)
    pair = lambda name, *shape: sb("wa_" + name, [P, 2, *shape])
    sq = pair("sq", 2, INNER)
    ss, rn, rq = ring("ss", 2 * WH), ring("rn", 2 * WH), ring("rq", WH)
    qr, kr = ring("qr", INNER), ring("kr", INNER)
    tmp = pair("tmp", 2, INNER)
    qT, kT = pair("qT", WH // 2, P), pair("kT", WH // 2, P)
    kbT = pair("kbT", WH // 2, P)
    mx, nb, rs, rrs = (ring(n, WH) for n in ("mx", "nb", "rs", "rrs"))
    pr = pair("p", WH, P)
    pT = pair("pT", 2, WH // 2, P)
    ob, oT = pair("o", INNER), pair("oT", INNER // P, P)

    loaded, pre = c.sem(ctx, "wa_loaded"), c.sem(ctx, "wa_pre")
    st = lambda name, *names: c.steps(ctx, "wa_" + name, *names)
    g_stage = st("g_stage", "rows")
    p_h, a_h = st("p_h", "hT"), st("a_h", "lo", "hi", "carry")
    p_qkv = st("p_qkv", "q", "k", "v")
    a_sq = st("a_sq", "q", "k", "v")
    v_rot = st("v_rot", "q1", "q2", "q3", "k1", "k2", "k3")
    v_ss = st("v_ss", "sum", "clip")
    g_rot = st("g_rot", "q", "pow", "k", "vlo", "vhi")
    v_scale = st("v_scale", "rq", "k")
    p_turn = st("p_turn", "qT", "kT")
    a_turn = st("a_turn", "qT", "kT", "kfT", "kbT")
    p_sim = st("p_sim", "even", "odd")
    v_max = st("v_max", "m0", "nb0", "m1", "nb1")
    a_exp = st("a_exp", *[f"e{h}" for h in (*range(0, WH, 2), *range(1, WH, 2))])
    p_pT, a_pT = st("p_pT", "even", "odd"), st("a_pT", "even", "odd")
    p_pv = st("p_pv", "o")
    v_o = st("v_o", "rrs", "o")
    p_oT, a_oT = st("p_oT", "oT"), st("a_oT", "oT")
    p_wo, v_y = st("p_wo", "wo"), st("v_y", "y")
    every = [g_stage, p_h, a_h, p_qkv, a_sq, v_rot, v_ss, g_rot, v_scale, p_turn, a_turn, p_sim, v_max, a_exp,
             p_pT, a_pT, p_pv, v_o, p_oT, a_oT, p_wo, v_y]

    def prepare():
        with nc.Block() as block:

            @block.gpsimd
            def _(gp):
                prime(gp, every)
                nc.gpsimd.memset(kbT[...], 0.0)
                nc.gpsimd.memset(vm[...], 0.0)
                nc.gpsimd.memset(hT[...], 0.0)

            @block.sync
            def _(sp):
                for t, name in ((bias32, "window_bias"), (keep, "batch_keep")):
                    sp.dma_start(t[...], inp[name]).then_inc(loaded, 16)

            @block.vector
            def _(dve):
                nc.vector.tensor_copy(identb[:, :], c.ident[:, :]).then_inc(pre, 1)
                dve.wait_ge(loaded, 32)
                nc.vector.tensor_copy(bias[...], bias32[...]).then_inc(pre, 1)
                dve.wait_ge(pre, 2)

    def load_layer(l):
        n = 10
        with nc.Block() as block:

            @block.sync
            def _(sp):
                li = bass.ds(l, 1)
                sp.dma_start(tabs[...], inp["rotations"]).then_inc(loaded, 16)
                for k, name in enumerate(("L0_ffn_q_scale", "L0_ffn_k_scale")):
                    row = inp[name][li, :]
                    h = WD // 2
                    for dst, lo in ((scales[:, 2 * k, :], 0), (scales[:, 2 * k + 1, 0:h], h),
                                    (scales[:, 2 * k + 1, h:WD], 0)):
                        w = dst.shape[1]
                        sp.dma_start(dst, row[:, lo:lo + w].broadcast_to([P, w])).then_inc(loaded, 16)
                sp.dma_start(wqkv[:, :], inp["L0_ffn_wqkv"][li, :, :].rearrange("a e n -> (a e) n"))\
                  .then_inc(loaded, 16)
                sp.dma_start(wo[...], inp["L0_ffn_wo"][li, :, :].rearrange("a (c p) e -> p (a c) e", p=P))\
                  .then_inc(loaded, 16)

            @block.vector
            def _(dve):
                dve.wait_ge(loaded, l * (16 * 9) + 16 * 11)
                for k in range(4):
                    nc.vector.tensor_tensor(tabs[:, k, :, :], tabs[:, k, :, :], rows_bc(scales[:, k, :], NT),
                                            ALU.mult).then_inc(pre, 1)
                dve.wait_ge(pre, 4 * l + 6)
                dve.nop(nofuse=True)

    def run(l):
        for s in every:
            s.base = l * TILES
        q_bank, k_bank, v_bank, hw_bank, turn_bank, even, odd, o_bank = bk
        heads = lambda ap: ap.rearrange("p (h d) -> p h d", d=WD)
        with nc.Block() as block:

            @block.gpsimd
            def _(gp):

                def stage(i, u):
                    gp.wait_ge(g_rot.sem, g_rot.at("vhi", i - 5))
                    gp.wait_ge(p_h.sem, p_h.at("hT", i - RING))
                    gp.nop(nofuse=True)
                    nc.gpsimd.tensor_copy(rows[:, u, :], y[:, i, :]).then_inc(g_stage("rows"), 1)

                def rotate(i, u):
                    gp.wait_ge(g_rot.sem, g_rot.at("vhi", i - 1))
                    gp.wait_ge(v_rot.sem, v_rot.at("q3", i))
                    nc.gpsimd.tensor_tensor(qr[:, u, :], qr[:, u, :], tmp[:, u % 2, 0, :], ALU.add)\
                      .then_inc(g_rot("q"), 1)
                    gp.wait_ge(v_ss.sem, v_ss.at("clip", i))
                    nc.gpsimd.tensor_tensor(rn[:, u, :], ss[:, u, :], c.minus_half[:, 0:2 * WH], ALU.pow)\
                      .then_inc(g_rot("pow"), 1)
                    gp.wait_ge(v_rot.sem, v_rot.at("k3", i))
                    nc.gpsimd.tensor_tensor(kr[:, u, :], kr[:, u, :], tmp[:, u % 2, 1, :], ALU.add)\
                      .then_inc(g_rot("k"), 1)
                    gp.wait_ge(a_sq.sem, a_sq.at("v", i))
                    gp.wait_ge(g_rot.sem, g_rot.at("k", i))
                    gp.nop(nofuse=True)
                    nc.gpsimd.tensor_copy(vm[0:WIN, u, :], ks[0:WIN, u, :]).then_inc(g_rot("vlo"), 1)
                    gp.wait_ge(g_rot.sem, g_rot.at("vlo", i))
                    gp.wait_ge(p_pv.sem, p_pv.at("o", i - 3))
                    gp.nop(nofuse=True)
                    nc.gpsimd.tensor_copy(vm[WIN:P, (u + 1) % RING, :], ks[WIN:P, u, :]).then_inc(g_rot("vhi"), 1)

                pipeline(gp, [(stage, 0), (rotate, 4)])

            @block.vector
            def _(dve):

                def rotate(i, u):
                    for k, (name, bank, dst) in enumerate((("q", q_bank, qr), ("k", k_bank, kr))):
                        src, out, cross = heads(bank), heads(dst[:, u, :]), heads(tmp[:, u % 2, k, :])
                        cos, sin = tabs[:, 2 * k, i % NT, :], tabs[:, 2 * k + 1, i % NT, :]
                        h = WD // 2
                        dve.wait_ge(a_sq.sem, a_sq.at(name, i))
                        nc.vector.tensor_tensor(out, src, rows_bc(cos, WH), ALU.mult).then_inc(v_rot(name + "1"), 1)
                        nc.vector.tensor_tensor(cross[:, :, 0:h], src[:, :, h:WD], rows_bc(sin[:, 0:h], WH),
                                                ALU.mult).then_inc(v_rot(name + "2"), 1)
                        nc.vector.tensor_tensor(cross[:, :, h:WD], src[:, :, 0:h], rows_bc(sin[:, h:WD], WH),
                                                ALU.mult).then_inc(v_rot(name + "3"), 1)

                def norms(i, u):
                    nc.vector.tensor_reduce(ss[:, u, :], sq[:, u % 2, :, :].rearrange("p a (h d) -> p (a h) d", d=WD),
                                            AX_X, ALU.add).then_inc(v_ss("sum"), 1)
                    dve.wait_ge(v_ss.sem, v_ss.at("sum", i))
                    nc.vector.tensor_scalar_max(ss[:, u, :], ss[:, u, :], 1e-24).then_inc(v_ss("clip"), 1)

                def scale(i, u):
                    dve.wait_ge(g_rot.sem, g_rot.at("pow", i))
                    nc.vector.tensor_scalar(rq[:, u, :], rn[:, u, 0:WH], QK_SCALE, None, ALU.mult)\
                      .then_inc(v_scale("rq"), 1)
                    dve.wait_ge(g_rot.sem, g_rot.at("k", i))
                    kh = heads(kr[:, u, :])
                    nc.vector.tensor_tensor(kh, kh, cols_bc(rn[:, u, WH:2 * WH], WD), ALU.mult)\
                      .then_inc(v_scale("k"), 1)

                def row_max(i, u):
                    m = mx[:, u, :].rearrange("p (h r) -> p r h", r=2)
                    by_parity = lambda t: t[:, u, :].rearrange("p (h r) -> p r h", r=2)
                    for r, (name, bank) in enumerate((("even", even), ("odd", odd))):
                        dve.wait_ge(p_sim.sem, p_sim.at(name, i))
                        nc.vector.tensor_reduce(m[:, r, :], bank.rearrange("p (h k) -> p h k", k=P), AX_X, ALU.max)\
                          .then_inc(v_max(f"m{r}"), 1)
                        dve.wait_ge(v_max.sem, v_max.at(f"m{r}", i))
                        nc.vector.scalar_tensor_tensor(out=by_parity(nb)[:, r, :], in0=m[:, r, :], scalar=-1.0,
                                                       in1=by_parity(rq)[:, r, :], op0=ALU.mult,
                                                       op1=ALU.mult).then_inc(v_max(f"nb{r}"), 1)

                def output(i, u):
                    dve.wait_ge(a_exp.sem, a_exp.at(f"e{WH - 1}", i))
                    nc.vector.reciprocal(rrs[:, u, :], rs[:, u, :]).then_inc(v_o("rrs"), 1)
                    dve.wait_ge(v_o.sem, v_o.at("rrs", i))
                    dve.wait_ge(p_pv.sem, p_pv.at("o", i))
                    nc.vector.tensor_tensor(heads(ob[:, u % 2, :]), heads(o_bank), cols_bc(rrs[:, u, :], WD), ALU.mult)\
                      .then_inc(v_o("o"), 1)

                def residual(i, u):
                    dve.wait_ge(p_wo.sem, p_wo.at("wo", i))
                    nc.vector.tensor_tensor(y[:, i, :], y[:, i, :], hw_bank[:, 0:E], ALU.add).then_inc(v_y("y"), 1)

                pipeline(dve, [(scale, 5), (row_max, 6), (residual, 9), (rotate, 3), (norms, 3), (output, 7)])

            @block.scalar
            def _(act):

                def o_columns(i, u):
                    act.wait_ge(p_oT.sem, p_oT.at("oT", i))
                    nc.scalar.activation(oT[:, u % 2, :, :].rearrange("p c t -> p (c t)"), turn_bank, ACT.Copy)\
                      .then_inc(a_oT("oT"), 1)

                def squares(i, u):
                    for k, (name, bank) in enumerate((("q", q_bank), ("k", k_bank))):
                        act.wait_ge(p_qkv.sem, p_qkv.at(name, i))
                        nc.scalar.activation(sq[:, u % 2, k, :], bank, ACT.Square).then_inc(a_sq(name), 1)

                def values(i, u):
                    act.wait_ge(p_qkv.sem, p_qkv.at("v", i))
                    act.wait_ge(p_pv.sem, p_pv.at("o", i - 4))
                    nc.scalar.activation(ks[:, u, :], v_bank, ACT.Copy).then_inc(a_sq("v"), 1)

                def turned(name, dst):
                    def f(i, u):
                        act.wait_ge(p_turn.sem, p_turn.at(name, i))
                        nc.scalar.activation(dst[:, u % 2, :, :].rearrange("p c t -> p (c t)"), turn_bank, ACT.Copy)\
                          .then_inc(a_turn(name), 1)
                        if name == "kT":
                            blocks = turn_bank.rearrange("p (c t) -> p c t", t=P)
                            nc.scalar.activation(kbT[:, u % 2, :, 0:WIN], blocks[:, :, 0:WIN], ACT.Copy)\
                              .then_inc(a_turn("kfT"), 1)
                            nc.scalar.activation(kbT[:, (u + 1) % 2, :, WIN:P], blocks[:, :, WIN:P], ACT.Copy,
                                                 scale=keep[:, bass.ds(i + 1, 1)]).then_inc(a_turn("kbT"), 1)
                    return f

                def p_columns(i, u):
                    for r, (name, bank) in enumerate((("even", even), ("odd", odd))):
                        act.wait_ge(p_pT.sem, p_pT.at(name, i))
                        nc.scalar.activation(pT[:, u % 2, r, :, :].rearrange("p c t -> p (c t)"), bank, ACT.Copy)\
                          .then_inc(a_pT(name), 1)

                def h_columns(i, u):
                    h = E // 2
                    act.wait_ge(p_h.sem, p_h.at("hT", i))
                    nc.scalar.activation(hT[0:h, u, 0:P], hw_bank[0:h, 0:P], ACT.Copy).then_inc(a_h("lo"), 1)
                    nc.scalar.activation(hT[h:P, u, 1:P + 1], hw_bank[h:P, 0:P], ACT.Copy).then_inc(a_h("hi"), 1)
                    act.wait_ge(a_h.sem, a_h.at("hi", i - 1))
                    nc.scalar.activation(hT[h:P, u, 0:1], hT[h:P, (u - 1) % RING, P:P + 1], ACT.Copy,
                                         scale=keep[h:P, bass.ds(i, 1)]).then_inc(a_h("carry"), 1)

                def exps(r):
                    def f(i, u):
                        act.wait_ge(v_max.sem, v_max.at(f"nb{r}", i))
                        for h in range(r, WH, 2):
                            k = h // 2
                            nc.scalar.activation(pr[:, u % 2, h, :], (even, odd)[r][:, P * k:P * k + P], ACT.Exp,
                                                 bias=nb[:, u, h:h + 1], scale=rq[:, u, h:h + 1],
                                                 accum_out=rs[:, u, h:h + 1]).then_inc(a_exp(f"e{h}"), 1)
                    return f

                nc.scalar.preload_act_table_set("natural_log_exp_and_others")
                pipeline(act, [(squares, 3), (exps(0), 6), (turned("qT", qT), 5), (exps(1), 6), (turned("kT", kT), 5), (values, 3),
                               (p_columns, 6), (o_columns, 8), (h_columns, 1)])

            @block.tensor
            def _(pe):

                def turn_o(i, u):
                    pe.wait_ge(v_o.sem, v_o.at("o", i))
                    pe.wait_ge(a_turn.sem, a_turn.at("kbT", i + 3))
                    for k in range(INNER // P):
                        m = nc.tensor.transpose(turn_bank[:, P * k:P * k + P], ob[:, u % 2, P * k:P * k + P],
                                                c.ident[:, :])
                    m.then_inc(p_oT("oT"), 1)

                def qkv(i, u):
                    pe.wait_ge(a_h.sem, a_h.at("carry", i))
                    for k, (name, bank) in enumerate((("q", q_bank), ("k", k_bank), ("v", v_bank))):
                        if name == "v":
                            pe.wait_ge(a_sq.sem, a_sq.at("v", i - 1))
                        else:
                            pe.wait_ge(v_rot.sem, v_rot.at(name + "3", i - 1))
                        nc.tensor.matmul(bank, hT[:, u, 0:P], wqkv[:, INNER * k:INNER * k + INNER], start=True,
                                         stop=True).then_inc(p_qkv(name), 1)

                def project(i, u):
                    pe.wait_ge(a_oT.sem, a_oT.at("oT", i))
                    pe.wait_ge(a_h.sem, a_h.at("carry", i + 7))
                    pe.wait_ge(v_y.sem, v_y.at("y", i - 1))
                    n = INNER // P
                    for k in range(n):
                        m = nc.tensor.matmul(hw_bank[:, 0:E], oT[:, u % 2, k, :], wo[:, k, :], start=k == 0,
                                             stop=k == n - 1)
                    m.then_inc(p_wo("wo"), 1)

                def turn_q(i, u):
                    pe.wait_ge(g_rot.sem, g_rot.at("q", i))
                    pe.wait_ge(a_turn.sem, a_turn.at("kbT", i - 1))
                    pe.wait_ge(a_oT.sem, a_oT.at("oT", i - 4))
                    for k in range(WH // 2):
                        m = nc.tensor.transpose(turn_bank[:, P * k:P * k + P], qr[:, u, P * k:P * k + P],
                                                c.ident[:, :])
                    m.then_inc(p_turn("qT"), 1)

                def turn_p(r):
                    name, bank = (("even", even), ("odd", odd))[r]

                    def f(i, u):
                        pe.wait_ge(a_exp.sem, a_exp.at(f"e{WH - 2 + r}", i))
                        for k in range(WH // 2):
                            m = nc.tensor.transpose(bank[:, P * k:P * k + P], pr[:, u % 2, 2 * k + r, :],
                                                    c.ident[:, :])
                        m.then_inc(p_pT(name), 1)
                    return f

                def turn_k(i, u):
                    pe.wait_ge(v_scale.sem, v_scale.at("k", i))
                    pe.wait_ge(a_turn.sem, a_turn.at("qT", i))
                    for k in range(WH // 2):
                        m = nc.tensor.transpose(turn_bank[:, P * k:P * k + P], kr[:, u, P * k:P * k + P],
                                                c.ident[:, :])
                    m.then_inc(p_turn("kT"), 1)

                def values(i, u):
                    pe.wait_ge(a_pT.sem, a_pT.at("odd", i))
                    pe.wait_ge(v_o.sem, v_o.at("o", i - 1))
                    pe.wait_ge(g_rot.sem, g_rot.at("vlo", i))
                    for h in range(WH):
                        p, d = pT[:, u % 2, h % 2, h // 2, :], slice(WD * h, WD * h + WD)
                        nc.tensor.matmul(o_bank[0:WIN, d], p[:, 0:WIN], vm[:, u, d], start=True, stop=True)
                        m = nc.tensor.matmul(o_bank[WIN:P, d], p[:, WIN:P], ks[:, u, d], start=True, stop=True)
                    m.then_inc(p_pv("o"), 1)

                def turn_h(i, u):
                    pe.wait_ge(g_stage.sem, g_stage.at("rows", i))
                    pe.wait_ge(v_y.sem, v_y.at("y", i - 8))
                    pe.wait_ge(a_h.sem, a_h.at("carry", i - 1))
                    nc.tensor.transpose(hw_bank[:, 0:P], rows[:, u, :], c.ident[:, :]).then_inc(p_h("hT"), 1)

                def scores(i, u):
                    pe.wait_ge(a_turn.sem, a_turn.at("kbT", i))
                    lo, hi = slice(0, WIN), slice(WIN, P)
                    n = WH // 2
                    for r, (name, bank) in enumerate((("even", even), ("odd", odd))):
                        pe.wait_ge(a_pT.sem, a_pT.at(name, i - 1))
                        heads_of = bank.rearrange("p (h k) -> p h k", k=P)
                        s = slice(WD * r, WD * r + WD)
                        nc.tensor.matmul(heads_of, identb[:, :], rows_bc(bias[:, (i % NT + NT - 1) // NT, :], n),
                                         start=True, stop=False, skip_group_check=True)
                        for h in range(n):
                            for part, k in ((lo, kbT), (hi, kT)):
                                m = nc.tensor.matmul(heads_of[part, h, :], qT[s, u % 2, h, part], k[s, u % 2, h, :],
                                                     start=False, stop=h == n - 1, skip_group_check=True)
                        m.then_inc(p_sim(name), 1)

                pipeline(pe, [(turn_q, 5), (values, 7), (turn_k, 5), (turn_p(0), 6), (turn_h, 1), (qkv, 2),
                              (turn_p(1), 6), (turn_o, 8), (scores, 5), (project, 8)])

    return prepare, load_layer, run


def gated_mlp(c, y, ctx):
    nc, inp, bk = c.nc, c.inp, c.bank
    sb = c.sb(ctx)
    w1 = sb("ml_w1", [P, 2 * HID])
    w2 = sb("ml_w2", [P, len(HCH), E])
    b1 = sb("ml_b1", [P, 2, len(HCH)])
    lng = sb("ml_ln", [P, 2])
    keep = sb("ml_keep", [P, TILES + 1])
    ring = lambda name, *shape: sb("ml_" + name, [P, RING, *shape])
    rows, hT, hn, hnT = ring("rows", E), ring("hT", P + 1), ring("hn", E), ring("hnT", P)
    st6, mv, rstd = ring("st6", 6), ring("mv", 2), ring("rstd", 1)
    gl, mT = ring("gelu", len(HCH), P), ring("mT", len(HCH), P)
    loaded = c.sem(ctx, "ml_loaded")
    st = lambda name, *names: c.steps(ctx, "ml_" + name, *names)
    g_stage = st("g_stage", "rows")
    p_h, a_h = st("p_h", "hT"), st("a_h", "lo", "hi", "carry")
    p_back = st("p_back", "h")
    v_ln = st("v_ln", "stats", "aggr", "eps")
    g_ln = st("g_ln", "pow")
    v_hn = st("v_hn", "hn")
    p_hn, a_hn = st("p_hn", "hnT"), st("a_hn", "hnT")
    p_up = st("p_up", "g", "a")
    a_gelu = st("a_gelu", "g0", "g1", "g2")
    v_mul = st("v_mul", "m0", "m1", "m2")
    p_down, v_y = st("p_down", "y"), st("v_y", "y")
    every = [g_stage, p_h, a_h, p_back, v_ln, g_ln, v_hn, p_hn, a_hn, p_up, a_gelu, v_mul, p_down, v_y]
    LAST, WL = len(HCH) - 1, HCH[-1][1]

    def prepare():
        with nc.Block() as block:

            @block.gpsimd
            def _(gp):
                prime(gp, every)
                nc.gpsimd.memset(hT[...], 0.0)
                nc.gpsimd.memset(mT[...], 1.0)

            @block.sync
            def _(sp):
                sp.dma_start(keep[...], inp["batch_keep"]).then_inc(loaded, 16)
                sp.wait_ge(loaded, 16)

    def load_layer(l):
        with nc.Block() as block:

            @block.sync
            def _(sp):
                li = bass.ds(l, 1)
                sp.dma_start(w1[:, :], inp["L0_ffn_w1"][li, :, :].rearrange("a e n -> (a e) n")).then_inc(loaded, 16)
                w2d = inp["L0_ffn_w2"][li, :, :].rearrange("a n e -> (a n) e")
                b1d = inp["L0_ffn_b1"][li, :].rearrange("a n -> n a")
                for k, (lo, w) in enumerate(HCH):
                    sp.dma_start(w2[0:w, k, :], w2d[lo:lo + w, :]).then_inc(loaded, 16)
                    for g in range(2):
                        sp.dma_start(b1[0:w, g, k:k + 1], b1d[g * HID + lo:g * HID + lo + w, :]).then_inc(loaded, 16)
                sp.dma_start(w2[WL:WL + 1, LAST, :], inp["L0_ffn_b2"][li, :]).then_inc(loaded, 16)
                sp.dma_start(lng[:, 0:1], inp["L0_ffn_ln_g"][li, :].rearrange("a n -> n a")).then_inc(loaded, 16)
                sp.dma_start(lng[:, 1:2], inp["L0_ffn_ln_b"][li, :].rearrange("a n -> n a")).then_inc(loaded, 16)
                sp.wait_ge(loaded, l * (16 * 13) + 16 * 14)
                sp.nop(nofuse=True)

    def run(l):
        for s in every:
            s.base = l * TILES
        h_bank, back_bank, hn_bank, g_bank, a_bank, y_bank = bk[0:6]
        with nc.Block() as block:

            @block.gpsimd
            def _(gp):

                def stage(i, u):
                    gp.wait_ge(p_h.sem, p_h.at("hT", i - RING))
                    gp.nop(nofuse=True)
                    nc.gpsimd.tensor_copy(rows[:, u, :], y[:, i, :]).then_inc(g_stage("rows"), 1)

                def inverse_std(i, u):
                    gp.wait_ge(v_ln.sem, v_ln.at("eps", i))
                    nc.gpsimd.tensor_tensor(rstd[:, u, :], mv[:, u, 1:2], c.minus_half[:, 0:1], ALU.pow)\
                      .then_inc(g_ln("pow"), 1)

                pipeline(gp, [(stage, 0), (inverse_std, 2)])

            @block.vector
            def _(dve):

                def statistics(i, u):
                    dve.wait_ge(p_back.sem, p_back.at("h", i))
                    nc.vector.bn_stats(st6[:, u, :], back_bank[:, 0:E]).then_inc(v_ln("stats"), 1)
                    dve.wait_ge(v_ln.sem, v_ln.at("stats", i))
                    dve.nop(nofuse=True)
                    nc.vector.bn_aggr(mv[:, u, :], st6[:, u, :]).then_inc(v_ln("aggr"), 1)
                    dve.wait_ge(v_ln.sem, v_ln.at("aggr", i))
                    nc.vector.tensor_scalar(mv[:, u, 1:2], mv[:, u, 1:2], LN_EPS, None, ALU.add)\
                      .then_inc(v_ln("eps"), 1)

                def normalize(i, u):
                    dve.wait_ge(g_ln.sem, g_ln.at("pow", i))
                    nc.vector.tensor_scalar(hn[:, u, :], back_bank[:, 0:E], mv[:, u, 0:1], rstd[:, u, :],
                                            ALU.subtract, ALU.mult).then_inc(v_hn("hn"), 1)

                def multiply(i, u):
                    dve.wait_ge(p_up.sem, p_up.at("a", i))
                    for k, (_, w) in enumerate(HCH):
                        dve.wait_ge(a_gelu.sem, a_gelu.at(f"g{k}", i))
                        nc.vector.scalar_tensor_tensor(out=mT[0:w, u, k, :], in0=a_bank[0:w, P * k:P * k + P],
                                                       scalar=b1[0:w, 0, k:k + 1], in1=gl[0:w, u, k, :],
                                                       op0=ALU.add, op1=ALU.mult).then_inc(v_mul(f"m{k}"), 1)

                def residual(i, u):
                    dve.wait_ge(p_down.sem, p_down.at("y", i))
                    nc.vector.tensor_tensor(y[:, i, :], y[:, i, :], y_bank[:, 0:E], ALU.add).then_inc(v_y("y"), 1)

                pipeline(dve, [(residual, 7), (normalize, 3), (multiply, 5), (statistics, 2)])

            @block.scalar
            def _(act):

                def h_columns(i, u):
                    h = E // 2
                    act.wait_ge(p_h.sem, p_h.at("hT", i))
                    nc.scalar.activation(hT[0:h, u, 0:P], h_bank[0:h, 0:P], ACT.Copy).then_inc(a_h("lo"), 1)
                    nc.scalar.activation(hT[h:P, u, 1:P + 1], h_bank[h:P, 0:P], ACT.Copy).then_inc(a_h("hi"), 1)
                    act.wait_ge(a_h.sem, a_h.at("hi", i - 1))
                    nc.scalar.activation(hT[h:P, u, 0:1], hT[h:P, (u - 1) % RING, P:P + 1], ACT.Copy,
                                         scale=keep[h:P, bass.ds(i, 1)]).then_inc(a_h("carry"), 1)

                def hn_columns(i, u):
                    act.wait_ge(p_hn.sem, p_hn.at("hnT", i))
                    nc.scalar.activation(hnT[:, u, :], hn_bank[:, 0:P], ACT.Identity, scale=lng[:, 0:1],
                                         bias=lng[:, 1:2]).then_inc(a_hn("hnT"), 1)

                def gelu(i, u):
                    act.wait_ge(p_up.sem, p_up.at("g", i))
                    for k, (_, w) in enumerate(HCH):
                        nc.scalar.activation(gl[0:w, u, k, :], g_bank[0:w, P * k:P * k + P], ACT.Gelu,
                                             bias=b1[0:w, 1, k:k + 1]).then_inc(a_gelu(f"g{k}"), 1)

                nc.scalar.preload_act_table_set("gelu_and_others")
                pipeline(act, [(gelu, 5), (hn_columns, 3), (h_columns, 1)])

            @block.tensor
            def _(pe):

                def turn_hn(i, u):
                    pe.wait_ge(v_hn.sem, v_hn.at("hn", i))
                    pe.wait_ge(a_hn.sem, a_hn.at("hnT", i - 1))
                    nc.tensor.transpose(hn_bank[:, 0:P], hn[:, u, :], c.ident[:, :]).then_inc(p_hn("hnT"), 1)

                def down(i, u):
                    pe.wait_ge(v_mul.sem, v_mul.at("m2", i))
                    pe.wait_ge(v_y.sem, v_y.at("y", i - 1))
                    for k, (_, w) in enumerate(HCH):
                        w += k == LAST
                        m = nc.tensor.matmul(y_bank[:, 0:E], mT[0:w, u, k, :], w2[0:w, k, :], start=k == 0,
                                             stop=k == LAST)
                    m.then_inc(p_down("y"), 1)

                def turn_back(i, u):
                    pe.wait_ge(a_h.sem, a_h.at("carry", i))
                    pe.wait_ge(v_hn.sem, v_hn.at("hn", i - 1))
                    nc.tensor.transpose(back_bank[:, 0:P], hT[:, u, 0:P], c.ident[:, :]).then_inc(p_back("h"), 1)

                def turn_h(i, u):
                    pe.wait_ge(g_stage.sem, g_stage.at("rows", i))
                    pe.wait_ge(a_h.sem, a_h.at("carry", i - 1))
                    nc.tensor.transpose(h_bank[:, 0:P], rows[:, u, :], c.ident[:, :]).then_inc(p_h("hT"), 1)

                def up(i, u):
                    pe.wait_ge(a_hn.sem, a_hn.at("hnT", i))
                    for name, bank, off in (("g", g_bank, HID), ("a", a_bank, 0)):
                        if name == "g":
                            pe.wait_ge(a_gelu.sem, a_gelu.at("g2", i - 1))
                        else:
                            pe.wait_ge(v_mul.sem, v_mul.at("m2", i - 1))
                        for k, (lo, w) in enumerate(HCH):
                            m = nc.tensor.matmul(bank[0:w, P * k:P * k + P], w1[:, off + lo:off + lo + w],
                                                 hnT[:, u, :], start=True, stop=True)
                        m.then_inc(p_up(name), 1)

                pipeline(pe, [(down, 6), (turn_hn, 3), (turn_back, 2), (turn_h, 1), (up, 4)])

    return prepare, load_layer, run


def causal_convolution(c):
    nc, inp, bk = c.nc, c.inp, c.bank
    PAIRS = B * CH
    with ExitStack() as ctx:
        sb = c.sb(ctx)
        w_in = sb("cv_w_in", [P, 3, E])
        waT, wvT, woT = sb("cv_waT", [P, CH]), sb("cv_wvT", [P, E]), sb("cv_woT", [P, E])
        wog, bog = sb("cv_wog", [P, B, E]), sb("cv_bog", [P, B, E])
        bo = sb("cv_bo", [P, E])
        flip = sb("cv_flip", [P, P])
        zs = sb("cv_z", [CH, B, T])
        zeros = sb("cv_zeros", [PAIRS, P])
        zmax, zneg, zsum, zrec = (sb(f"cv_{n}", [CH, B]) for n in ("zmax", "zneg", "zsum", "zrec"))
        vall, oall = sb("cv_v", [P, TILES, E]), sb("cv_o", [P, TILES, E])
        ring = lambda name, *shape: sb("cv_" + name, [P, RING, *shape])
        rows, hT, orow, oT = (ring(n, w) for n, w in (("rows", P), ("hT", 2 * P), ("orow", P), ("oT", P)))
        toep = ring("toep", T)
        zpad = nc.dram_tensor("cv_zpad", (PAIRS, P + T), F32).ap()

        loaded, turned, evac = c.sem(ctx, "cv_loaded"), c.sem(ctx, "cv_turned"), c.sem(ctx, "cv_evac")
        pre, vec, spread = c.sem(ctx, "cv_pre"), c.sem(ctx, "cv_vec"), c.sem(ctx, "cv_spread")
        expo = c.sem(ctx, "cv_exp")
        st = lambda name, *names: c.steps(ctx, "cv_" + name, *names)
        v_norm, g_norm = st("v_norm", "norm"), st("g_norm", "scaled", "shifted")
        p_h, a_h = st("p_h", "hT"), st("a_h", "hT")
        p_zv, a_zv = st("p_zv", "z", "v"), st("a_zv", "z", "v")
        p_conv, v_conv = st("p_conv", "o"), st("v_conv", "o")
        g_o, p_oT, a_oT, p_wo = st("g_o", "rows"), st("p_oT", "oT"), st("a_oT", "oT"), st("p_wo", "wo")
        v_x = st("v_x", "bias", "x")
        statistics, inverse = row_statistics(c, ctx, "cv")
        toep_in = [c.sem(ctx, f"cv_toep_in{u}") for u in range(RING)]

        with nc.Block() as block:

            @block.sync
            def _(sp):
                sp.dma_start(w_in[:, 0, :], inp["L1_attn_W_V"]).then_inc(loaded, 16)
                sp.dma_start(w_in[:, 1, :], inp["L1_attn_W_O"]).then_inc(loaded, 16)
                sp.dma_start(w_in[0:CH, 2, :], inp["L1_attn_W_A"]).then_inc(loaded, 16)
                sp.dma_start(bo[:, :], inp["L1_attn_b_O"].unsqueeze(0).broadcast_to([P, E])).then_inc(loaded, 16)
                sp.dma_start(flip[:, :], inp["flip"]).then_inc(loaded, 16)

            @block.gpsimd
            def _(gp):
                inverse(gp)
                prime(gp, [v_norm, g_norm, p_h, a_h, p_zv, a_zv, p_conv, v_conv, g_o, p_oT, a_oT, p_wo, v_x])
                nc.gpsimd.memset(zeros[:, :], 0.0)

            @block.tensor
            def _(pe):
                pe.wait_ge(loaded, 80)
                nc.tensor.transpose(bk[0][:, 0:P], w_in[:, 0, :], c.ident[:, :])
                nc.tensor.transpose(bk[0][:, P:2 * P], w_in[:, 1, :], c.ident[:, :])
                nc.tensor.transpose(bk[0][:, 2 * P:2 * P + CH], w_in[0:CH, 2, :], c.ident[0:CH, 0:CH])\
                  .then_inc(turned, 1)

            @block.vector
            def _(dve):
                statistics(dve)
                dve.wait_ge(turned, 1)
                nc.vector.tensor_copy(wvT[:, :], bk[0][:, 0:P]).then_inc(pre, 1)
                nc.vector.tensor_copy(woT[:, :], bk[0][:, P:2 * P]).then_inc(pre, 1)
                nc.vector.tensor_copy(waT[:, :], bk[0][:, 2 * P:2 * P + CH]).then_inc(pre, 1)
                dve.wait_ge(pre, 2)
                nc.vector.tensor_tensor(wog[...], rows_bc(woT[:, :], B), c.mod[:, 1, :, GA, :], ALU.mult)\
                  .then_inc(pre, 1)
                nc.vector.tensor_tensor(bog[...], rows_bc(bo[:, :], B), c.mod[:, 1, :, GA, :], ALU.mult)\
                  .then_inc(pre, 1)

        with nc.Block() as block:

            @block.vector
            def _(dve):

                def norm(i, u):
                    dve.wait_ge(p_h.sem, p_h.at("hT", i - RING))
                    normalize(c, v_norm, rows[:, u, :], i)

                pipeline(dve, [(norm, 0)])

            @block.gpsimd
            def _(gp):

                def shift(i, u):
                    gp.wait_ge(v_norm.sem, v_norm.at("norm", i))
                    modulate(c, nc.gpsimd, g_norm, rows[:, u, :], i, 1, SA, CA)

                pipeline(gp, [(shift, 0)])

            @block.tensor
            def _(pe):

                def turn_h(i, u):
                    pe.wait_ge(g_norm.sem, g_norm.at("shifted", i))
                    pe.wait_ge(a_h.sem, a_h.at("hT", i - 2))
                    nc.tensor.transpose(bk[u % 2][:, 0:P], rows[:, u, :], c.ident[:, :])
                    nc.tensor.matmul(bk[u % 2][:, P:2 * P], rows[:, u, :], flip[:, :], start=True, stop=True)\
                      .then_inc(p_h("hT"), 1)

                def project(i, u):
                    pe.wait_ge(a_h.sem, a_h.at("hT", i))
                    pe.wait_ge(a_zv.sem, a_zv.at("v", i - 2))
                    nc.tensor.matmul(bk[2 + u % 2][0:CH, 0:P], waT[:, :], hT[:, u, 0:P], start=True, stop=True)\
                      .then_inc(p_zv("z"), 1)
                    nc.tensor.matmul(bk[2 + u % 2][:, P:2 * P], hT[:, u, P:2 * P], wvT[:, :], start=True, stop=True)\
                      .then_inc(p_zv("v"), 1)

                pipeline(pe, [(turn_h, 0), (project, 1)])

            @block.scalar
            def _(act):

                def h_columns(i, u):
                    act.wait_ge(p_h.sem, p_h.at("hT", i))
                    nc.scalar.activation(hT[:, u, :], bk[u % 2][:, 0:2 * P], ACT.Copy).then_inc(a_h("hT"), 1)

                def outputs(i, u):
                    act.wait_ge(p_zv.sem, p_zv.at("v", i))
                    zflat = zs[:, :, :].rearrange("h b t -> h (b t)")
                    nc.scalar.activation(zflat[:, bass.ds(i * P, P)], bk[2 + u % 2][0:CH, 0:P], ACT.Copy,
                                         scale=float(CD ** -0.5)).then_inc(a_zv("z"), 1)
                    nc.scalar.activation(vall[:, i, :], bk[2 + u % 2][:, P:2 * P], ACT.Copy).then_inc(a_zv("v"), 1)

                pipeline(act, [(outputs, 1), (h_columns, 0)])

        with nc.Block() as block:

            @block.vector
            def _(dve):
                nc.vector.tensor_reduce(zmax[:, :], zs[...], AX_X, ALU.max).then_inc(vec, 1)
                dve.wait_ge(vec, 1)
                nc.vector.tensor_scalar(zneg[:, :], zmax[:, :], -1.0, None, ALU.mult).then_inc(vec, 1)
                dve.wait_ge(expo, B)
                nc.vector.reciprocal(zrec[:, :], zsum[:, :]).then_inc(vec, 1)
                dve.wait_ge(vec, 3)
                for b in range(B):
                    nc.vector.tensor_scalar(zs[:, b, :], zs[:, b, :], zrec[:, b:b + 1], None, ALU.mult)\
                      .then_inc(vec, 1)

            @block.scalar
            def _(act):
                act.wait_ge(vec, 2)
                for b in range(B):
                    nc.scalar.activation(zs[:, b, :], zs[:, b, :], ACT.Exp, bias=zneg[:, b:b + 1],
                                         accum_out=zsum[:, b:b + 1]).then_inc(expo, 1)

            @block.sync
            def _(sp):
                sp.dma_start(zpad[:, 0:P], zeros[:, :]).then_inc(spread, 16)
                for b in range(B):
                    sp.wait_ge(vec, 4 + b)
                    sp.dma_start(zpad[b * CH:b * CH + CH, P:P + T], zs[:, b, :]).then_inc(spread, 16)
                sp.wait_ge(spread, 16 * (B + 1))

        with nc.Block() as block:

            @block.sync
            def _(sp):

                def fetch(s, u):
                    sp.wait_ge(p_conv.sem, p_conv.at("o", s - RING))
                    row = bass.AP(tensor=zpad.tensor, offset=s * (P + T) + 1, ap=[[1, P], [1, T]])
                    sp.dma_start(toep[:, u, :], row).then_inc(toep_in[u], 16)

                pipeline(sp, [(fetch, 0)], n=PAIRS)
                sp.nop(nofuse=True)

            @block.tensor
            def _(pe):

                def convolve(s, u):
                    pe.wait_ge(toep_in[u], (s // RING) * 16 + 16)
                    pe.wait_ge(v_conv.sem, v_conv.at("o", s - 2))
                    b, h = s // CH, s % CH
                    for m in range(NT):
                        v = vall[:, bass.ds(b * NT, NT - m), bass.ds(h * CD, CD)]
                        mm = nc.tensor.matmul(bk[u % 2][:, CD * m:P].rearrange("p (n d) -> p n d", d=CD),
                                              toep[:, u, P * m:P * m + P], v, start=m == 0, stop=True,
                                              skip_group_check=True)
                    mm.then_inc(p_conv("o"), 1)

                pipeline(pe, [(convolve, 0)], n=PAIRS)

            @block.vector
            def _(dve):

                def keep(s, u):
                    dve.wait_ge(p_conv.sem, p_conv.at("o", s))
                    b, h = s // CH, s % CH
                    nc.vector.tensor_copy(oall[:, bass.ds(b * NT, NT), bass.ds(h * CD, CD)],
                                          bk[u % 2][:, 0:P].rearrange("p (n d) -> p n d", d=CD))\
                      .then_inc(v_conv("o"), 1)

                pipeline(dve, [(keep, 0)], n=PAIRS)

        with nc.Block() as block:

            @block.gpsimd
            def _(gp):

                def stage(i, u):
                    gp.wait_ge(p_oT.sem, p_oT.at("oT", i - RING))
                    gp.nop(nofuse=True)
                    nc.gpsimd.tensor_copy(orow[:, u, :], oall[:, i, :]).then_inc(g_o("rows"), 1)

                pipeline(gp, [(stage, 0)])

            @block.tensor
            def _(pe):

                def turn_o(i, u):
                    pe.wait_ge(g_o.sem, g_o.at("rows", i))
                    pe.wait_ge(a_oT.sem, a_oT.at("oT", i - 2))
                    nc.tensor.transpose(bk[u % 2][:, 0:P], orow[:, u, :], c.ident[:, :]).then_inc(p_oT("oT"), 1)

                def project(i, u):
                    pe.wait_ge(a_oT.sem, a_oT.at("oT", i))
                    pe.wait_ge(v_x.sem, v_x.at("x", i - 2))
                    nc.tensor.matmul(bk[2 + u % 2][:, 0:P], oT[:, u, :], wog[:, i // NT, :], start=True, stop=True)\
                      .then_inc(p_wo("wo"), 1)

                pipeline(pe, [(turn_o, 0), (project, 1)])

            @block.scalar
            def _(act):

                def o_columns(i, u):
                    act.wait_ge(p_oT.sem, p_oT.at("oT", i))
                    nc.scalar.activation(oT[:, u, :], bk[u % 2][:, 0:P], ACT.Copy).then_inc(a_oT("oT"), 1)

                pipeline(act, [(o_columns, 0)])

            @block.vector
            def _(dve):

                def residual(i, u):
                    x = c.x[:, i, :]
                    nc.vector.tensor_tensor(x, x, bog[:, i // NT, :], ALU.add).then_inc(v_x("bias"), 1)
                    dve.wait_ge(v_x.sem, v_x.at("bias", i))
                    dve.wait_ge(p_wo.sem, p_wo.at("wo", i))
                    nc.vector.tensor_tensor(x, x, bk[2 + u % 2][:, 0:P], ALU.add).then_inc(v_x("x"), 1)

                pipeline(dve, [(residual, 1)])


def experts(c, out_ap):
    nc, inp, bk = c.nc, c.inp, c.bank
    with ExitStack() as ctx:
        sb = c.sb(ctx)
        w_in = sb("ex_w_in", [P, NE, E])
        wT = sb("ex_wT", [P, NE * E])
        gate_in, gateT = sb("ex_gate_in", [NE, E]), sb("ex_gateT", [P, NE])
        b_in, b_rest = sb("ex_b_in", [NE, E]), sb("ex_b_rest", [NE, 2, E])
        b_parts = sb("ex_b_parts", [NE, 3, E], BF16)
        b_rows = sb("ex_b_rows", [3, NE, E], BF16)
        ones = sb("ex_ones", [3, P], BF16)
        iota = sb("ex_iota", [P, NE])
        ring = lambda name, *shape: sb("ex_" + name, [P, RING, *shape])
        rows, hT, total = ring("rows", P), ring("hT", P), ring("total", P)
        zmax, zneg, zsum, zrec = (ring(n, 1) for n in ("zmax", "zneg", "zsum", "zrec"))
        prob, top, topf, sel, w = ring("prob", NE), ring("top", 8), ring("topf", 8), ring("sel", NE), ring("w", NE)
        topi = ctx.enter_context(nc.sbuf_tensor("ex_topi", [P, RING, 8], U32))
        yw = sb("ex_yw", [P, 2, NE, E])

        loaded, turned, pre = c.sem(ctx, "ex_loaded"), c.sem(ctx, "ex_turned"), c.sem(ctx, "ex_pre")
        copied, moved, stored = c.sem(ctx, "ex_copied"), c.sem(ctx, "ex_moved"), c.sem(ctx, "ex_stored")
        st = lambda name, *names: c.steps(ctx, "ex_" + name, *names)
        v_norm, g_norm = st("v_norm", "norm"), st("g_norm", "scaled", "shifted")
        p_h, a_h = st("p_h", "hT"), st("a_h", "hT")
        p_gate = st("p_gate", "logits")
        v_max, a_exp = st("v_max", "max", "neg"), st("a_exp", "exp")
        v_top = st("v_top", "rec", "prob", "top", "idx", "float", "first", "both", "w")
        p_up = st("p_up", *[f"bank{k}" for k in range(4)])
        v_relu, a_relu = st("v_relu", "y0", "y1"), st("a_relu", *[f"e{e}" for e in range(NE // 2, NE)])
        v_out, g_out = st("v_out", "sum"), st("g_out", "gated", "x")
        every = [v_norm, p_h, a_h, p_gate, v_max, a_exp, v_top, p_up, v_relu, a_relu, v_out, g_norm,
                 g_out]
        statistics, inverse = row_statistics(c, ctx, "ex")

        with nc.Block() as block:

            @block.sync
            def _(sp):
                sp.dma_start(w_in[...], inp["L1_ffn_expert_w"].rearrange("e d h -> d e h")).then_inc(loaded, 16)
                sp.dma_start(gate_in[...], inp["L1_ffn_gate_w"]).then_inc(loaded, 16)
                sp.dma_start(b_in[...], inp["L1_ffn_expert_b"]).then_inc(loaded, 16)
                sp.dma_start(iota[...], inp["expert_numbers"]).then_inc(loaded, 16)
                sp.wait_ge(pre, 5)
                for k in range(3):
                    sp.dma_start(b_rows[k:k + 1, :, :], b_parts[:, k, :]).then_inc(moved, 16)
                sp.wait_ge(moved, 48)

            @block.gpsimd
            def _(gp):
                prime(gp, every)
                nc.gpsimd.memset(ones[...], 1.0)
                inverse(gp)

            @block.vector
            def _(dve):
                statistics(dve)
                dve.wait_ge(loaded, 64)
                src = b_in[...]
                for k in range(3):
                    nc.vector.tensor_copy(b_parts[:, k, :], src).then_inc(pre, 1)
                    if k < 2:
                        dve.wait_ge(pre, 2 * k + 1)
                        nc.vector.tensor_tensor(b_rest[:, k, :], src, b_parts[:, k, :], ALU.subtract)\
                          .then_inc(pre, 1)
                        src = b_rest[:, k, :]
                        dve.wait_ge(pre, 2 * k + 2)

            @block.tensor
            def _(pe):
                pe.wait_ge(loaded, 64)
                for e in range(NE):
                    m = nc.tensor.transpose(bk[e // 4][:, P * (e % 4):P * (e % 4) + P], w_in[:, e, :], c.ident[:, :])
                    if e % 4 == 3:
                        m.then_inc(turned, 1)
                nc.tensor.transpose(bk[4][:, 0:NE], gate_in[...], c.ident[0:NE, 0:NE]).then_inc(turned, 1)

            @block.scalar
            def _(act):
                for k in range(NE // 4):
                    act.wait_ge(turned, k + 1)
                    nc.scalar.activation(wT[:, BANK * k:BANK * k + BANK], bk[k], ACT.Copy).then_inc(copied, 1)
                act.wait_ge(turned, NE // 4 + 1)
                nc.scalar.activation(gateT[...], bk[4][:, 0:NE], ACT.Copy).then_inc(copied, 1)

        h_bank, gate_bank = bk[6], bk[7]
        with nc.Block() as block:

            @block.vector
            def _(dve):

                def norm(i, u):
                    dve.wait_ge(p_h.sem, p_h.at("hT", i - RING))
                    normalize(c, v_norm, rows[:, u, :], i)

                def gate_max(i, u):
                    dve.wait_ge(p_gate.sem, p_gate.at("logits", i))
                    nc.vector.tensor_reduce(zmax[:, u, :], gate_bank[:, 0:NE], AX_X, ALU.max)\
                      .then_inc(v_max("max"), 1)
                    dve.wait_ge(v_max.sem, v_max.at("max", i))
                    nc.vector.tensor_scalar(zneg[:, u, :], zmax[:, u, :], -1.0, None, ALU.mult)\
                      .then_inc(v_max("neg"), 1)

                def choose(i, u):
                    def after(name):
                        dve.wait_ge(v_top.sem, v_top.at(name, i))
                    dve.wait_ge(a_exp.sem, a_exp.at("exp", i))
                    nc.vector.reciprocal(zrec[:, u, :], zsum[:, u, :]).then_inc(v_top("rec"), 1)
                    after("rec")
                    nc.vector.tensor_scalar(prob[:, u, :], prob[:, u, :], zrec[:, u, :], None, ALU.mult)\
                      .then_inc(v_top("prob"), 1)
                    after("prob")
                    dve.nop(nofuse=True)
                    nc.vector.max(top[:, u, :], prob[:, u, :]).then_inc(v_top("top"), 1)
                    after("top")
                    dve.nop(nofuse=True)
                    nc.vector.max_index(topi[:, u, :], top[:, u, :], prob[:, u, :]).then_inc(v_top("idx"), 1)
                    after("idx")
                    nc.vector.tensor_copy(topf[:, u, :], topi[:, u, :]).then_inc(v_top("float"), 1)
                    after("float")
                    nc.vector.tensor_scalar(sel[:, u, :], iota[:, :], topf[:, u, 0:1], None, ALU.is_equal)\
                      .then_inc(v_top("first"), 1)
                    after("first")
                    nc.vector.scalar_tensor_tensor(out=sel[:, u, :], in0=iota[:, :], scalar=topf[:, u, 1:2],
                                                   in1=sel[:, u, :], op0=ALU.is_equal, op1=ALU.add)\
                      .then_inc(v_top("both"), 1)
                    after("both")
                    nc.vector.tensor_tensor(w[:, u, :], prob[:, u, :], sel[:, u, :], ALU.mult)\
                      .then_inc(v_top("w"), 1)

                def relu(i, u):
                    dve.wait_ge(v_top.sem, v_top.at("w", i))
                    dve.wait_ge(v_out.sem, v_out.at("sum", i - 2))
                    for k in range(2):
                        dve.wait_ge(p_up.sem, p_up.at(f"bank{k}", i))
                        nc.vector.scalar_tensor_tensor(
                            out=yw[:, u % 2, 4 * k:4 * k + 4, :], in0=bk[k].rearrange("p (e f) -> p e f", f=E),
                            scalar=0.0, in1=cols_bc(w[:, u, 4 * k:4 * k + 4], E), op0=ALU.max, op1=ALU.mult)\
                          .then_inc(v_relu(f"y{k}"), 1)

                def total_of(i, u):
                    dve.wait_ge(a_relu.sem, a_relu.at(f"e{NE - 1}", i))
                    dve.wait_ge(v_relu.sem, v_relu.at("y1", i))
                    dve.wait_ge(g_out.sem, g_out.at("x", i - RING))
                    nc.vector.tensor_reduce(total[:, u, :], yw[:, u % 2, :, :].rearrange("p e f -> p f e"), AX_X,
                                            ALU.add).then_inc(v_out("sum"), 1)

                pipeline(dve, [(relu, 4), (norm, 0), (choose, 3), (total_of, 5), (gate_max, 2)])

            @block.gpsimd
            def _(gp):

                def shift(i, u):
                    gp.wait_ge(v_norm.sem, v_norm.at("norm", i))
                    modulate(c, nc.gpsimd, g_norm, rows[:, u, :], i, 1, SB, CB)

                def residual(i, u):
                    gp.wait_ge(v_out.sem, v_out.at("sum", i))
                    nc.gpsimd.tensor_tensor(total[:, u, :], total[:, u, :], c.mod[:, 1, i // NT, GB, :], ALU.mult)\
                      .then_inc(g_out("gated"), 1)
                    gp.wait_ge(g_out.sem, g_out.at("gated", i))
                    nc.gpsimd.tensor_tensor(c.x[:, i, :], c.x[:, i, :], total[:, u, :], ALU.add)\
                      .then_inc(g_out("x"), 1)

                pipeline(gp, [(shift, 0), (residual, 5)])

            @block.tensor
            def _(pe):

                def turn_h(i, u):
                    pe.wait_ge(g_norm.sem, g_norm.at("shifted", i))
                    pe.wait_ge(a_h.sem, a_h.at("hT", i - 1))
                    nc.tensor.transpose(h_bank[:, 0:P], rows[:, u, :], c.ident[:, :]).then_inc(p_h("hT"), 1)

                def gate(i, u):
                    pe.wait_ge(a_h.sem, a_h.at("hT", i))
                    pe.wait_ge(a_exp.sem, a_exp.at("exp", i - 1))
                    nc.tensor.matmul(gate_bank[:, 0:NE], hT[:, u, :], gateT[:, :], start=True, stop=True)\
                      .then_inc(p_gate("logits"), 1)

                def up(i, u):
                    readers = [(v_relu, "y0"), (v_relu, "y1"), (a_relu, "e11"), (a_relu, "e15")]
                    for k, (reader, name) in enumerate(readers):
                        pe.wait_ge(reader.sem, reader.at(name, i - 1))
                        brow = b_rows[:, 4 * k:4 * k + 4, :].rearrange("p e f -> p (e f)")
                        nc.tensor.matmul(bk[k], ones[:, :], brow, start=True, stop=False)
                        nc.tensor.matmul(bk[k], hT[:, u, :], wT[:, BANK * k:BANK * k + BANK], start=False,
                                         stop=True).then_inc(p_up(f"bank{k}"), 1)

                pipeline(pe, [(turn_h, 1), (gate, 2), (up, 3)])

            @block.scalar
            def _(act):

                def h_columns(i, u):
                    act.wait_ge(p_h.sem, p_h.at("hT", i))
                    nc.scalar.activation(hT[:, u, :], h_bank[:, 0:P], ACT.Copy).then_inc(a_h("hT"), 1)

                def gate_exp(i, u):
                    act.wait_ge(v_max.sem, v_max.at("neg", i))
                    nc.scalar.activation(prob[:, u, :], gate_bank[:, 0:NE], ACT.Exp, bias=zneg[:, u, :],
                                         accum_out=zsum[:, u, :]).then_inc(a_exp("exp"), 1)

                def relu(i, u):
                    act.wait_ge(v_top.sem, v_top.at("w", i))
                    act.wait_ge(v_out.sem, v_out.at("sum", i - 2))
                    for e in range(NE // 2, NE):
                        act.wait_ge(p_up.sem, p_up.at(f"bank{e // 4}", i))
                        nc.scalar.activation(yw[:, u % 2, e, :], bk[e // 4][:, P * (e % 4):P * (e % 4) + P], ACT.Relu,
                                             scale=w[:, u, e:e + 1]).then_inc(a_relu(f"e{e}"), 1)

                nc.scalar.preload_act_table_set("natural_log_exp_and_others")
                pipeline(act, [(relu, 4), (h_columns, 1), (gate_exp, 2)])

            @block.sync
            def _(sp):

                def write(i, u):
                    sp.wait_ge(g_out.sem, g_out.at("x", i))
                    sp.dma_start(row_tiles(out_ap)[:, i, :], c.x[:, i, :]).then_inc(stored, 16)

                with sp.Fori(0, TILES) as i:
                    write(i, 0)
                sp.wait_ge(stored, 16 * TILES)
                sp.nop(nofuse=True)


def adaln_program(nc, inp, out):
    with ExitStack() as ctx:
        ctx.enter_context(nc.allow_non_contiguous_dma(reason="weight vectors as columns"))
        c = Core(nc, ctx, inp)
        setup(c)
        linear_attention(c)
        with ExitStack() as scope:
            y = c.sb(scope)("y_rows", [P, TILES, E])
            start_layers(c, y)
            attn_prepare, attn_load, attn_run = windowed_attention(c, y, scope)
            mlp_prepare, mlp_load, mlp_run = gated_mlp(c, y, scope)
            attn_prepare()
            mlp_prepare()
            with nc.Fori(0, DEPTH) as l:
                attn_load(l)
                attn_run(l)
                mlp_load(l)
                mlp_run(l)
            end_layers(c, y)
        causal_convolution(c)
        experts(c, out)


def shape_constants():
    s, t = np.arange(P)[:, None], np.arange(P)[None, :]
    masks = np.zeros((P, NLEV, P), np.uint32)
    masks[:, 0] = (s // (2 * HALVES[0]) == t // (2 * HALVES[0])) & (s <= t)
    for k in range(1, NLEV):
        h = HALVES[k]
        masks[:, k] = (s // (2 * h) == t // (2 * h)) & (s % (2 * h) < h) & (t % (2 * h) >= h)
    reset = np.zeros((P, TILES), np.float32)
    reset[:, ::NT] = -200.0
    keep = np.ones((P, TILES + 1), np.float32)
    keep[:, ::NT] = 0.0
    q, k = np.arange(WIN)[:, None], np.arange(WIN)[None, :]
    own, before, none = np.where(k <= q, 0.0, NEG), np.where(k >= q, 0.0, NEG), np.full((WIN, WIN), NEG)
    tile = np.block([[own, before], [before, own]])
    first = np.block([[own, none], [before, own]])
    bias = np.stack([first, tile], 1).astype(np.float32)
    f32 = np.float32
    half = np.arange(0, WD, 2, dtype=f32)
    t = np.arange(T, dtype=f32)
    freq = t[:, None] * (f32(1) / np.power(f32(10000), half / f32(WD)))[None, :]
    base = ((half + f32(0.4 * WD)) / f32(1.4 * WD)).astype(np.float64)
    scale = base[None, :] ** ((t - T // 2) / f32(WIN // 2))[:, None].astype(np.float64)
    cos, sin = np.cos(freq.astype(np.float64)), np.sin(freq.astype(np.float64))
    tabs = [np.concatenate(p, 1) for p in ((cos * scale, cos * scale), (-sin * scale, sin * scale),
                                           (cos / scale, cos / scale), (-sin / scale, sin / scale))]
    rot = np.stack(tabs).astype(f32).reshape(4, NT, P, WD).transpose(2, 0, 1, 3)
    eye = np.eye(P, dtype=f32)
    return {"ident": eye, "level_masks": masks, "batch_reset": reset,
            "batch_keep": keep, "window_bias": bias, "rotations": rot, "flip": np.ascontiguousarray(eye[::-1]),
            "expert_numbers": np.tile(np.arange(NE, dtype=f32), (P, 1))}


_INS = ["L0_attn_x", "L0_attn_Wq", "L0_attn_Wk", "L0_attn_Wv", "L0_attn_Wo", "L0_attn_delta", "L0_attn_G1",
        "L0_attn_G2", "L0_attn_norm_w", "L0_ffn_wqkv", "L0_ffn_q_scale", "L0_ffn_k_scale", "L0_ffn_wo",
        "L0_ffn_ln_g", "L0_ffn_ln_b", "L0_ffn_w1", "L0_ffn_b1", "L0_ffn_w2", "L0_ffn_b2", "L0_c", "L0_wmod",
        "L1_attn_W_A", "L1_attn_W_V", "L1_attn_W_O", "L1_attn_b_O", "L1_ffn_gate_w", "L1_ffn_expert_w",
        "L1_ffn_expert_b", "L1_c", "L1_wmod"]


def kernel(**inputs):
    import concourse.bacc as bacc
    from concourse.bass_utils import run_bass_kernel_spmd

    nc = bacc.Bacc("TRN2", target_bir_lowering=False, num_devices=1)
    arrays, aps = {}, {}
    for name, a in [(n, inputs[n]) for n in _INS] + list(shape_constants().items()):
        a = np.ascontiguousarray(a)
        arrays[f"in_{name}_dram"] = a
        aps[name] = nc.dram_tensor(f"in_{name}_dram", a.shape, mybir.dt.from_np(a.dtype), kind="ExternalInput").ap()
    out = nc.dram_tensor("out_0_dram", (B, T, E), F32, kind="ExternalOutput").ap()
    adaln_program(nc, aps, out)
    r = run_bass_kernel_spmd(nc, [arrays], core_ids=[0])
    return r.results[0]["out_0_dram"]
```

```python
from contextlib import ExitStack
from typing import Callable, NamedTuple

import concourse.bass as bass
import numpy as np
from concourse import mybir

F32 = mybir.dt.float32
BF16 = mybir.dt.bfloat16
U32 = mybir.dt.uint32
ALU = mybir.AluOpType
ACT = mybir.ActivationFunctionType
AX_X = mybir.AxisListType.X

P = 128
B, T, E = 2, 2048, 128
NT = T // P
TILES = B * NT
BANK = 512
LN_EPS = 1e-5
RING = 4
PRIMED = 8

GH, GD = 2, 64
HALVES = (4, 8, 16, 32, 64)
NLEV = len(HALVES)
MAX_EXP = float(np.exp(20.0))
MAX_SIG = 1e18

DEPTH, WH, WD, WIN = 2, 8, 64, 64
INNER = WH * WD
QK_SCALE = 8.0
NEG = -1e30
HID = int(E * 4 * 2 / 3)
HCH = [(0, 128), (128, 128), (256, HID - 256)]

CH, CD = 16, 8
NE = 16


class Steps:

    def __init__(self, sem, *names):
        self.sem, self.names, self.n = sem, names, 0
        self.base = 0

    def __call__(self, name):
        assert self.names[self.n % len(self.names)] == name, (self.names, self.n, name)
        self.n += 1
        return self.sem

    def at(self, name, i):
        if isinstance(i, int):
            i = min(i, TILES - 1)
        return (i + self.base + PRIMED) * len(self.names) + self.names.index(name) + 1


def prime(eng, steps):
    for s in steps:
        eng.sem_inc(s.sem, PRIMED * len(s.names))


def pipeline(eng, stages, n=TILES):
    lag = max(k for _, k in stages)
    start = -(-lag // RING) * RING
    for s in range(start):
        for f, k in stages:
            if 0 <= s - k:
                f(s - k, (s - k) % RING)
    with eng.Fori(0, (n - start) // RING) as j:
        for u in range(RING):
            for f, k in stages:
                f(j * RING + (start + u - k), (start + u - k) % RING)
    for s in range(n, n + lag):
        for f, k in stages:
            if s - k < n:
                f(s - k, (s - k) % RING)


def rows_bc(ap, n):
    return ap.unsqueeze(1).broadcast_to([ap.shape[0], n, ap.shape[1]])


def cols_bc(ap, w):
    return ap.unsqueeze(2).broadcast_to([ap.shape[0], ap.shape[1], w])


def row_tiles(ap):
    return ap.rearrange("b (n p) e -> p (b n) e", p=P)


class Core:

    def __init__(self, nc, ctx, inp):
        self.nc, self.ctx, self.inp = nc, ctx, inp
        self.psum = ctx.enter_context(nc.psum_tensor("psum", [P, 8, BANK], F32))
        self.bank = [self.psum[:, k, :] for k in range(8)]
        sb = self.sb(ctx)
        self.x = sb("x_rows", [P, TILES, E])
        self.ident = sb("ident", [P, P])
        self.mod = sb("mod", [P, 2, B, 6, E])
        self.mean = sb("mean", [P, TILES])
        self.rstd = sb("rstd", [P, TILES])
        self.minus_half = sb("minus_half", [P, TILES])

    def sb(self, ctx):
        return lambda name, shape, dt=F32: ctx.enter_context(self.nc.sbuf_tensor(name, shape, dt))

    def steps(self, ctx, name, *names):
        return Steps(ctx.enter_context(self.nc.semaphore(name)), *names)

    def sem(self, ctx, name):
        return ctx.enter_context(self.nc.semaphore(name))


SA, CA, GA, SB, CB, GB = range(6)


def setup(c, load_next):
    nc, inp = c.nc, c.inp
    with ExitStack() as ctx:
        sb = c.sb(ctx)
        cT = sb("cT", [P, 4])
        wmod = sb("wmod", [P, 2, 6 * E])
        ex = sb("ex", [P, 4])
        sig = sb("sig", [P, 4])
        silu = sb("silu", [P, 4])
        lhs = sb("silu_bc", [P, 4, P])
        sign = sb("sign", [P, 2, B, 2, E])
        loaded, x_loaded = c.sem(ctx, "setup_loaded"), c.sem(ctx, "setup_x_loaded")
        act_done = c.sem(ctx, "setup_act")
        vec = c.sem(ctx, "setup_vec")
        pe_done = c.sem(ctx, "setup_pe")
        statistics, inverse = row_statistics(c, ctx, "setup")
        LOADS = 5
        with nc.Block() as block:

            @block.sync
            def _(sp):
                for k, name in enumerate(("L0_c", "L1_c")):
                    sp.dma_start(cT[:, 2 * k:2 * k + 2], inp[name].rearrange("b e -> e b")).then_inc(loaded, 16)
                for k, name in enumerate(("L0_wmod", "L1_wmod")):
                    sp.dma_start(wmod[:, k, :], inp[name]).then_inc(loaded, 16)
                sp.dma_start(c.ident[:, :], inp["ident"]).then_inc(loaded, 16)
                sp.dma_start(c.x[:, :, :], row_tiles(inp["L0_attn_x"])).then_inc(x_loaded, 16)
                load_next(sp)
                sp.wait_ge(x_loaded, 16)

            @block.gpsimd
            def _(gp):
                inverse(gp)

            @block.scalar
            def _(act):
                act.wait_ge(loaded, 16 * LOADS)
                nc.scalar.activation(ex[:, :], cT[:, :], ACT.Exp, scale=-1.0).then_inc(act_done, 1)
                flat = c.mod[:, :, :, :, :].rearrange("p k b m e -> p (k b) (m e)")
                for r in range(4):
                    act.wait_ge(pe_done, r + 1)
                    for h, (lo, hi) in enumerate(((0, 512), (512, 768))):
                        nc.scalar.activation(flat[:, r, lo:hi], c.bank[2 * r + h][:, 0:hi - lo], ACT.Copy)\
                          .then_inc(act_done, 1)

            @block.vector
            def _(dve):
                nc.vector.memset(c.minus_half[:, :], -0.5).then_inc(vec, 1)
                dve.wait_ge(act_done, 1)
                nc.vector.tensor_scalar(ex[:, :], ex[:, :], 1.0, None, ALU.add).then_inc(vec, 1)
                dve.wait_ge(vec, 2)
                nc.vector.reciprocal(sig[:, :], ex[:, :]).then_inc(vec, 1)
                dve.wait_ge(vec, 3)
                nc.vector.tensor_tensor(silu[:, :], cT[:, :], sig[:, :], ALU.mult).then_inc(vec, 1)
                dve.wait_ge(vec, 4)
                nc.vector.tensor_copy(lhs[:, :, :], cols_bc(silu[:, :], P)).then_inc(vec, 1)
                dve.wait_ge(x_loaded, 16)
                statistics(dve)
                dve.wait_ge(act_done, 9)
                m = c.mod[:, :, :, :, :].rearrange("p k b (s m) e -> p (k b) s m e", s=2)
                for r in range(4):
                    nc.vector.tensor_scalar(m[:, r, :, 1, :], m[:, r, :, 1, :], 1.0, None, ALU.add).then_inc(vec, 1)
                    sg = sign[:, r // 2, r % 2, :, :]
                    nc.vector.tensor_scalar(sg, m[:, r, :, 2, :], 0.0, 2.0, ALU.is_ge, ALU.mult).then_inc(vec, 1)
                    mag = m[:, r, :, 2, :]
                    dve.wait_ge(vec, 5 + 5 * r + 2)
                    nc.vector.scalar_tensor_tensor(out=mag, in0=mag, scalar=-1.0, in1=mag, op0=ALU.mult,
                                                   op1=ALU.max).then_inc(vec, 1)
                    dve.wait_ge(vec, 5 + 5 * r + 3)
                    nc.vector.tensor_scalar(mag, mag, 0.25, None, ALU.max).then_inc(vec, 1)
                    dve.wait_ge(vec, 5 + 5 * r + 4)
                    nc.vector.scalar_tensor_tensor(out=m[:, r, :, 2, :], in0=sg, scalar=-1.0,
                                                   in1=m[:, r, :, 2, :], op0=ALU.add,
                                                   op1=ALU.mult).then_inc(vec, 1)
                dve.wait_ge(vec, 25)

            @block.tensor
            def _(pe):
                pe.wait_ge(vec, 5)
                for r in range(4):
                    nc.tensor.matmul(c.bank[2 * r][:, :], lhs[:, r, :], wmod[:, r // 2, 0:512], start=True, stop=True)
                    nc.tensor.matmul(c.bank[2 * r + 1][:, 0:256], lhs[:, r, :], wmod[:, r // 2, 512:768],
                                     start=True, stop=True).then_inc(pe_done, 1)


def row_statistics(c, ctx, tag):
    nc, sb = c.nc, c.sb(ctx)
    st = sb(f"{tag}_stats", [P, TILES, 6])
    tmp = sb(f"{tag}_stats_tmp", [P, 3, TILES])
    vec = c.sem(ctx, f"{tag}_stats_vec")
    pool = c.sem(ctx, f"{tag}_stats_pool")
    n, step = TILES, 8

    def on_vector(dve):
        with dve.Fori(0, n // step) as j:
            for u in range(step):
                i = j * step + u
                nc.vector.bn_stats(st[:, i, :], c.x[:, i, :]).then_inc(vec, 1)
        me, ve, mo, vo = (st[:, :, k] for k in (1, 2, 4, 5))
        s, d, v = (tmp[:, k, :] for k in range(3))
        dve.wait_ge(vec, n)
        nc.vector.tensor_tensor(s, me, mo, ALU.add).then_inc(vec, 1)
        nc.vector.tensor_tensor(d, me, mo, ALU.subtract).then_inc(vec, 1)
        nc.vector.tensor_tensor(v, ve, vo, ALU.add).then_inc(vec, 1)
        dve.wait_ge(vec, n + 3)
        nc.vector.tensor_scalar(c.mean[:, :], s, 0.5, None, ALU.mult).then_inc(vec, 1)
        nc.vector.tensor_tensor(d, d, d, ALU.mult).then_inc(vec, 1)
        dve.wait_ge(vec, n + 5)
        nc.vector.scalar_tensor_tensor(out=v, in0=d, scalar=E / 4.0, in1=v, op0=ALU.mult,
                                       op1=ALU.add).then_inc(vec, 1)
        dve.wait_ge(vec, n + 6)
        nc.vector.tensor_scalar(v, v, 1.0 / E, LN_EPS, ALU.mult, ALU.add).then_inc(vec, 1)

    def on_gpsimd(gp):
        gp.wait_ge(vec, n + 7)
        nc.gpsimd.tensor_tensor(c.rstd[:, :], tmp[:, 2, :], c.minus_half[:, :], ALU.pow).then_inc(pool, 1)
        gp.wait_ge(pool, 1)

    return on_vector, on_gpsimd


def normalize(c, st, rows, i):
    c.nc.vector.tensor_scalar(rows, c.x[:, i, :], c.mean[:, bass.ds(i, 1)], c.rstd[:, bass.ds(i, 1)],
                              ALU.subtract, ALU.mult).then_inc(st("norm"), 1)


def modulate(c, eng, st, rows, i, block, shift, scale):
    b = i // NT
    eng.tensor_tensor(rows, rows, c.mod[:, block, b, scale, :], ALU.mult).then_inc(st("scaled"), 1)
    eng.wait_ge(st.sem, st.at("scaled", i))
    eng.tensor_tensor(rows, rows, c.mod[:, block, b, shift, :], ALU.add).then_inc(st("shifted"), 1)


def linear_attention(c):
    nc, inp, bk = c.nc, c.inp, c.bank
    proj, small, tr, out = bk[0], bk[1], bk[6], bk[7]
    level = [c.psum[:, 2:4, P * k:P * k + P] for k in range(4)] + [c.psum[:, 4:6, 0:P]]
    level_step = ("l0123",) * 4 + ("l4",)
    with ExitStack() as ctx:
        sb = c.sb(ctx)
        wk, wq, wv, wo = (sb(f"la_{n}", [P, E]) for n in ("wk", "wq", "wv", "wo"))
        g1 = sb("la_g1", [P, GD])
        g2 = sb("la_g2", [GD, E])
        wog = sb("la_wog", [P, B, E])
        delta = sb("la_delta", [P, 2])
        norm_w = sb("la_norm_w", [P, 1])
        masks = sb("la_masks", [P, NLEV, P], U32)
        ones = sb("la_ones", [P, P])
        reset = sb("la_reset", [P, TILES])
        state = sb("la_state", [P, P])
        ring = lambda name, *shape: sb("la_" + name, [P, RING, *shape])
        rows, hT, v, g1T, y = (ring(n, P) for n in ("rows", "hT", "v", "g1T", "y"))
        ex = ring("ex", 2, P)
        ln = ring("ln", 2, P)
        sg = ring("sg", 2, P)
        kq = ring("kq", 2, P)
        cum = ring("cum", P)
        last = ring("last", 1)
        dist = ring("dist", NLEV, P)
        dec = ring("dec", NLEV + 1, P)
        qe, ke = ring("qe", NLEV, P), ring("ke", NLEV, P)
        dstart, dend = ring("dstart", P), ring("dend", P)
        qs, kend, kendT = ring("qs", P), ring("kend", P), ring("kendT", P)
        attn = ring("attn", GH, P)
        eg, lg, sgate = ring("eg", E), ring("lg", E), ring("sgate", E)
        og, osq, oT = ring("og", E), ring("osq", E), ring("oT", E)
        ms, rr = ring("ms", GH), ring("rr", GH)

        loaded, pre = c.sem(ctx, "la_loaded"), c.sem(ctx, "la_pre")
        st = lambda name, *names: c.steps(ctx, "la_" + name, *names)
        v_norm, g_norm = st("v_norm", "norm"), st("g_norm", "scaled", "shifted")
        p_h, a_h = st("p_h", "hT"), st("a_h", "hT")
        p_proj = st("p_proj", "z", "y", "v", "g1")
        a_proj = st("a_proj", "exz", "exy", "y", "v", "g1")
        v_clip = st("v_clip", "exz", "exy")
        a_sig = st("a_sig", "ln", "sg")
        v_kq = st("v_kq", "cum", "last", "k", "q")
        g_dist = st("g_dist", "d0", *[f"d{k}{side}" for k in range(1, NLEV) for side in ("left", "right")])
        a_dec = st("a_dec", "start", "end", "base", "inv", "levels")
        v_qk = st("v_qk", "qe", "ke")
        g_qk = st("g_qk", "qs", "kend")
        p_att = st("p_att", "l0123", "l4", "kendT", "gate")
        v_att = st("v_att", *[f"m{k}" for k in range(NLEV)], "clip")
        a_kend = st("a_kend", "kendT", "eg")
        a_gate = st("a_gate", "ln", "sg")
        p_out = st("p_out", "o", "state")
        v_state = st("v_state", "s0", "s1", "og")
        a_sq = st("a_sq", *[f"sq{h}" for h in range(GH)])
        v_ms = st("v_ms", "eps")
        g_rr = st("g_rr", "pow", "on")
        p_oT, a_oT = st("p_oT", "oT"), st("a_oT", "oT")
        p_wo, v_x = st("p_wo", "wo"), st("v_x", "x")
        every = [v_norm, g_norm, p_h, a_h, p_proj, a_proj, v_clip, a_sig, v_kq, g_dist, a_dec, v_qk, g_qk, p_att,
                 v_att, a_kend, a_gate, p_out, v_state, a_sq, v_ms, g_rr, p_oT, a_oT, p_wo, v_x]
        LOADS = 10

        def load(sp):
            for t, name in ((wk, "L0_attn_Wk"), (wq, "L0_attn_Wq"), (wv, "L0_attn_Wv"), (g1, "L0_attn_G1"),
                            (g2, "L0_attn_G2"), (wo, "L0_attn_Wo"), (masks, "level_masks")):
                sp.dma_start(t[...], inp[name]).then_inc(loaded, 16)
            sp.dma_start(delta[:, 1:2], inp["L0_attn_delta"].unsqueeze(1)).then_inc(loaded, 16)
            sp.dma_start(norm_w[:, :], inp["L0_attn_norm_w"].unsqueeze(1)).then_inc(loaded, 16)
            sp.dma_start(reset[:, :], inp["batch_reset"]).then_inc(loaded, 16)

        setup(c, load)
        with nc.Block() as block:

            @block.gpsimd
            def _(gp):
                prime(gp, every)
                nc.gpsimd.memset(attn[...], 0.0)
                nc.gpsimd.memset(ones[:, :], 1.0)
                nc.gpsimd.memset(state[:, :], 0.0)

            @block.vector
            def _(dve):
                dve.wait_ge(loaded, 16 * LOADS)
                nc.vector.tensor_scalar(delta[:, 0:1], delta[:, 1:2], -1.0, None, ALU.mult).then_inc(pre, 1)
                nc.vector.tensor_scalar(wo[:, :], wo[:, :], norm_w[:, 0:1], None, ALU.mult).then_inc(pre, 1)
                dve.wait_ge(pre, 2)
                nc.vector.tensor_tensor(wog[:, :, :], rows_bc(wo[:, :], B), c.mod[:, 0, :, GA, :],
                                        ALU.mult).then_inc(pre, 1)
                dve.wait_ge(pre, 3)

        with nc.Block() as block:

            @block.vector
            def _(dve):

                def norm(i, u):
                    dve.wait_ge(p_h.sem, p_h.at("hT", i - RING))
                    normalize(c, v_norm, rows[:, u, :], i)

                def clip(k, name, bound):
                    def f(i, u):
                        dve.wait_ge(a_proj.sem, a_proj.at(name, i))
                        nc.vector.tensor_scalar_min(ex[:, u, k, :], ex[:, u, k, :], bound).then_inc(v_clip(name), 1)
                    return f

                def running_sum(i, u):
                    dve.wait_ge(a_sig.sem, a_sig.at("ln", i))
                    nc.vector.tensor_tensor_scan(cum[:, u, :], ones[:, :], ln[:, u, 0, :], 0.0, ALU.mult, ALU.add)\
                      .then_inc(v_kq("cum"), 1)

                def keys(i, u):
                    dve.wait_ge(v_kq.sem, v_kq.at("cum", i))
                    nc.vector.tensor_scalar(last[:, u, :], cum[:, u, P - 1:P], -1.0, None, ALU.mult)\
                      .then_inc(v_kq("last"), 1)
                    dve.wait_ge(a_sig.sem, a_sig.at("sg", i))
                    nc.vector.tensor_tensor(kq[:, u, 0, :], ex[:, u, 0, :], sg[:, u, 0, :], ALU.mult)\
                      .then_inc(v_kq("k"), 1)
                    nc.vector.tensor_tensor(kq[:, u, 1, :], y[:, u, :], sg[:, u, 1, :], ALU.mult)\
                      .then_inc(v_kq("q"), 1)

                def scaled(i, u):
                    dve.wait_ge(a_dec.sem, a_dec.at("levels", i))
                    nc.vector.tensor_tensor(qe[:, u, :, :], dec[:, u, 0:NLEV, :], rows_bc(kq[:, u, 1, :], NLEV),
                                            ALU.mult).then_inc(v_qk("qe"), 1)
                    nc.vector.tensor_tensor(ke[:, u, :, :], dec[:, u, 1:NLEV + 1, :],
                                            rows_bc(kq[:, u, 0, :], NLEV), ALU.mult).then_inc(v_qk("ke"), 1)

                def levels(k):
                    def f(i, u):
                        dve.wait_ge(p_att.sem, p_att.at(level_step[k], i))
                        if k:
                            dve.wait_ge(v_att.sem, v_att.at(f"m{k - 1}", i))
                        dve.nop(nofuse=True)
                        nc.vector.copy_predicated(attn[:, u, :, :], rows_bc(masks[:, k, :], GH), level[k])\
                          .then_inc(v_att(f"m{k}"), 1)
                    return f

                def gate_clip(i, u):
                    dve.wait_ge(a_kend.sem, a_kend.at("eg", i))
                    nc.vector.tensor_scalar_min(eg[:, u, :], eg[:, u, :], MAX_SIG).then_inc(v_att("clip"), 1)

                def update(i, u):
                    dve.wait_ge(p_out.sem, p_out.at("state", i))
                    for h in range(GH):
                        s = slice(GD * h, GD * h + GD)
                        nc.vector.scalar_tensor_tensor(
                            out=state[s, s], in0=state[s, s], scalar=dstart[s, u, P - 1:P],
                            in1=out[s, E + GD * h:E + GD * h + GD], op0=ALU.mult, op1=ALU.add)\
                          .then_inc(v_state(f"s{h}"), 1)
                    dve.wait_ge(a_gate.sem, a_gate.at("sg", i))
                    nc.vector.tensor_tensor(og[:, u, :], out[:, 0:E], sgate[:, u, :], ALU.mult)\
                      .then_inc(v_state("og"), 1)

                def mean_square(i, u):
                    dve.wait_ge(a_sq.sem, a_sq.at(f"sq{GH - 1}", i))
                    nc.vector.tensor_scalar(ms[:, u, :], ms[:, u, :], 1.0 / GD, 1e-5, ALU.mult, ALU.add)\
                      .then_inc(v_ms("eps"), 1)

                def residual(i, u):
                    dve.wait_ge(p_wo.sem, p_wo.at("wo", i))
                    nc.vector.tensor_tensor(c.x[:, i, :], c.x[:, i, :], tr[:, 3 * P:4 * P], ALU.add)\
                      .then_inc(v_x("x"), 1)

                pipeline(dve, [(clip(0, "exz", MAX_EXP), 3), (levels(0), 6), (clip(1, "exy", MAX_SIG), 3),
                               (levels(1), 6), (norm, 0), (levels(2), 6), (running_sum, 3), (levels(3), 6),
                               (levels(4), 6), (gate_clip, 6), (keys, 3), (update, 6), (scaled, 4),
                               (residual, 7), (mean_square, 6)])

            @block.gpsimd
            def _(gp):

                def distances(i, u):
                    gp.wait_ge(v_kq.sem, v_kq.at("cum", i))
                    for k, h in enumerate(HALVES):
                        blocks, out = (t.rearrange("p (n w) -> p n w", w=2 * h)
                                       for t in (cum[:, u, :], dist[:, u, k, :]))
                        border = blocks[:, :, h - 1:h]
                        spread = lambda w: border.broadcast_to([P, P // (2 * h), w])
                        if k == 0:
                            nc.gpsimd.tensor_tensor(out, blocks, spread(2 * h), ALU.subtract)\
                              .then_inc(g_dist("d0"), 1)
                            continue
                        nc.gpsimd.tensor_tensor(out[:, :, 0:h], blocks[:, :, 0:h], spread(h), ALU.subtract)\
                          .then_inc(g_dist(f"d{k}left"), 1)
                        nc.gpsimd.tensor_tensor(out[:, :, h:], spread(h), blocks[:, :, h:], ALU.subtract)\
                          .then_inc(g_dist(f"d{k}right"), 1)

                def ends(i, u):
                    gp.wait_ge(v_kq.sem, v_kq.at("q", i))
                    gp.wait_ge(a_dec.sem, a_dec.at("end", i))
                    nc.gpsimd.tensor_tensor(qs[:, u, :], kq[:, u, 1, :], dstart[:, u, :], ALU.mult)\
                      .then_inc(g_qk("qs"), 1)
                    nc.gpsimd.tensor_tensor(kend[:, u, :], kq[:, u, 0, :], dend[:, u, :], ALU.mult)\
                      .then_inc(g_qk("kend"), 1)

                def inverse_rms(i, u):
                    gp.wait_ge(v_ms.sem, v_ms.at("eps", i))
                    nc.gpsimd.tensor_tensor(rr[:, u, :], ms[:, u, :], c.minus_half[:, 0:GH], ALU.pow)\
                      .then_inc(g_rr("pow"), 1)
                    gp.wait_ge(g_rr.sem, g_rr.at("pow", i))
                    o3 = og[:, u, :].rearrange("p (h d) -> p h d", h=GH)
                    nc.gpsimd.tensor_tensor(o3, o3, cols_bc(rr[:, u, :], GD), ALU.mult).then_inc(g_rr("on"), 1)

                def shift(i, u):
                    gp.wait_ge(v_norm.sem, v_norm.at("norm", i))
                    modulate(c, nc.gpsimd, g_norm, rows[:, u, :], i, 0, SA, CA)

                pipeline(gp, [(inverse_rms, 7), (ends, 4), (distances, 3), (shift, 0)])

            @block.scalar
            def _(act):

                def kend_rows(i, u):
                    act.wait_ge(p_att.sem, p_att.at("gate", i))
                    nc.scalar.activation(kendT[:, u, :], tr[:, 0:P], ACT.Copy).then_inc(a_kend("kendT"), 1)
                    nc.scalar.activation(eg[:, u, :], tr[:, 2 * P:3 * P], ACT.Exp, scale=-1.0)\
                      .then_inc(a_kend("eg"), 1)

                def square(i, u):
                    act.wait_ge(v_state.sem, v_state.at("og", i))
                    for h in range(GH):
                        s = slice(GD * h, GD * h + GD)
                        nc.scalar.activation(osq[:, u, s], og[:, u, s], ACT.Square,
                                             accum_out=ms[:, u, h:h + 1]).then_inc(a_sq(f"sq{h}"), 1)

                def o_columns(i, u):
                    act.wait_ge(p_oT.sem, p_oT.at("oT", i))
                    nc.scalar.activation(oT[:, u, :], tr[:, P:2 * P], ACT.Copy).then_inc(a_oT("oT"), 1)

                def decays(i, u):
                    act.wait_ge(v_kq.sem, v_kq.at("last", i))
                    nc.scalar.activation(dstart[:, u, :], cum[:, u, :], ACT.Exp, scale=-1.0,
                                         bias=reset[:, bass.ds(i, 1)]).then_inc(a_dec("start"), 1)
                    nc.scalar.activation(dend[:, u, :], cum[:, u, :], ACT.Exp, bias=last[:, u, :])\
                      .then_inc(a_dec("end"), 1)
                    act.wait_ge(g_dist.sem, g_dist.at("d0", i))
                    nc.scalar.activation(dec[:, u, 0, :], dist[:, u, 0, :], ACT.Exp, scale=-1.0)\
                      .then_inc(a_dec("base"), 1)
                    nc.scalar.activation(dec[:, u, NLEV, :], dist[:, u, 0, :], ACT.Exp).then_inc(a_dec("inv"), 1)
                    act.wait_ge(g_dist.sem, g_dist.at(f"d{NLEV - 1}right", i))
                    nc.scalar.activation(dec[:, u, 1:NLEV, :], dist[:, u, 1:NLEV, :], ACT.Exp)\
                      .then_inc(a_dec("levels"), 1)

                def projections(i, u):
                    act.wait_ge(p_proj.sem, p_proj.at("g1", i))
                    act.wait_ge(p_out.sem, p_out.at("state", i - 4))
                    nc.scalar.activation(ex[:, u, 0, :], proj[:, 0:P], ACT.Exp, bias=delta[:, 0:1], scale=-1.0)\
                      .then_inc(a_proj("exz"), 1)
                    nc.scalar.activation(ex[:, u, 1, :], proj[:, P:2 * P], ACT.Exp, scale=-1.0)\
                      .then_inc(a_proj("exy"), 1)
                    nc.scalar.activation(y[:, u, :], proj[:, P:2 * P], ACT.Copy).then_inc(a_proj("y"), 1)
                    nc.scalar.activation(v[:, u, :], proj[:, 2 * P:3 * P], ACT.Copy).then_inc(a_proj("v"), 1)
                    nc.scalar.activation(g1T[0:GD, u, :], proj[0:GD, 3 * P:4 * P], ACT.Copy)\
                      .then_inc(a_proj("g1"), 1)

                def sigmoids(i, u):
                    act.wait_ge(v_clip.sem, v_clip.at("exy", i))
                    nc.scalar.activation(ln[:, u, :, :], ex[:, u, :, :], ACT.Ln, bias=1.0).then_inc(a_sig("ln"), 1)
                    act.wait_ge(a_sig.sem, a_sig.at("ln", i))
                    nc.scalar.activation(sg[:, u, :, :], ln[:, u, :, :], ACT.Exp, scale=-1.0).then_inc(a_sig("sg"), 1)

                def gate(i, u):
                    act.wait_ge(v_att.sem, v_att.at("clip", i))
                    nc.scalar.activation(lg[:, u, :], eg[:, u, :], ACT.Ln, bias=1.0).then_inc(a_gate("ln"), 1)
                    act.wait_ge(a_gate.sem, a_gate.at("ln", i))
                    nc.scalar.activation(sgate[:, u, :], lg[:, u, :], ACT.Exp, scale=-1.0).then_inc(a_gate("sg"), 1)

                def h_columns(i, u):
                    act.wait_ge(p_h.sem, p_h.at("hT", i))
                    nc.scalar.activation(hT[:, u, :], small[:, 0:P], ACT.Copy).then_inc(a_h("hT"), 1)

                nc.scalar.preload_act_table_set("natural_log_exp_and_others")
                pipeline(act, [(sigmoids, 3), (kend_rows, 6), (decays, 4), (gate, 6), (o_columns, 7),
                               (h_columns, 1), (projections, 2), (square, 6)])

            @block.tensor
            def _(pe):

                def output(i, u):
                    pe.wait_ge(v_state.sem, v_state.at("og", i - 1))
                    pe.wait_ge(g_qk.sem, g_qk.at("qs", i))
                    nc.tensor.matmul(out[:, 0:E], qs[:, u, :], state[:, :], start=True, stop=True)
                    pe.wait_ge(v_att.sem, v_att.at(f"m{NLEV - 1}", i))
                    for h in range(GH):
                        m = nc.tensor.matmul(out[:, GD * h:GD * h + GD], attn[:, u, h, :],
                                             v[:, u, GD * h:GD * h + GD], start=False, stop=True,
                                             skip_group_check=True)
                    m.then_inc(p_out("o"), 1)
                    pe.wait_ge(a_kend.sem, a_kend.at("kendT", i))
                    nc.tensor.matmul(out[:, E:2 * E], kendT[:, u, :], v[:, u, :], start=True, stop=True)\
                      .then_inc(p_out("state"), 1)

                def scores(i, u):
                    pe.wait_ge(v_qk.sem, v_qk.at("ke", i))
                    for k in range(NLEV):
                        pe.wait_ge(v_att.sem, v_att.at("m3" if k < 4 else "m4", i - 1))
                        for h in range(GH):
                            s = slice(GD * h, GD * h + GD)
                            lv = (k + NLEV - 1) % NLEV
                            m = nc.tensor.matmul(level[k][:, h, :], ke[s, u, lv, :], qe[s, u, k, :],
                                                 start=True, stop=True)
                        if k >= 3:
                            m.then_inc(p_att(level_step[k]), 1)
                    pe.wait_ge(g_qk.sem, g_qk.at("kend", i))
                    pe.wait_ge(v_x.sem, v_x.at("x", i - 2))
                    pe.wait_ge(a_kend.sem, a_kend.at("eg", i - 1))
                    nc.tensor.transpose(tr[:, 0:P], kend[:, u, :], c.ident[:, :]).then_inc(p_att("kendT"), 1)
                    nc.tensor.matmul(tr[:, 2 * P:3 * P], g1T[0:GD, u, :], g2[:, :], start=True, stop=True)\
                      .then_inc(p_att("gate"), 1)

                def o_turn(i, u):
                    pe.wait_ge(a_kend.sem, a_kend.at("eg", i + 1))
                    pe.wait_ge(g_rr.sem, g_rr.at("on", i))
                    nc.tensor.transpose(tr[:, P:2 * P], og[:, u, :], c.ident[:, :]).then_inc(p_oT("oT"), 1)

                def project(i, u):
                    pe.wait_ge(a_h.sem, a_h.at("hT", i))
                    pe.wait_ge(a_proj.sem, a_proj.at("g1", i - 1))
                    nc.tensor.matmul(proj[:, 0:P], wk[:, :], hT[:, u, :], start=True, stop=True)\
                      .then_inc(p_proj("z"), 1)
                    nc.tensor.matmul(proj[:, P:2 * P], wq[:, :], hT[:, u, :], start=True, stop=True)\
                      .then_inc(p_proj("y"), 1)
                    nc.tensor.matmul(proj[:, 2 * P:3 * P], hT[:, u, :], wv[:, :], start=True, stop=True)\
                      .then_inc(p_proj("v"), 1)
                    nc.tensor.matmul(proj[0:GD, 3 * P:4 * P], g1[:, :], hT[:, u, :], start=True, stop=True)\
                      .then_inc(p_proj("g1"), 1)

                def o_project(i, u):
                    pe.wait_ge(a_oT.sem, a_oT.at("oT", i))
                    nc.tensor.matmul(tr[:, 3 * P:4 * P], oT[:, u, :], wog[:, i // NT, :], start=True, stop=True)\
                      .then_inc(p_wo("wo"), 1)

                def h_turn(i, u):
                    pe.wait_ge(g_norm.sem, g_norm.at("shifted", i))
                    pe.wait_ge(a_h.sem, a_h.at("hT", i - 1))
                    nc.tensor.transpose(small[:, 0:P], rows[:, u, :], c.ident[:, :]).then_inc(p_h("hT"), 1)

                pipeline(pe, [(project, 2), (h_turn, 1), (output, 6), (o_turn, 7), (o_project, 7), (scores, 5)])


def start_layers(c, y, phases):
    nc = c.nc
    with ExitStack() as ctx:
        normed = c.sem(ctx, "sl_normed")
        statistics, inverse = row_statistics(c, ctx, "sl")
        shifted = [c.sem(ctx, f"sl_shifted{b}") for b in range(B)]

        def modulate_batch(eng, b):
            t = y[:, b * NT:b * NT + NT, :]
            eng.tensor_tensor(t, t, rows_bc(c.mod[:, 0, b, CB, :], NT), ALU.mult).then_inc(shifted[b], 1)
            eng.wait_ge(shifted[b], 1)
            eng.tensor_tensor(t, t, rows_bc(c.mod[:, 0, b, SB, :], NT), ALU.add).then_inc(shifted[b], 1)
            eng.wait_ge(shifted[b], 2)

        with nc.Block() as block:

            @block.vector
            def _(dve):
                statistics(dve)

            @block.gpsimd
            def _(gp):
                inverse(gp)
                for phase in phases:
                    phase.prepare_gpsimd(gp)

            @block.sync
            def _(sp):
                for phase in phases:
                    phase.load_constants(sp)
                phases[0].load_layer(sp, 0)

        with nc.Block() as block:

            @block.vector
            def _(dve):
                for b in (1, 0):
                    with dve.Fori(0, NT // 8) as j:
                        for u in range(8):
                            i = j * 8 + (b * NT + u)
                            nc.vector.tensor_scalar(y[:, i, :], c.x[:, i, :], c.mean[:, bass.ds(i, 1)],
                                                    c.rstd[:, bass.ds(i, 1)], ALU.subtract, ALU.mult)\
                              .then_inc(normed, 1)
                dve.wait_ge(normed, TILES)
                modulate_batch(nc.vector, 0)
                for phase in phases:
                    phase.prepare_vector(dve)

            @block.gpsimd
            def _(gp):
                gp.wait_ge(normed, NT)
                modulate_batch(nc.gpsimd, 1)


def end_layers(c, y):
    nc = c.nc
    with ExitStack() as ctx:
        done = c.sem(ctx, "el_done")
        with nc.Block() as block:

            @block.vector
            def _(dve):
                for b in range(B):
                    t = slice(b * NT, b * NT + NT)
                    nc.vector.tensor_tensor(y[:, t, :], y[:, t, :], rows_bc(c.mod[:, 0, b, GB, :], NT), ALU.mult)\
                      .then_inc(done, 1)
                    dve.wait_ge(done, 2 * b + 1)
                    nc.vector.tensor_tensor(c.x[:, t, :], c.x[:, t, :], y[:, t, :], ALU.add).then_inc(done, 1)


class Phase(NamedTuple):
    prepare_gpsimd: Callable
    load_constants: Callable
    prepare_vector: Callable
    load_layer: Callable
    wait_layer: Callable
    run: Callable


def windowed_attention(c, y, ctx):
    nc, inp, bk = c.nc, c.inp, c.bank
    sb = c.sb(ctx)
    wqkv = sb("wa_wqkv", [P, 3 * INNER])
    wo = sb("wa_wo", [P, INNER // P, E])
    tabs = sb("wa_tabs", [P, 4, NT, WD])
    scales = sb("wa_scales", [P, 4, WD])
    bias32 = sb("wa_bias32", [P, 2, P])
    bias = sb("wa_bias", [P, 2, P], BF16)
    identb = sb("wa_identb", [P, P], BF16)
    keep = sb("wa_keep", [P, TILES + 1])
    ring = lambda name, *shape: sb("wa_" + name, [P, RING, *shape])
    rows, hT = ring("rows", E), ring("hT", P + 1)
    vs = ring("v", INNER)
    vm = ring("vm", INNER)
    pair = lambda name, *shape: sb("wa_" + name, [P, 2, *shape])
    sq = pair("sq", 2, INNER)
    ss, rn, rq = ring("ss", 2 * WH), ring("rn", 2 * WH), ring("rq", WH)
    qr, kr = ring("qr", INNER), ring("kr", INNER)
    tmp = pair("tmp", 2, INNER)
    qT, kT = pair("qT", WH // 2, P), pair("kT", WH // 2, P)
    kbT = pair("kbT", WH // 2, P)
    mx, nb, rs, rrs = (ring(n, WH) for n in ("mx", "nb", "rs", "rrs"))
    pr = pair("p", WH, P)
    pT = pair("pT", 2, WH // 2, P)
    ob, oT = pair("o", INNER), pair("oT", INNER // P, P)

    loaded, pre = c.sem(ctx, "wa_loaded"), c.sem(ctx, "wa_pre")
    st = lambda name, *names: c.steps(ctx, "wa_" + name, *names)
    g_stage = st("g_stage", "rows")
    p_h, a_h = st("p_h", "hT"), st("a_h", "lo", "hi", "carry")
    p_qkv = st("p_qkv", "q", "k", "v")
    a_sq = st("a_sq", "q", "k", "v")
    v_rot = st("v_rot", "q1", "q2", "q3", "k1", "k2", "k3")
    v_ss = st("v_ss", "sum", "clip")
    g_rot, v_vlo = st("g_rot", "q", "pow", "k", "vhi"), st("v_vlo", "vlo")
    v_scale = st("v_scale", "rq", "k")
    p_turn = st("p_turn", "qT", "kT")
    a_turn = st("a_turn", "qT", "kT", "kfT", "kbT")
    p_sim = st("p_sim", "even", "odd")
    v_max = st("v_max", "m0", "nb0", "m1", "nb1")
    a_exp = st("a_exp", *[f"e{h}" for h in (*range(0, WH, 2), *range(1, WH, 2))])
    p_pT, a_pT = st("p_pT", "even", "odd"), st("a_pT", "even", "odd")
    p_pv = st("p_pv", "o")
    v_o = st("v_o", "rrs", "o")
    p_oT, a_oT = st("p_oT", "oT"), st("a_oT", "oT")
    p_wo, v_y = st("p_wo", "wo"), st("v_y", "y")
    every = [v_vlo, g_stage, p_h, a_h, p_qkv, a_sq, v_rot, v_ss, g_rot, v_scale, p_turn, a_turn, p_sim, v_max, a_exp,
             p_pT, a_pT, p_pv, v_o, p_oT, a_oT, p_wo, v_y]

    def prepare_gpsimd(gp):
        prime(gp, every)
        nc.gpsimd.memset(kbT[...], 0.0)
        nc.gpsimd.memset(vm[...], 0.0)
        nc.gpsimd.memset(hT[...], 0.0)

    CONSTANTS, PER_LAYER = 2, 9

    def load_constants(sp):
        for t, name in ((bias32, "window_bias"), (keep, "batch_keep")):
            sp.dma_start(t[...], inp[name]).then_inc(loaded, 16)

    def prepare_vector(dve):
        nc.vector.tensor_copy(identb[:, :], c.ident[:, :]).then_inc(pre, 1)
        dve.wait_ge(loaded, 16 * (CONSTANTS + PER_LAYER))
        nc.vector.tensor_copy(bias[...], bias32[...]).then_inc(pre, 1)
        dve.wait_ge(pre, 2)

    def load_layer(sp, l):
        li = bass.ds(l, 1)
        sp.dma_start(tabs[...], inp["rotations"]).then_inc(loaded, 16)
        for k, name in enumerate(("L0_ffn_q_scale", "L0_ffn_k_scale")):
            row = inp[name][li, :]
            h = WD // 2
            for dst, lo in ((scales[:, 2 * k, :], 0), (scales[:, 2 * k + 1, 0:h], h),
                            (scales[:, 2 * k + 1, h:WD], 0)):
                w = dst.shape[1]
                sp.dma_start(dst, row[:, lo:lo + w].broadcast_to([P, w])).then_inc(loaded, 16)
        sp.dma_start(wqkv[:, :], inp["L0_ffn_wqkv"][li, :, :].rearrange("a e n -> (a e) n")).then_inc(loaded, 16)
        sp.dma_start(wo[...], inp["L0_ffn_wo"][li, :, :].rearrange("a (c p) e -> p (a c) e", p=P))\
          .then_inc(loaded, 16)

    def wait_layer(eng, l):
        eng.wait_ge(loaded, l * (16 * PER_LAYER) + 16 * (CONSTANTS + PER_LAYER))

    def run(l, meanwhile):
        for s in every:
            s.base = l * TILES
        q_bank, k_bank, v_bank, hw_bank, turn_bank, even, odd, o_bank = bk
        heads = lambda ap: ap.rearrange("p (h d) -> p h d", d=WD)
        with nc.Block() as block:

            @block.sync
            def _(sp):
                meanwhile(sp)

            @block.gpsimd
            def _(gp):

                def stage(i, u):
                    gp.wait_ge(g_rot.sem, g_rot.at("vhi", i - 5))
                    gp.wait_ge(p_h.sem, p_h.at("hT", i - RING))
                    gp.nop(nofuse=True)
                    nc.gpsimd.tensor_copy(rows[:, u, :], y[:, i, :]).then_inc(g_stage("rows"), 1)

                def rotate(i, u):
                    gp.wait_ge(g_rot.sem, g_rot.at("vhi", i - 1))
                    gp.wait_ge(v_rot.sem, v_rot.at("q3", i))
                    nc.gpsimd.tensor_tensor(qr[:, u, :], qr[:, u, :], tmp[:, u % 2, 0, :], ALU.add)\
                      .then_inc(g_rot("q"), 1)
                    gp.wait_ge(v_ss.sem, v_ss.at("clip", i))
                    nc.gpsimd.tensor_tensor(rn[:, u, :], ss[:, u, :], c.minus_half[:, 0:2 * WH], ALU.pow)\
                      .then_inc(g_rot("pow"), 1)
                    gp.wait_ge(v_rot.sem, v_rot.at("k3", i))
                    nc.gpsimd.tensor_tensor(kr[:, u, :], kr[:, u, :], tmp[:, u % 2, 1, :], ALU.add)\
                      .then_inc(g_rot("k"), 1)
                    gp.wait_ge(a_sq.sem, a_sq.at("v", i))
                    gp.wait_ge(g_rot.sem, g_rot.at("k", i))
                    gp.wait_ge(p_pv.sem, p_pv.at("o", i - 3))
                    gp.nop(nofuse=True)
                    nc.gpsimd.tensor_copy(vm[WIN:P, (u + 1) % RING, :], vs[WIN:P, u, :]).then_inc(g_rot("vhi"), 1)

                pipeline(gp, [(stage, 0), (rotate, 4)])

            @block.vector
            def _(dve):

                def rotate(i, u):
                    for k, (name, bank, dst) in enumerate((("q", q_bank, qr), ("k", k_bank, kr))):
                        src, out, cross = heads(bank), heads(dst[:, u, :]), heads(tmp[:, u % 2, k, :])
                        cos, sin = tabs[:, 2 * k, i % NT, :], tabs[:, 2 * k + 1, i % NT, :]
                        h = WD // 2
                        dve.wait_ge(a_sq.sem, a_sq.at(name, i))
                        nc.vector.tensor_tensor(out, src, rows_bc(cos, WH), ALU.mult).then_inc(v_rot(name + "1"), 1)
                        nc.vector.tensor_tensor(cross[:, :, 0:h], src[:, :, h:WD], rows_bc(sin[:, 0:h], WH),
                                                ALU.mult).then_inc(v_rot(name + "2"), 1)
                        nc.vector.tensor_tensor(cross[:, :, h:WD], src[:, :, 0:h], rows_bc(sin[:, h:WD], WH),
                                                ALU.mult).then_inc(v_rot(name + "3"), 1)

                def norms(i, u):
                    nc.vector.tensor_reduce(ss[:, u, :], sq[:, u % 2, :, :].rearrange("p a (h d) -> p (a h) d", d=WD),
                                            AX_X, ALU.add).then_inc(v_ss("sum"), 1)
                    dve.wait_ge(v_ss.sem, v_ss.at("sum", i))
                    nc.vector.tensor_scalar_max(ss[:, u, :], ss[:, u, :], 1e-24).then_inc(v_ss("clip"), 1)

                def first_values(i, u):
                    dve.wait_ge(a_sq.sem, a_sq.at("v", i))
                    dve.wait_ge(p_pv.sem, p_pv.at("o", i - 4))
                    nc.vector.tensor_copy(vm[0:WIN, u, :], vs[0:WIN, u, :]).then_inc(v_vlo("vlo"), 1)

                def scale(i, u):
                    dve.wait_ge(g_rot.sem, g_rot.at("pow", i))
                    nc.vector.tensor_scalar(rq[:, u, :], rn[:, u, 0:WH], QK_SCALE, None, ALU.mult)\
                      .then_inc(v_scale("rq"), 1)
                    dve.wait_ge(g_rot.sem, g_rot.at("k", i))
                    kh = heads(kr[:, u, :])
                    nc.vector.tensor_tensor(kh, kh, cols_bc(rn[:, u, WH:2 * WH], WD), ALU.mult)\
                      .then_inc(v_scale("k"), 1)

                def row_max(i, u):
                    m = mx[:, u, :].rearrange("p (h r) -> p r h", r=2)
                    by_parity = lambda t: t[:, u, :].rearrange("p (h r) -> p r h", r=2)
                    for r, (name, bank) in enumerate((("even", even), ("odd", odd))):
                        dve.wait_ge(p_sim.sem, p_sim.at(name, i))
                        nc.vector.tensor_reduce(m[:, r, :], bank.rearrange("p (h k) -> p h k", k=P), AX_X, ALU.max)\
                          .then_inc(v_max(f"m{r}"), 1)
                        dve.wait_ge(v_max.sem, v_max.at(f"m{r}", i))
                        nc.vector.scalar_tensor_tensor(out=by_parity(nb)[:, r, :], in0=m[:, r, :], scalar=-1.0,
                                                       in1=by_parity(rq)[:, r, :], op0=ALU.mult,
                                                       op1=ALU.mult).then_inc(v_max(f"nb{r}"), 1)

                def output(i, u):
                    dve.wait_ge(a_exp.sem, a_exp.at(f"e{WH - 1}", i))
                    nc.vector.reciprocal(rrs[:, u, :], rs[:, u, :]).then_inc(v_o("rrs"), 1)
                    dve.wait_ge(v_o.sem, v_o.at("rrs", i))
                    dve.wait_ge(p_pv.sem, p_pv.at("o", i))
                    nc.vector.tensor_tensor(heads(ob[:, u % 2, :]), heads(o_bank), cols_bc(rrs[:, u, :], WD), ALU.mult)\
                      .then_inc(v_o("o"), 1)

                def residual(i, u):
                    dve.wait_ge(p_wo.sem, p_wo.at("wo", i))
                    nc.vector.tensor_tensor(y[:, i, :], y[:, i, :], hw_bank[:, 0:E], ALU.add).then_inc(v_y("y"), 1)

                wait_layer(dve, l)
                for k in range(4):
                    nc.vector.tensor_tensor(tabs[:, k, :, :], tabs[:, k, :, :], rows_bc(scales[:, k, :], NT),
                                            ALU.mult).then_inc(pre, 1)
                dve.wait_ge(pre, 4 * l + 6)
                dve.nop(nofuse=True)
                pipeline(dve, [(scale, 5), (row_max, 6), (residual, 9), (first_values, 4), (rotate, 3),
                               (norms, 3), (output, 7)])

            @block.scalar
            def _(act):

                def o_columns(i, u):
                    act.wait_ge(p_oT.sem, p_oT.at("oT", i))
                    nc.scalar.activation(oT[:, u % 2, :, :].rearrange("p c t -> p (c t)"), turn_bank, ACT.Copy)\
                      .then_inc(a_oT("oT"), 1)

                def squares(i, u):
                    for k, (name, bank) in enumerate((("q", q_bank), ("k", k_bank))):
                        act.wait_ge(p_qkv.sem, p_qkv.at(name, i))
                        nc.scalar.activation(sq[:, u % 2, k, :], bank, ACT.Square).then_inc(a_sq(name), 1)

                def values(i, u):
                    act.wait_ge(p_qkv.sem, p_qkv.at("v", i))
                    act.wait_ge(p_pv.sem, p_pv.at("o", i - 4))
                    nc.scalar.activation(vs[:, u, :], v_bank, ACT.Copy).then_inc(a_sq("v"), 1)

                def turned(name, dst):
                    def f(i, u):
                        act.wait_ge(p_turn.sem, p_turn.at(name, i))
                        nc.scalar.activation(dst[:, u % 2, :, :].rearrange("p c t -> p (c t)"), turn_bank, ACT.Copy)\
                          .then_inc(a_turn(name), 1)
                        if name == "kT":
                            blocks = turn_bank.rearrange("p (c t) -> p c t", t=P)
                            nc.scalar.activation(kbT[:, u % 2, :, 0:WIN], blocks[:, :, 0:WIN], ACT.Copy)\
                              .then_inc(a_turn("kfT"), 1)
                            nc.scalar.activation(kbT[:, (u + 1) % 2, :, WIN:P], blocks[:, :, WIN:P], ACT.Copy,
                                                 scale=keep[:, bass.ds(i + 1, 1)]).then_inc(a_turn("kbT"), 1)
                    return f

                def p_columns(i, u):
                    for r, (name, bank) in enumerate((("even", even), ("odd", odd))):
                        act.wait_ge(p_pT.sem, p_pT.at(name, i))
                        nc.scalar.activation(pT[:, u % 2, r, :, :].rearrange("p c t -> p (c t)"), bank, ACT.Copy)\
                          .then_inc(a_pT(name), 1)

                def h_columns(i, u):
                    h = E // 2
                    act.wait_ge(p_h.sem, p_h.at("hT", i))
                    nc.scalar.activation(hT[0:h, u, 0:P], hw_bank[0:h, 0:P], ACT.Copy).then_inc(a_h("lo"), 1)
                    nc.scalar.activation(hT[h:P, u, 1:P + 1], hw_bank[h:P, 0:P], ACT.Copy).then_inc(a_h("hi"), 1)
                    act.wait_ge(a_h.sem, a_h.at("hi", i - 1))
                    nc.scalar.activation(hT[h:P, u, 0:1], hT[h:P, (u - 1) % RING, P:P + 1], ACT.Copy,
                                         scale=keep[h:P, bass.ds(i, 1)]).then_inc(a_h("carry"), 1)

                def exps(r):
                    def f(i, u):
                        act.wait_ge(v_max.sem, v_max.at(f"nb{r}", i))
                        for h in range(r, WH, 2):
                            k = h // 2
                            nc.scalar.activation(pr[:, u % 2, h, :], (even, odd)[r][:, P * k:P * k + P], ACT.Exp,
                                                 bias=nb[:, u, h:h + 1], scale=rq[:, u, h:h + 1],
                                                 accum_out=rs[:, u, h:h + 1]).then_inc(a_exp(f"e{h}"), 1)
                    return f

                nc.scalar.preload_act_table_set("natural_log_exp_and_others")
                pipeline(act, [(squares, 3), (exps(0), 6), (turned("qT", qT), 5), (exps(1), 6), (turned("kT", kT), 5),
                               (values, 3), (p_columns, 6), (o_columns, 8), (h_columns, 1)])

            @block.tensor
            def _(pe):

                def turn_o(i, u):
                    pe.wait_ge(v_o.sem, v_o.at("o", i))
                    pe.wait_ge(a_turn.sem, a_turn.at("kbT", i + 3))
                    for k in range(INNER // P):
                        m = nc.tensor.transpose(turn_bank[:, P * k:P * k + P], ob[:, u % 2, P * k:P * k + P],
                                                c.ident[:, :])
                    m.then_inc(p_oT("oT"), 1)

                def qkv(i, u):
                    pe.wait_ge(a_h.sem, a_h.at("carry", i))
                    for k, (name, bank) in enumerate((("q", q_bank), ("k", k_bank), ("v", v_bank))):
                        if name == "v":
                            pe.wait_ge(a_sq.sem, a_sq.at("v", i - 1))
                        else:
                            pe.wait_ge(v_rot.sem, v_rot.at(name + "3", i - 1))
                        nc.tensor.matmul(bank, hT[:, u, 0:P], wqkv[:, INNER * k:INNER * k + INNER], start=True,
                                         stop=True).then_inc(p_qkv(name), 1)

                def project(i, u):
                    pe.wait_ge(a_oT.sem, a_oT.at("oT", i))
                    pe.wait_ge(a_h.sem, a_h.at("carry", i + 7))
                    pe.wait_ge(v_y.sem, v_y.at("y", i - 1))
                    n = INNER // P
                    for k in range(n):
                        m = nc.tensor.matmul(hw_bank[:, 0:E], oT[:, u % 2, k, :], wo[:, k, :], start=k == 0,
                                             stop=k == n - 1)
                    m.then_inc(p_wo("wo"), 1)

                def turn_q(i, u):
                    pe.wait_ge(g_rot.sem, g_rot.at("q", i))
                    pe.wait_ge(a_turn.sem, a_turn.at("kbT", i - 1))
                    pe.wait_ge(a_oT.sem, a_oT.at("oT", i - 4))
                    for k in range(WH // 2):
                        m = nc.tensor.transpose(turn_bank[:, P * k:P * k + P], qr[:, u, P * k:P * k + P],
                                                c.ident[:, :])
                    m.then_inc(p_turn("qT"), 1)

                def turn_p(r):
                    name, bank = (("even", even), ("odd", odd))[r]

                    def f(i, u):
                        pe.wait_ge(a_exp.sem, a_exp.at(f"e{WH - 2 + r}", i))
                        for k in range(WH // 2):
                            m = nc.tensor.transpose(bank[:, P * k:P * k + P], pr[:, u % 2, 2 * k + r, :],
                                                    c.ident[:, :])
                        m.then_inc(p_pT(name), 1)
                    return f

                def turn_k(i, u):
                    pe.wait_ge(v_scale.sem, v_scale.at("k", i))
                    pe.wait_ge(a_turn.sem, a_turn.at("qT", i))
                    for k in range(WH // 2):
                        m = nc.tensor.transpose(turn_bank[:, P * k:P * k + P], kr[:, u, P * k:P * k + P],
                                                c.ident[:, :])
                    m.then_inc(p_turn("kT"), 1)

                def values(i, u):
                    pe.wait_ge(a_pT.sem, a_pT.at("odd", i))
                    pe.wait_ge(v_o.sem, v_o.at("o", i - 1))
                    pe.wait_ge(v_vlo.sem, v_vlo.at("vlo", i))
                    pe.wait_ge(g_rot.sem, g_rot.at("vhi", i - 1))
                    for h in range(WH):
                        p, d = pT[:, u % 2, h % 2, h // 2, :], slice(WD * h, WD * h + WD)
                        nc.tensor.matmul(o_bank[0:WIN, d], p[:, 0:WIN], vm[:, u, d], start=True, stop=True)
                        m = nc.tensor.matmul(o_bank[WIN:P, d], p[:, WIN:P], vs[:, u, d], start=True, stop=True)
                    m.then_inc(p_pv("o"), 1)

                def turn_h(i, u):
                    pe.wait_ge(g_stage.sem, g_stage.at("rows", i))
                    pe.wait_ge(v_y.sem, v_y.at("y", i - 8))
                    pe.wait_ge(a_h.sem, a_h.at("carry", i - 1))
                    nc.tensor.transpose(hw_bank[:, 0:P], rows[:, u, :], c.ident[:, :]).then_inc(p_h("hT"), 1)

                def scores(i, u):
                    pe.wait_ge(a_turn.sem, a_turn.at("kbT", i))
                    lo, hi = slice(0, WIN), slice(WIN, P)
                    n = WH // 2
                    for r, (name, bank) in enumerate((("even", even), ("odd", odd))):
                        pe.wait_ge(a_pT.sem, a_pT.at(name, i - 1))
                        heads_of = bank.rearrange("p (h k) -> p h k", k=P)
                        s = slice(WD * r, WD * r + WD)
                        nc.tensor.matmul(heads_of, identb[:, :], rows_bc(bias[:, (i % NT + NT - 1) // NT, :], n),
                                         start=True, stop=False, skip_group_check=True)
                        for h in range(n):
                            for part, k in ((lo, kbT), (hi, kT)):
                                m = nc.tensor.matmul(heads_of[part, h, :], qT[s, u % 2, h, part], k[s, u % 2, h, :],
                                                     start=False, stop=h == n - 1, skip_group_check=True)
                        m.then_inc(p_sim(name), 1)

                wait_layer(pe, l)
                pe.nop(nofuse=True)
                pipeline(pe, [(turn_q, 5), (values, 7), (turn_k, 5), (turn_p(0), 6), (turn_h, 1), (turn_p(1), 6),
                              (qkv, 2), (turn_o, 8), (scores, 5), (project, 8)])

    return Phase(prepare_gpsimd, load_constants, prepare_vector, load_layer, wait_layer, run)


def gated_mlp(c, y, ctx):
    nc, inp, bk = c.nc, c.inp, c.bank
    sb = c.sb(ctx)
    w1 = sb("ml_w1", [P, 2 * HID])
    w2 = sb("ml_w2", [P, len(HCH), E])
    b1 = sb("ml_b1", [P, 2, len(HCH)])
    lng = sb("ml_ln", [P, 2])
    keep = sb("ml_keep", [P, TILES + 1])
    ring = lambda name, *shape: sb("ml_" + name, [P, RING, *shape])
    rows, hT, hn, hnT = ring("rows", E), ring("hT", P + 1), ring("hn", E), ring("hnT", P)
    st6, mv, rstd = ring("st6", 6), ring("mv", 2), ring("rstd", 1)
    gl, mT = ring("gelu", len(HCH), P), ring("mT", len(HCH), P)
    loaded = c.sem(ctx, "ml_loaded")
    st = lambda name, *names: c.steps(ctx, "ml_" + name, *names)
    g_stage = st("g_stage", "rows")
    p_h, a_h = st("p_h", "hT"), st("a_h", "lo", "hi", "carry")
    p_back = st("p_back", "h")
    v_ln = st("v_ln", "stats", "aggr", "eps")
    g_ln = st("g_ln", "pow")
    v_hn = st("v_hn", "hn")
    p_hn, a_hn = st("p_hn", "hnT"), st("a_hn", "hnT")
    p_up = st("p_up", "g", "a")
    a_gelu = st("a_gelu", "g0", "g1", "g2")
    v_mul = st("v_mul", "m0", "m1", "m2")
    p_down, v_y = st("p_down", "y"), st("v_y", "y")
    every = [g_stage, p_h, a_h, p_back, v_ln, g_ln, v_hn, p_hn, a_hn, p_up, a_gelu, v_mul, p_down, v_y]
    LAST, WL = len(HCH) - 1, HCH[-1][1]

    def prepare_gpsimd(gp):
        prime(gp, every)
        nc.gpsimd.memset(hT[...], 0.0)
        nc.gpsimd.memset(mT[...], 1.0)

    CONSTANTS, PER_LAYER = 1, 4 + 3 * len(HCH)

    def load_constants(sp):
        sp.dma_start(keep[...], inp["batch_keep"]).then_inc(loaded, 16)

    def prepare_vector(dve):
        pass

    def load_layer(sp, l):
        li = bass.ds(l, 1)
        sp.dma_start(w1[:, :], inp["L0_ffn_w1"][li, :, :].rearrange("a e n -> (a e) n")).then_inc(loaded, 16)
        w2d = inp["L0_ffn_w2"][li, :, :].rearrange("a n e -> (a n) e")
        b1d = inp["L0_ffn_b1"][li, :].rearrange("a n -> n a")
        for k, (lo, w) in enumerate(HCH):
            sp.dma_start(w2[0:w, k, :], w2d[lo:lo + w, :]).then_inc(loaded, 16)
            for g in range(2):
                sp.dma_start(b1[0:w, g, k:k + 1], b1d[g * HID + lo:g * HID + lo + w, :]).then_inc(loaded, 16)
        sp.dma_start(w2[WL:WL + 1, LAST, :], inp["L0_ffn_b2"][li, :]).then_inc(loaded, 16)
        sp.dma_start(lng[:, 0:1], inp["L0_ffn_ln_g"][li, :].rearrange("a n -> n a")).then_inc(loaded, 16)
        sp.dma_start(lng[:, 1:2], inp["L0_ffn_ln_b"][li, :].rearrange("a n -> n a")).then_inc(loaded, 16)

    def wait_layer(eng, l):
        eng.wait_ge(loaded, l * (16 * PER_LAYER) + 16 * (CONSTANTS + PER_LAYER))
        eng.nop(nofuse=True)

    def run(l, meanwhile):
        for s in every:
            s.base = l * TILES
        h_bank, back_bank, hn_bank, g_bank, a_bank, y_bank = bk[0:6]
        with nc.Block() as block:

            @block.sync
            def _(sp):
                meanwhile(sp)

            @block.gpsimd
            def _(gp):

                def stage(i, u):
                    gp.wait_ge(p_h.sem, p_h.at("hT", i - RING))
                    gp.nop(nofuse=True)
                    nc.gpsimd.tensor_copy(rows[:, u, :], y[:, i, :]).then_inc(g_stage("rows"), 1)

                def inverse_std(i, u):
                    gp.wait_ge(v_ln.sem, v_ln.at("eps", i))
                    nc.gpsimd.tensor_tensor(rstd[:, u, :], mv[:, u, 1:2], c.minus_half[:, 0:1], ALU.pow)\
                      .then_inc(g_ln("pow"), 1)

                pipeline(gp, [(stage, 0), (inverse_std, 2)])

            @block.vector
            def _(dve):

                def statistics(i, u):
                    dve.wait_ge(p_back.sem, p_back.at("h", i))
                    nc.vector.bn_stats(st6[:, u, :], back_bank[:, 0:E]).then_inc(v_ln("stats"), 1)
                    dve.wait_ge(v_ln.sem, v_ln.at("stats", i))
                    dve.nop(nofuse=True)
                    nc.vector.bn_aggr(mv[:, u, :], st6[:, u, :]).then_inc(v_ln("aggr"), 1)
                    dve.wait_ge(v_ln.sem, v_ln.at("aggr", i))
                    nc.vector.tensor_scalar(mv[:, u, 1:2], mv[:, u, 1:2], LN_EPS, None, ALU.add)\
                      .then_inc(v_ln("eps"), 1)

                def normalize(i, u):
                    dve.wait_ge(g_ln.sem, g_ln.at("pow", i))
                    nc.vector.tensor_scalar(hn[:, u, :], back_bank[:, 0:E], mv[:, u, 0:1], rstd[:, u, :],
                                            ALU.subtract, ALU.mult).then_inc(v_hn("hn"), 1)

                def multiply(i, u):
                    dve.wait_ge(p_up.sem, p_up.at("a", i))
                    for k, (_, w) in enumerate(HCH):
                        dve.wait_ge(a_gelu.sem, a_gelu.at(f"g{k}", i))
                        nc.vector.scalar_tensor_tensor(out=mT[0:w, u, k, :], in0=a_bank[0:w, P * k:P * k + P],
                                                       scalar=b1[0:w, 0, k:k + 1], in1=gl[0:w, u, k, :],
                                                       op0=ALU.add, op1=ALU.mult).then_inc(v_mul(f"m{k}"), 1)

                def residual(i, u):
                    dve.wait_ge(p_down.sem, p_down.at("y", i))
                    nc.vector.tensor_tensor(y[:, i, :], y[:, i, :], y_bank[:, 0:E], ALU.add).then_inc(v_y("y"), 1)

                wait_layer(dve, l)
                pipeline(dve, [(residual, 7), (normalize, 3), (multiply, 5), (statistics, 2)])

            @block.scalar
            def _(act):

                def h_columns(i, u):
                    h = E // 2
                    act.wait_ge(p_h.sem, p_h.at("hT", i))
                    nc.scalar.activation(hT[0:h, u, 0:P], h_bank[0:h, 0:P], ACT.Copy).then_inc(a_h("lo"), 1)
                    nc.scalar.activation(hT[h:P, u, 1:P + 1], h_bank[h:P, 0:P], ACT.Copy).then_inc(a_h("hi"), 1)
                    act.wait_ge(a_h.sem, a_h.at("hi", i - 1))
                    nc.scalar.activation(hT[h:P, u, 0:1], hT[h:P, (u - 1) % RING, P:P + 1], ACT.Copy,
                                         scale=keep[h:P, bass.ds(i, 1)]).then_inc(a_h("carry"), 1)

                def hn_columns(i, u):
                    act.wait_ge(p_hn.sem, p_hn.at("hnT", i))
                    nc.scalar.activation(hnT[:, u, :], hn_bank[:, 0:P], ACT.Identity, scale=lng[:, 0:1],
                                         bias=lng[:, 1:2]).then_inc(a_hn("hnT"), 1)

                def gelu(i, u):
                    act.wait_ge(p_up.sem, p_up.at("g", i))
                    for k, (_, w) in enumerate(HCH):
                        nc.scalar.activation(gl[0:w, u, k, :], g_bank[0:w, P * k:P * k + P], ACT.Gelu,
                                             bias=b1[0:w, 1, k:k + 1]).then_inc(a_gelu(f"g{k}"), 1)

                nc.scalar.preload_act_table_set("gelu_and_others")
                wait_layer(act, l)
                pipeline(act, [(gelu, 5), (hn_columns, 3), (h_columns, 1)])

            @block.tensor
            def _(pe):

                def turn_hn(i, u):
                    pe.wait_ge(v_hn.sem, v_hn.at("hn", i))
                    pe.wait_ge(a_hn.sem, a_hn.at("hnT", i - 1))
                    nc.tensor.transpose(hn_bank[:, 0:P], hn[:, u, :], c.ident[:, :]).then_inc(p_hn("hnT"), 1)

                def down(i, u):
                    pe.wait_ge(v_mul.sem, v_mul.at("m2", i))
                    pe.wait_ge(v_y.sem, v_y.at("y", i - 1))
                    for k, (_, w) in enumerate(HCH):
                        w += k == LAST
                        m = nc.tensor.matmul(y_bank[:, 0:E], mT[0:w, u, k, :], w2[0:w, k, :], start=k == 0,
                                             stop=k == LAST)
                    m.then_inc(p_down("y"), 1)

                def turn_back(i, u):
                    pe.wait_ge(a_h.sem, a_h.at("carry", i))
                    pe.wait_ge(v_hn.sem, v_hn.at("hn", i - 1))
                    nc.tensor.transpose(back_bank[:, 0:P], hT[:, u, 0:P], c.ident[:, :]).then_inc(p_back("h"), 1)

                def turn_h(i, u):
                    pe.wait_ge(g_stage.sem, g_stage.at("rows", i))
                    pe.wait_ge(a_h.sem, a_h.at("carry", i - 1))
                    nc.tensor.transpose(h_bank[:, 0:P], rows[:, u, :], c.ident[:, :]).then_inc(p_h("hT"), 1)

                def up(i, u):
                    pe.wait_ge(a_hn.sem, a_hn.at("hnT", i))
                    for name, bank, off in (("g", g_bank, HID), ("a", a_bank, 0)):
                        if name == "g":
                            pe.wait_ge(a_gelu.sem, a_gelu.at("g2", i - 1))
                        else:
                            pe.wait_ge(v_mul.sem, v_mul.at("m2", i - 1))
                        for k, (lo, w) in enumerate(HCH):
                            m = nc.tensor.matmul(bank[0:w, P * k:P * k + P], w1[:, off + lo:off + lo + w],
                                                 hnT[:, u, :], start=True, stop=True)
                        m.then_inc(p_up(name), 1)

                wait_layer(pe, l)
                pipeline(pe, [(down, 6), (turn_hn, 3), (turn_back, 2), (turn_h, 1), (up, 4)])

    return Phase(prepare_gpsimd, load_constants, prepare_vector, load_layer, wait_layer, run)


def causal_convolution(c):
    nc, inp, bk = c.nc, c.inp, c.bank
    PAIRS = B * CH
    with ExitStack() as ctx:
        sb = c.sb(ctx)
        w_in = sb("cv_w_in", [P, 3, E])
        waT, wvT, woT = sb("cv_waT", [P, CH]), sb("cv_wvT", [P, E]), sb("cv_woT", [P, E])
        wog, bog = sb("cv_wog", [P, B, E]), sb("cv_bog", [P, B, E])
        bo = sb("cv_bo", [P, E])
        flip = sb("cv_flip", [P, P])
        zs = sb("cv_z", [CH, B, T])
        zeros = sb("cv_zeros", [PAIRS, P])
        zmax, zneg, zsum, zrec = (sb(f"cv_{n}", [CH, B]) for n in ("zmax", "zneg", "zsum", "zrec"))
        vall, oall = sb("cv_v", [P, B, 2, NT, E]), sb("cv_o", [P, TILES, E])
        ring = lambda name, *shape: sb("cv_" + name, [P, RING, *shape])
        rows, hT, orow, oT = (ring(n, w) for n, w in (("rows", P), ("hT", 2 * P), ("orow", P), ("oT", P)))
        toep = ring("toep", T)
        zpad = nc.dram_tensor("cv_zpad", (PAIRS, P + T), F32).ap()

        loaded, turned = c.sem(ctx, "cv_loaded"), c.sem(ctx, "cv_turned")
        pre, vec, spread = c.sem(ctx, "cv_pre"), c.sem(ctx, "cv_vec"), c.sem(ctx, "cv_spread")
        expo = c.sem(ctx, "cv_exp")
        st = lambda name, *names: c.steps(ctx, "cv_" + name, *names)
        v_norm, g_norm = st("v_norm", "norm"), st("g_norm", "scaled", "shifted")
        p_h, a_h = st("p_h", "hT"), st("a_h", "hT")
        p_zv, a_zv = st("p_zv", "z", "v"), st("a_zv", "z", "v")
        p_conv, v_conv = st("p_conv", "o"), st("v_conv", "o")
        g_o, p_oT, a_oT, p_wo = st("g_o", "rows"), st("p_oT", "oT"), st("a_oT", "oT"), st("p_wo", "wo")
        v_x = st("v_x", "bias", "x")
        statistics, inverse = row_statistics(c, ctx, "cv")
        toep_in = [c.sem(ctx, f"cv_toep_in{u}") for u in range(RING)]

        with nc.Block() as block:

            @block.sync
            def _(sp):
                sp.dma_start(w_in[:, 0, :], inp["L1_attn_W_V"]).then_inc(loaded, 16)
                sp.dma_start(w_in[:, 1, :], inp["L1_attn_W_O"]).then_inc(loaded, 16)
                sp.dma_start(w_in[0:CH, 2, :], inp["L1_attn_W_A"]).then_inc(loaded, 16)
                sp.dma_start(bo[:, :], inp["L1_attn_b_O"].unsqueeze(0).broadcast_to([P, E])).then_inc(loaded, 16)
                sp.dma_start(flip[:, :], inp["flip"]).then_inc(loaded, 16)

            @block.gpsimd
            def _(gp):
                inverse(gp)
                prime(gp, [v_norm, g_norm, p_h, a_h, p_zv, a_zv, p_conv, v_conv, g_o, p_oT, a_oT, p_wo, v_x])
                nc.gpsimd.memset(zeros[:, :], 0.0)
                nc.gpsimd.memset(vall[:, :, 0, :, :], 0.0)

            @block.tensor
            def _(pe):
                pe.wait_ge(loaded, 80)
                nc.tensor.transpose(bk[0][:, 0:P], w_in[:, 0, :], c.ident[:, :])
                nc.tensor.transpose(bk[0][:, P:2 * P], w_in[:, 1, :], c.ident[:, :])
                nc.tensor.transpose(bk[0][:, 2 * P:2 * P + CH], w_in[0:CH, 2, :], c.ident[0:CH, 0:CH])\
                  .then_inc(turned, 1)

            @block.vector
            def _(dve):
                statistics(dve)
                dve.wait_ge(turned, 1)
                nc.vector.tensor_copy(wvT[:, :], bk[0][:, 0:P]).then_inc(pre, 1)
                nc.vector.tensor_copy(woT[:, :], bk[0][:, P:2 * P]).then_inc(pre, 1)
                nc.vector.tensor_copy(waT[:, :], bk[0][:, 2 * P:2 * P + CH]).then_inc(pre, 1)
                dve.wait_ge(pre, 2)
                nc.vector.tensor_tensor(wog[...], rows_bc(woT[:, :], B), c.mod[:, 1, :, GA, :], ALU.mult)\
                  .then_inc(pre, 1)
                nc.vector.tensor_tensor(bog[...], rows_bc(bo[:, :], B), c.mod[:, 1, :, GA, :], ALU.mult)\
                  .then_inc(pre, 1)

        with nc.Block() as block:

            @block.vector
            def _(dve):

                def norm(i, u):
                    dve.wait_ge(p_h.sem, p_h.at("hT", i - RING))
                    normalize(c, v_norm, rows[:, u, :], i)

                pipeline(dve, [(norm, 0)])

            @block.gpsimd
            def _(gp):

                def shift(i, u):
                    gp.wait_ge(v_norm.sem, v_norm.at("norm", i))
                    modulate(c, nc.gpsimd, g_norm, rows[:, u, :], i, 1, SA, CA)

                pipeline(gp, [(shift, 0)])

            @block.tensor
            def _(pe):

                def turn_h(i, u):
                    pe.wait_ge(g_norm.sem, g_norm.at("shifted", i))
                    pe.wait_ge(a_h.sem, a_h.at("hT", i - 2))
                    nc.tensor.transpose(bk[u % 2][:, 0:P], rows[:, u, :], c.ident[:, :])
                    nc.tensor.matmul(bk[u % 2][:, P:2 * P], rows[:, u, :], flip[:, :], start=True, stop=True)\
                      .then_inc(p_h("hT"), 1)

                def project(i, u):
                    pe.wait_ge(a_h.sem, a_h.at("hT", i))
                    pe.wait_ge(a_zv.sem, a_zv.at("v", i - 2))
                    nc.tensor.matmul(bk[2 + u % 2][0:CH, 0:P], waT[:, :], hT[:, u, 0:P], start=True, stop=True)\
                      .then_inc(p_zv("z"), 1)
                    nc.tensor.matmul(bk[2 + u % 2][:, P:2 * P], hT[:, u, P:2 * P], wvT[:, :], start=True, stop=True)\
                      .then_inc(p_zv("v"), 1)

                pipeline(pe, [(turn_h, 0), (project, 1)])

            @block.scalar
            def _(act):

                def h_columns(i, u):
                    act.wait_ge(p_h.sem, p_h.at("hT", i))
                    nc.scalar.activation(hT[:, u, :], bk[u % 2][:, 0:2 * P], ACT.Copy).then_inc(a_h("hT"), 1)

                def outputs(i, u):
                    act.wait_ge(p_zv.sem, p_zv.at("v", i))
                    zflat = zs[:, :, :].rearrange("h b t -> h (b t)")
                    nc.scalar.activation(zflat[:, bass.ds(i * P, P)], bk[2 + u % 2][0:CH, 0:P], ACT.Copy,
                                         scale=float(CD ** -0.5)).then_inc(a_zv("z"), 1)
                    vflat = vall[...].rearrange("p b s n e -> p (b s n) e")
                    nc.scalar.activation(vflat[:, i + (i // NT + 1) * NT, :], bk[2 + u % 2][:, P:2 * P], ACT.Copy)\
                      .then_inc(a_zv("v"), 1)

                pipeline(act, [(outputs, 1), (h_columns, 0)])

        with nc.Block() as block:

            @block.scalar
            def _(act):
                for b in range(B):
                    act.wait_ge(vec, 2 * b + 2)
                    nc.scalar.activation(zs[:, b, :], zs[:, b, :], ACT.Exp, bias=zneg[:, b:b + 1],
                                         accum_out=zsum[:, b:b + 1]).then_inc(expo, 1)

            @block.sync
            def _(sp):

                def fetch(s, u):
                    sp.wait_ge(p_conv.sem, p_conv.at("o", s - RING))
                    row = bass.AP(tensor=zpad.tensor, offset=s * (P + T) + 1, ap=[[1, P], [1, T]])
                    sp.dma_start(toep[:, u, :], row).then_inc(toep_in[u], 16)

                sp.dma_start(zpad[:, 0:P], zeros[:, :]).then_inc(spread, 16)
                for b in range(B):
                    sp.wait_ge(vec, 2 * B + 2 * b + 2)
                    sp.dma_start(zpad[b * CH:b * CH + CH, P:P + T], zs[:, b, :]).then_inc(spread, 16)
                sp.wait_ge(spread, 16 * (B + 1))
                pipeline(sp, [(fetch, 0)], n=PAIRS)
                sp.nop(nofuse=True)

            @block.tensor
            def _(pe):

                def convolve(s, u):
                    pe.wait_ge(toep_in[u], (s // RING) * 16 + 16)
                    pe.wait_ge(v_conv.sem, v_conv.at("o", s - 2))
                    b, h = s // CH, s % CH
                    vflat = vall[...].rearrange("p b s n e -> p (b s n) e")
                    for m in range(NT):
                        v = vflat[:, bass.ds(b * (2 * NT) + (NT - m), NT), bass.ds(h * CD, CD)]
                        mm = nc.tensor.matmul(bk[u % 2][:, 0:P].rearrange("p (n d) -> p n d", d=CD),
                                              toep[:, u, P * m:P * m + P], v, start=m == 0, stop=m == NT - 1)
                    mm.then_inc(p_conv("o"), 1)

                pipeline(pe, [(convolve, 0)], n=PAIRS)

            @block.vector
            def _(dve):

                def keep(s, u):
                    dve.wait_ge(p_conv.sem, p_conv.at("o", s))
                    b, h = s // CH, s % CH
                    nc.vector.tensor_copy(oall[:, bass.ds(b * NT, NT), bass.ds(h * CD, CD)],
                                          bk[u % 2][:, 0:P].rearrange("p (n d) -> p n d", d=CD))\
                      .then_inc(v_conv("o"), 1)

                for b in range(B):
                    nc.vector.tensor_reduce(zmax[:, b:b + 1], zs[:, b, :], AX_X, ALU.max).then_inc(vec, 1)
                    dve.wait_ge(vec, 2 * b + 1)
                    nc.vector.tensor_scalar(zneg[:, b:b + 1], zmax[:, b:b + 1], -1.0, None, ALU.mult)\
                      .then_inc(vec, 1)
                for b in range(B):
                    dve.wait_ge(expo, b + 1)
                    nc.vector.reciprocal(zrec[:, b:b + 1], zsum[:, b:b + 1]).then_inc(vec, 1)
                    dve.wait_ge(vec, 2 * B + 2 * b + 1)
                    nc.vector.tensor_scalar(zs[:, b, :], zs[:, b, :], zrec[:, b:b + 1], None, ALU.mult)\
                      .then_inc(vec, 1)
                pipeline(dve, [(keep, 0)], n=PAIRS)

        with nc.Block() as block:

            @block.gpsimd
            def _(gp):

                def stage(i, u):
                    gp.wait_ge(p_oT.sem, p_oT.at("oT", i - RING))
                    gp.nop(nofuse=True)
                    nc.gpsimd.tensor_copy(orow[:, u, :], oall[:, i, :]).then_inc(g_o("rows"), 1)

                pipeline(gp, [(stage, 0)])

            @block.tensor
            def _(pe):

                def turn_o(i, u):
                    pe.wait_ge(g_o.sem, g_o.at("rows", i))
                    pe.wait_ge(a_oT.sem, a_oT.at("oT", i - 2))
                    nc.tensor.transpose(bk[u % 2][:, 0:P], orow[:, u, :], c.ident[:, :]).then_inc(p_oT("oT"), 1)

                def project(i, u):
                    pe.wait_ge(a_oT.sem, a_oT.at("oT", i))
                    pe.wait_ge(v_x.sem, v_x.at("x", i - 2))
                    nc.tensor.matmul(bk[2 + u % 2][:, 0:P], oT[:, u, :], wog[:, i // NT, :], start=True, stop=True)\
                      .then_inc(p_wo("wo"), 1)

                pipeline(pe, [(turn_o, 0), (project, 1)])

            @block.scalar
            def _(act):

                def o_columns(i, u):
                    act.wait_ge(p_oT.sem, p_oT.at("oT", i))
                    nc.scalar.activation(oT[:, u, :], bk[u % 2][:, 0:P], ACT.Copy).then_inc(a_oT("oT"), 1)

                pipeline(act, [(o_columns, 0)])

            @block.vector
            def _(dve):

                def residual(i, u):
                    x = c.x[:, i, :]
                    nc.vector.tensor_tensor(x, x, bog[:, i // NT, :], ALU.add).then_inc(v_x("bias"), 1)
                    dve.wait_ge(v_x.sem, v_x.at("bias", i))
                    dve.wait_ge(p_wo.sem, p_wo.at("wo", i))
                    nc.vector.tensor_tensor(x, x, bk[2 + u % 2][:, 0:P], ALU.add).then_inc(v_x("x"), 1)

                pipeline(dve, [(residual, 1)])


def experts(c, out_ap):
    nc, inp, bk = c.nc, c.inp, c.bank
    with ExitStack() as ctx:
        sb = c.sb(ctx)
        w_in = sb("ex_w_in", [P, NE, E])
        wT = sb("ex_wT", [P, NE * E])
        gate_in, gateT = sb("ex_gate_in", [NE, E]), sb("ex_gateT", [P, NE])
        b_in, b_rest = sb("ex_b_in", [NE, E]), sb("ex_b_rest", [NE, 2, E])
        b_parts = sb("ex_b_parts", [NE, 3, E], BF16)
        b_rows = sb("ex_b_rows", [3, NE, E], BF16)
        ones = sb("ex_ones", [3, P], BF16)
        iota = sb("ex_iota", [P, NE])
        ring = lambda name, *shape: sb("ex_" + name, [P, RING, *shape])
        rows, hT, total = ring("rows", P), ring("hT", P), ring("total", P)
        zmax, zneg, zsum, zrec = (ring(n, 1) for n in ("zmax", "zneg", "zsum", "zrec"))
        prob, top, topf, sel, w = ring("prob", NE), ring("top", 8), ring("topf", 8), ring("sel", NE), ring("w", NE)
        topi = ctx.enter_context(nc.sbuf_tensor("ex_topi", [P, RING, 8], U32))
        yw = sb("ex_yw", [P, 2, NE, E])

        loaded, turned, pre = c.sem(ctx, "ex_loaded"), c.sem(ctx, "ex_turned"), c.sem(ctx, "ex_pre")
        copied, moved, stored = c.sem(ctx, "ex_copied"), c.sem(ctx, "ex_moved"), c.sem(ctx, "ex_stored")
        st = lambda name, *names: c.steps(ctx, "ex_" + name, *names)
        v_norm, g_norm = st("v_norm", "norm"), st("g_norm", "scaled", "shifted")
        p_h, a_h = st("p_h", "hT"), st("a_h", "hT")
        p_gate = st("p_gate", "logits")
        v_max, a_exp = st("v_max", "max", "neg"), st("a_exp", "exp")
        v_top = st("v_top", "rec", "prob", "top", "idx", "float", "first", "both", "w")
        p_up = st("p_up", *[f"bank{k}" for k in range(4)])
        v_relu, a_relu = st("v_relu", "y0"), st("a_relu", *[f"e{e}" for e in range(NE // 4, NE)])
        v_out, g_out = st("v_out", "low", "sum"), st("g_out", "gated", "x")
        every = [v_norm, p_h, a_h, p_gate, v_max, a_exp, v_top, p_up, v_relu, a_relu, v_out, g_norm,
                 g_out]
        statistics, inverse = row_statistics(c, ctx, "ex")

        with nc.Block() as block:

            @block.sync
            def _(sp):
                sp.dma_start(w_in[...], inp["L1_ffn_expert_w"].rearrange("e d h -> d e h")).then_inc(loaded, 16)
                sp.dma_start(gate_in[...], inp["L1_ffn_gate_w"]).then_inc(loaded, 16)
                sp.dma_start(b_in[...], inp["L1_ffn_expert_b"]).then_inc(loaded, 16)
                sp.dma_start(iota[...], inp["expert_numbers"]).then_inc(loaded, 16)
                sp.wait_ge(pre, 5)
                for k in range(3):
                    sp.dma_start(b_rows[k:k + 1, :, :], b_parts[:, k, :]).then_inc(moved, 16)
                sp.wait_ge(moved, 48)

            @block.gpsimd
            def _(gp):
                prime(gp, every)
                nc.gpsimd.memset(ones[...], 1.0)
                inverse(gp)

            @block.vector
            def _(dve):
                statistics(dve)
                dve.wait_ge(loaded, 64)
                src = b_in[...]
                for k in range(3):
                    nc.vector.tensor_copy(b_parts[:, k, :], src).then_inc(pre, 1)
                    if k < 2:
                        dve.wait_ge(pre, 2 * k + 1)
                        nc.vector.tensor_tensor(b_rest[:, k, :], src, b_parts[:, k, :], ALU.subtract)\
                          .then_inc(pre, 1)
                        src = b_rest[:, k, :]
                        dve.wait_ge(pre, 2 * k + 2)

            @block.tensor
            def _(pe):
                pe.wait_ge(loaded, 64)
                for e in range(NE):
                    m = nc.tensor.transpose(bk[e // 4][:, P * (e % 4):P * (e % 4) + P], w_in[:, e, :], c.ident[:, :])
                    if e % 4 == 3:
                        m.then_inc(turned, 1)
                nc.tensor.transpose(bk[4][:, 0:NE], gate_in[...], c.ident[0:NE, 0:NE]).then_inc(turned, 1)

            @block.scalar
            def _(act):
                for k in range(NE // 4):
                    act.wait_ge(turned, k + 1)
                    nc.scalar.activation(wT[:, BANK * k:BANK * k + BANK], bk[k], ACT.Copy).then_inc(copied, 1)
                act.wait_ge(turned, NE // 4 + 1)
                nc.scalar.activation(gateT[...], bk[4][:, 0:NE], ACT.Copy).then_inc(copied, 1)

        h_bank, gate_bank = bk[6], bk[7]
        with nc.Block() as block:

            @block.vector
            def _(dve):

                def norm(i, u):
                    dve.wait_ge(p_h.sem, p_h.at("hT", i - RING))
                    normalize(c, v_norm, rows[:, u, :], i)

                def gate_max(i, u):
                    dve.wait_ge(p_gate.sem, p_gate.at("logits", i))
                    nc.vector.tensor_reduce(zmax[:, u, :], gate_bank[:, 0:NE], AX_X, ALU.max)\
                      .then_inc(v_max("max"), 1)

                def gate_neg(i, u):
                    dve.wait_ge(v_max.sem, v_max.at("max", i))
                    nc.vector.tensor_scalar(zneg[:, u, :], zmax[:, u, :], -1.0, None, ALU.mult)\
                      .then_inc(v_max("neg"), 1)

                def after(name, i):
                    dve.wait_ge(v_top.sem, v_top.at(name, i))

                def reciprocal(i, u):
                    dve.wait_ge(a_exp.sem, a_exp.at("exp", i))
                    nc.vector.reciprocal(zrec[:, u, :], zsum[:, u, :]).then_inc(v_top("rec"), 1)

                def softmax(i, u):
                    after("rec", i)
                    nc.vector.tensor_scalar(prob[:, u, :], prob[:, u, :], zrec[:, u, :], None, ALU.mult)\
                      .then_inc(v_top("prob"), 1)

                def top_values(i, u):
                    after("prob", i)
                    dve.nop(nofuse=True)
                    nc.vector.max(top[:, u, :], prob[:, u, :]).then_inc(v_top("top"), 1)

                def top_indices(i, u):
                    after("top", i)
                    dve.nop(nofuse=True)
                    nc.vector.max_index(topi[:, u, :], top[:, u, :], prob[:, u, :]).then_inc(v_top("idx"), 1)

                def indices_float(i, u):
                    after("idx", i)
                    nc.vector.tensor_copy(topf[:, u, :], topi[:, u, :]).then_inc(v_top("float"), 1)

                def is_first(i, u):
                    after("float", i)
                    nc.vector.tensor_scalar(sel[:, u, :], iota[:, :], topf[:, u, 0:1], None, ALU.is_equal)\
                      .then_inc(v_top("first"), 1)

                def is_either(i, u):
                    after("first", i)
                    nc.vector.scalar_tensor_tensor(out=sel[:, u, :], in0=iota[:, :], scalar=topf[:, u, 1:2],
                                                   in1=sel[:, u, :], op0=ALU.is_equal, op1=ALU.add)\
                      .then_inc(v_top("both"), 1)

                def chosen_weights(i, u):
                    after("both", i)
                    nc.vector.tensor_tensor(w[:, u, :], prob[:, u, :], sel[:, u, :], ALU.mult)\
                      .then_inc(v_top("w"), 1)

                def relu(i, u):
                    dve.wait_ge(v_top.sem, v_top.at("w", i))
                    dve.wait_ge(v_out.sem, v_out.at("sum", i - 2))
                    dve.wait_ge(p_up.sem, p_up.at("bank0", i))
                    n = NE // 4
                    nc.vector.scalar_tensor_tensor(
                        out=yw[:, u % 2, 0:n, :], in0=bk[0].rearrange("p (e f) -> p e f", f=E), scalar=0.0,
                        in1=cols_bc(w[:, u, 0:n], E), op0=ALU.max, op1=ALU.mult).then_inc(v_relu("y0"), 1)

                def total_of(half):
                    f = slice(half * (E // 2), half * (E // 2) + E // 2)
                    return lambda i, u: sum_of(i, u, half, f)

                def sum_of(i, u, half, f):
                    dve.wait_ge(a_relu.sem, a_relu.at(f"e{NE - 1}", i))
                    dve.wait_ge(v_relu.sem, v_relu.at("y0", i))
                    dve.wait_ge(g_out.sem, g_out.at("x", i - RING))
                    nc.vector.tensor_reduce(total[:, u, f], yw[:, u % 2, :, f].rearrange("p e f -> p f e"), AX_X,
                                            ALU.add).then_inc(v_out(("low", "sum")[half]), 1)

                pipeline(dve, [(relu, 4), (reciprocal, 3), (norm, 0), (softmax, 3), (gate_max, 2), (top_values, 3),
                               (gate_neg, 2), (top_indices, 3), (total_of(0), 5), (indices_float, 3),
                               (total_of(1), 5), (is_first, 3), (is_either, 3), (chosen_weights, 3)])

            @block.gpsimd
            def _(gp):

                def shift(i, u):
                    gp.wait_ge(v_norm.sem, v_norm.at("norm", i))
                    modulate(c, nc.gpsimd, g_norm, rows[:, u, :], i, 1, SB, CB)

                def residual(i, u):
                    gp.wait_ge(v_out.sem, v_out.at("sum", i))
                    nc.gpsimd.tensor_tensor(total[:, u, :], total[:, u, :], c.mod[:, 1, i // NT, GB, :], ALU.mult)\
                      .then_inc(g_out("gated"), 1)
                    gp.wait_ge(g_out.sem, g_out.at("gated", i))
                    nc.gpsimd.tensor_tensor(c.x[:, i, :], c.x[:, i, :], total[:, u, :], ALU.add)\
                      .then_inc(g_out("x"), 1)

                pipeline(gp, [(shift, 0), (residual, 5)])

            @block.tensor
            def _(pe):

                def turn_h(i, u):
                    pe.wait_ge(g_norm.sem, g_norm.at("shifted", i))
                    pe.wait_ge(a_h.sem, a_h.at("hT", i - 1))
                    nc.tensor.transpose(h_bank[:, 0:P], rows[:, u, :], c.ident[:, :]).then_inc(p_h("hT"), 1)

                def gate(i, u):
                    pe.wait_ge(a_h.sem, a_h.at("hT", i))
                    pe.wait_ge(a_exp.sem, a_exp.at("exp", i - 1))
                    nc.tensor.matmul(gate_bank[:, 0:NE], hT[:, u, :], gateT[:, :], start=True, stop=True)\
                      .then_inc(p_gate("logits"), 1)

                def up(i, u):
                    readers = [(v_relu, "y0"), (a_relu, "e7"), (a_relu, "e11"), (a_relu, "e15")]
                    for k, (reader, name) in enumerate(readers):
                        pe.wait_ge(reader.sem, reader.at(name, i - 1))
                        brow = b_rows[:, 4 * k:4 * k + 4, :].rearrange("p e f -> p (e f)")
                        nc.tensor.matmul(bk[k], ones[:, :], brow, start=True, stop=False)
                        nc.tensor.matmul(bk[k], hT[:, u, :], wT[:, BANK * k:BANK * k + BANK], start=False,
                                         stop=True).then_inc(p_up(f"bank{k}"), 1)

                pipeline(pe, [(turn_h, 1), (gate, 2), (up, 3)])

            @block.scalar
            def _(act):

                def h_columns(i, u):
                    act.wait_ge(p_h.sem, p_h.at("hT", i))
                    nc.scalar.activation(hT[:, u, :], h_bank[:, 0:P], ACT.Copy).then_inc(a_h("hT"), 1)

                def gate_exp(i, u):
                    act.wait_ge(v_max.sem, v_max.at("neg", i))
                    nc.scalar.activation(prob[:, u, :], gate_bank[:, 0:NE], ACT.Exp, bias=zneg[:, u, :],
                                         accum_out=zsum[:, u, :]).then_inc(a_exp("exp"), 1)

                def relu(i, u):
                    act.wait_ge(v_top.sem, v_top.at("w", i))
                    act.wait_ge(v_out.sem, v_out.at("sum", i - 2))
                    for e in range(NE // 4, NE):
                        act.wait_ge(p_up.sem, p_up.at(f"bank{e // 4}", i))
                        nc.scalar.activation(yw[:, u % 2, e, :], bk[e // 4][:, P * (e % 4):P * (e % 4) + P], ACT.Relu,
                                             scale=w[:, u, e:e + 1]).then_inc(a_relu(f"e{e}"), 1)

                nc.scalar.preload_act_table_set("natural_log_exp_and_others")
                pipeline(act, [(relu, 4), (h_columns, 1), (gate_exp, 2)])

            @block.sync
            def _(sp):

                def write(i, u):
                    sp.wait_ge(g_out.sem, g_out.at("x", i))
                    sp.dma_start(row_tiles(out_ap)[:, i, :], c.x[:, i, :]).then_inc(stored, 16)

                with sp.Fori(0, TILES) as i:
                    write(i, 0)
                sp.wait_ge(stored, 16 * TILES)
                sp.nop(nofuse=True)


def adaln_program(nc, inp, out):
    with ExitStack() as ctx:
        ctx.enter_context(nc.allow_non_contiguous_dma(reason="weight vectors as columns"))
        c = Core(nc, ctx, inp)
        linear_attention(c)
        with ExitStack() as scope:
            y = c.sb(scope)("y_rows", [P, TILES, E])
            attn = windowed_attention(c, y, scope)
            mlp = gated_mlp(c, y, scope)
            start_layers(c, y, (attn, mlp))

            def load_next(sp, l):
                attn.load_layer(sp, (l + 1) % DEPTH)
                attn.wait_layer(sp, l + 1)
                sp.nop(nofuse=True)

            def load_mlp(sp, l):
                mlp.load_layer(sp, l)

            with nc.Fori(0, DEPTH) as l:
                attn.run(l, lambda sp: load_mlp(sp, l))
                mlp.run(l, lambda sp: load_next(sp, l))
            end_layers(c, y)
        causal_convolution(c)
        experts(c, out)


def shape_constants():
    s, t = np.arange(P)[:, None], np.arange(P)[None, :]
    masks = np.zeros((P, NLEV, P), np.uint32)
    masks[:, 0] = (s // (2 * HALVES[0]) == t // (2 * HALVES[0])) & (s <= t)
    for k in range(1, NLEV):
        h = HALVES[k]
        masks[:, k] = (s // (2 * h) == t // (2 * h)) & (s % (2 * h) < h) & (t % (2 * h) >= h)
    reset = np.zeros((P, TILES), np.float32)
    reset[:, ::NT] = -200.0
    keep = np.ones((P, TILES + 1), np.float32)
    keep[:, ::NT] = 0.0
    q, k = np.arange(WIN)[:, None], np.arange(WIN)[None, :]
    own, before, none = np.where(k <= q, 0.0, NEG), np.where(k >= q, 0.0, NEG), np.full((WIN, WIN), NEG)
    tile = np.block([[own, before], [before, own]])
    first = np.block([[own, none], [before, own]])
    bias = np.stack([first, tile], 1).astype(np.float32)
    f32 = np.float32
    half = np.arange(0, WD, 2, dtype=f32)
    t = np.arange(T, dtype=f32)
    freq = t[:, None] * (f32(1) / np.power(f32(10000), half / f32(WD)))[None, :]
    base = ((half + f32(0.4 * WD)) / f32(1.4 * WD)).astype(np.float64)
    scale = base[None, :] ** ((t - T // 2) / f32(WIN // 2))[:, None].astype(np.float64)
    cos, sin = np.cos(freq.astype(np.float64)), np.sin(freq.astype(np.float64))
    tabs = [np.concatenate(p, 1) for p in ((cos * scale, cos * scale), (-sin * scale, sin * scale),
                                           (cos / scale, cos / scale), (-sin / scale, sin / scale))]
    rot = np.stack(tabs).astype(f32).reshape(4, NT, P, WD).transpose(2, 0, 1, 3)
    eye = np.eye(P, dtype=f32)
    return {"ident": eye, "level_masks": masks, "batch_reset": reset,
            "batch_keep": keep, "window_bias": bias, "rotations": rot, "flip": np.ascontiguousarray(eye[::-1]),
            "expert_numbers": np.tile(np.arange(NE, dtype=f32), (P, 1))}


_INS = ["L0_attn_x", "L0_attn_Wq", "L0_attn_Wk", "L0_attn_Wv", "L0_attn_Wo", "L0_attn_delta", "L0_attn_G1",
        "L0_attn_G2", "L0_attn_norm_w", "L0_ffn_wqkv", "L0_ffn_q_scale", "L0_ffn_k_scale", "L0_ffn_wo",
        "L0_ffn_ln_g", "L0_ffn_ln_b", "L0_ffn_w1", "L0_ffn_b1", "L0_ffn_w2", "L0_ffn_b2", "L0_c", "L0_wmod",
        "L1_attn_W_A", "L1_attn_W_V", "L1_attn_W_O", "L1_attn_b_O", "L1_ffn_gate_w", "L1_ffn_expert_w",
        "L1_ffn_expert_b", "L1_c", "L1_wmod"]


def kernel(**inputs):
    import concourse.bacc as bacc
    from concourse.bass_utils import run_bass_kernel_spmd

    nc = bacc.Bacc("TRN2", target_bir_lowering=False, num_devices=1)
    arrays, aps = {}, {}
    for name, a in [(n, inputs[n]) for n in _INS] + list(shape_constants().items()):
        a = np.ascontiguousarray(a)
        arrays[f"in_{name}_dram"] = a
        aps[name] = nc.dram_tensor(f"in_{name}_dram", a.shape, mybir.dt.from_np(a.dtype), kind="ExternalInput").ap()
    out = nc.dram_tensor("out_0_dram", (B, T, E), F32, kind="ExternalOutput").ap()
    adaln_program(nc, aps, out)
    r = run_bass_kernel_spmd(nc, [arrays], core_ids=[0])
    return r.results[0]["out_0_dram"]
```
